# Optimizing a Trainium2 kernel written in Bass

```python
import numpy as np
import jax
import jax.numpy as jnp

def _softmax(x, axis=-1):
    return jax.nn.softmax(x, axis=axis)

def _gelu(x):
    return jax.nn.gelu(x, approximate=True)

def _silu(x):
    return jax.nn.silu(x)

def _sigmoid(x):
    return jax.nn.sigmoid(x)

def _layernorm(x, axis=-1, eps=1e-05):
    m = jnp.mean(x, axis=axis, keepdims=True)
    v = jnp.var(x, axis=axis, keepdims=True)
    return (x - m) / jnp.sqrt(v + eps)

def _scatter_add(tgt, idx, src, axis=0):
    return tgt.at[idx].add(src)

def _segment_sum(src, seg, n):
    return jax.ops.segment_sum(src, seg, n)
kernel_name = 'mk_vit_tower_d2_tok_img1024_r4_640e9c'

def setup_inputs(seed: int=0):
    np.random.seed(seed)
    _w = jnp.asarray

    def _rec_inputs():
        import jax
        import jax.numpy as jnp
        _rk = jax.random.key(seed)
        x = -0.000222058 + 0.999998 * jax.random.normal(jax.random.fold_in(_rk, 1), (64, 3, 128, 128), jnp.float32)
        return x
    x = _rec_inputs()

    def _L0_tok_setup():
        import jax, jax.numpy as jnp
        import numpy as np
        P = 16
        C = 3
        D = 256

        def _patchify(x, p):
            B, Cc, H, W = x.shape
            gh, gw = (H // p, W // p)
            x = x.reshape(B, Cc, gh, p, gw, p)
            x = x.transpose(0, 2, 4, 1, 3, 5)
            return x.reshape(B, gh * gw, Cc * p * p)
        key = jax.random.key(seed)
        k1, k2, k3, k4, k5 = jax.random.split(key, 5)
        patch_dim = C * P * P
        s1 = 1.0 / np.sqrt(patch_dim)
        s2 = 1.0 / np.sqrt(D)
        return {'x': jax.random.normal(k1, (32, C, 128, 128), dtype=jnp.float32), 'W1': jax.random.uniform(k2, (patch_dim, D), jnp.float32, -s1, s1), 'b1': jax.random.uniform(k3, (D,), jnp.float32, -s1, s1), 'W2': jax.random.uniform(k4, (D, D), jnp.float32, -s2, s2), 'b2': jax.random.uniform(k5, (D,), jnp.float32, -s2, s2)}
    _L0_tok_all = _L0_tok_setup()
    _L0_tok_in = {k: v for k, v in _L0_tok_all.items() if k in ('W1', 'b1', 'W2', 'b2')}
    del _L0_tok_all

    def _L0_attn_setup():
        import jax, jax.numpy as jnp
        import numpy as np
        import math
        D_MODEL = 256
        D_K = 64
        D_V = 64
        N_HEADS = 16
        key = jax.random.key(seed)
        ks = jax.random.split(key, 5)
        std = 1.0 / math.sqrt(D_MODEL)
        x = jax.random.normal(ks[0], (2, 512, D_MODEL), dtype=jnp.float32)
        Wq = jax.random.normal(ks[1], (D_MODEL, N_HEADS * D_K), dtype=jnp.float32) * std
        Wk = jax.random.normal(ks[2], (D_MODEL, N_HEADS * D_K), dtype=jnp.float32) * std
        Wv = jax.random.normal(ks[3], (D_MODEL, N_HEADS * D_V), dtype=jnp.float32) * std
        Wo = jax.random.normal(ks[4], (N_HEADS * D_V, D_MODEL), dtype=jnp.float32) * std
        return {'x': x, 'Wq': Wq, 'Wk': Wk, 'Wv': Wv, 'Wo': Wo}
    _L0_attn_all = _L0_attn_setup()
    _L0_attn_in = {k: v for k, v in _L0_attn_all.items() if k in ('Wq', 'Wk', 'Wv', 'Wo')}
    del _L0_attn_all

    def _L0_ffn_setup():
        import jax, jax.numpy as jnp
        import numpy as np
        D = 256
        I = 128
        E = 7
        TOPK = 2
        B, S = (4, 1024)

        def _expert(xt, wg, wu, wd):
            return jax.nn.silu(xt @ wg) * (xt @ wu) @ wd
        key = jax.random.key(seed)
        ks = jax.random.split(key, 10)
        s = 0.02
        return {'x': jax.random.normal(ks[0], (B, S, D), dtype=jnp.float32), 'sh_gate': jax.random.normal(ks[1], (D, I), dtype=jnp.float32) * s, 'sh_up': jax.random.normal(ks[2], (D, I), dtype=jnp.float32) * s, 'sh_down': jax.random.normal(ks[3], (I, D), dtype=jnp.float32) * s, 'r_gate': jax.random.normal(ks[4], (E, D, I), dtype=jnp.float32) * s, 'r_up': jax.random.normal(ks[5], (E, D, I), dtype=jnp.float32) * s, 'r_down': jax.random.normal(ks[6], (E, I, D), dtype=jnp.float32) * s, 'w_r': jax.random.normal(ks[7], (D, E), dtype=jnp.float32) * s, 'b_r': jnp.zeros((E,), dtype=jnp.float32), 'routing_bias': jnp.zeros((E,), dtype=jnp.float32)}
    _L0_ffn_all = _L0_ffn_setup()
    _L0_ffn_in = {k: v for k, v in _L0_ffn_all.items() if k in ('sh_gate', 'sh_up', 'sh_down', 'r_gate', 'r_up', 'r_down', 'w_r', 'b_r', 'routing_bias')}
    del _L0_ffn_all

    def _L1_attn_setup():
        import jax, jax.numpy as jnp
        import numpy as np
        import math
        B, S, E = (2, 512, 256)
        H, DC, DR = (16, 64, 128)
        HD = E // H

        def _linear_params(key, din, dout):
            k1, k2 = jax.random.split(key)
            bound = 1.0 / math.sqrt(din)
            w = jax.random.uniform(k1, (din, dout), minval=-bound, maxval=bound, dtype=jnp.float32)
            b = jax.random.uniform(k2, (dout,), minval=-bound, maxval=bound, dtype=jnp.float32)
            return (w, b)

        def _gelu(x):
            return jax.nn.gelu(x, approximate=False)

        def _rope_cos_sin(seq_len, d_rope):
            inv_freq = 1.0 / 10000.0 ** (jnp.arange(0, d_rope, 2, dtype=jnp.float32) / d_rope)
            t = jnp.arange(seq_len, dtype=jnp.float32)
            freqs = t[:, None] * inv_freq[None, :]
            emb = jnp.concatenate([freqs, freqs], axis=-1)
            return (jnp.cos(emb), jnp.sin(emb))

        def _apply_rope(x, cos, sin):
            d = x.shape[-1]
            x1, x2 = (x[..., :d // 2], x[..., d // 2:])
            rot = jnp.concatenate([-x2, x1], axis=-1)
            return x * cos + rot * sin
        key = jax.random.key(seed)
        ks = jax.random.split(key, 10)
        x = jax.random.normal(ks[0], (B, S, E), dtype=jnp.float32)
        wq, bq = _linear_params(ks[1], E, DC)
        wqc, bqc = _linear_params(ks[2], DC, E - DR)
        wqr, bqr = _linear_params(ks[3], E, DR)
        wkv, bkv = _linear_params(ks[4], E, DC)
        wkr, bkr = _linear_params(ks[5], E, DR)
        wkc, bkc = _linear_params(ks[6], DC, E - DR)
        wv, bv = _linear_params(ks[7], DC, E)
        wo, bo = _linear_params(ks[8], E, E)
        return dict(x=x, wq=wq, bq=bq, wqc=wqc, bqc=bqc, wqr=wqr, bqr=bqr, wkv=wkv, bkv=bkv, wkr=wkr, bkr=bkr, wkc=wkc, bkc=bkc, wv=wv, bv=bv, wo=wo, bo=bo)
    _L1_attn_all = _L1_attn_setup()
    _L1_attn_in = {k: v for k, v in _L1_attn_all.items() if k in ('wq', 'bq', 'wqc', 'bqc', 'wqr', 'bqr', 'wkv', 'bkv', 'wkr', 'bkr', 'wkc', 'bkc', 'wv', 'bv', 'wo', 'bo')}
    del _L1_attn_all

    def _L1_ffn_setup():
        import jax, jax.numpy as jnp
        import numpy as np
        from jax import lax
        TOP_K = 4
        N_GROUP = 4
        TOPK_GROUP = 2
        ROUTED_SCALE = 2.5
        NEG_INF = -1000000000.0

        def _route(xf, router_weight, router_bias):
            T = xf.shape[0]
            E = router_weight.shape[0]
            logits = xf @ router_weight.T
            scores = jax.nn.sigmoid(logits)
            s_choice = scores + router_bias
            per_group = E // N_GROUP
            sg = s_choice.reshape(T, N_GROUP, per_group)
            group_scores = lax.top_k(sg, 2)[0].sum(-1)
            _, gidx = lax.top_k(group_scores, TOPK_GROUP)
            gmask = jnp.zeros((T, N_GROUP), dtype=bool).at[jnp.arange(T)[:, None], gidx].set(True)
            masked = jnp.where(gmask[:, :, None], sg, NEG_INF).reshape(T, E)
            _, topk_idx = lax.top_k(masked, TOP_K)
            w = jnp.take_along_axis(scores, topk_idx, axis=1)
            w = w / (w.sum(-1, keepdims=True) + 1e-20) * ROUTED_SCALE
            combine = jnp.zeros((T, E), dtype=xf.dtype).at[jnp.arange(T)[:, None], topk_idx].add(w)
            return combine
        key = jax.random.key(seed)
        ks = jax.random.split(key, 6)
        B, S, H, I, E = (2, 512, 256, 128, 16)
        x = jax.random.normal(ks[0], (B, S, H), dtype=jnp.float32)
        router_weight = jax.random.normal(ks[1], (E, H), dtype=jnp.float32) * 0.02
        router_bias = jnp.zeros((E,), dtype=jnp.float32)
        w_gate = jax.random.normal(ks[2], (E, I, H), dtype=jnp.float32) * 0.02
        w_up = jax.random.normal(ks[3], (E, I, H), dtype=jnp.float32) * 0.02
        w_down = jax.random.normal(ks[4], (E, H, I), dtype=jnp.float32) * 0.02
        return {'x': x, 'router_weight': router_weight, 'router_bias': router_bias, 'w_gate': w_gate, 'w_up': w_up, 'w_down': w_down}
    _L1_ffn_all = _L1_ffn_setup()
    _L1_ffn_in = {k: v for k, v in _L1_ffn_all.items() if k in ('router_weight', 'router_bias', 'w_gate', 'w_up', 'w_down')}
    del _L1_ffn_all
    return {'x': x, 'L0_tok_W1': _L0_tok_in['W1'], 'L0_tok_b1': _L0_tok_in['b1'], 'L0_tok_W2': _L0_tok_in['W2'], 'L0_tok_b2': _L0_tok_in['b2'], 'L0_attn_Wq': _L0_attn_in['Wq'], 'L0_attn_Wk': _L0_attn_in['Wk'], 'L0_attn_Wv': _L0_attn_in['Wv'], 'L0_attn_Wo': _L0_attn_in['Wo'], 'L0_ffn_sh_gate': _L0_ffn_in['sh_gate'], 'L0_ffn_sh_up': _L0_ffn_in['sh_up'], 'L0_ffn_sh_down': _L0_ffn_in['sh_down'], 'L0_ffn_r_gate': _L0_ffn_in['r_gate'], 'L0_ffn_r_up': _L0_ffn_in['r_up'], 'L0_ffn_r_down': _L0_ffn_in['r_down'], 'L0_ffn_w_r': _L0_ffn_in['w_r'], 'L0_ffn_b_r': _L0_ffn_in['b_r'], 'L0_ffn_routing_bias': _L0_ffn_in['routing_bias'], 'L1_attn_wq': _L1_attn_in['wq'], 'L1_attn_bq': _L1_attn_in['bq'], 'L1_attn_wqc': _L1_attn_in['wqc'], 'L1_attn_bqc': _L1_attn_in['bqc'], 'L1_attn_wqr': _L1_attn_in['wqr'], 'L1_attn_bqr': _L1_attn_in['bqr'], 'L1_attn_wkv': _L1_attn_in['wkv'], 'L1_attn_bkv': _L1_attn_in['bkv'], 'L1_attn_wkr': _L1_attn_in['wkr'], 'L1_attn_bkr': _L1_attn_in['bkr'], 'L1_attn_wkc': _L1_attn_in['wkc'], 'L1_attn_bkc': _L1_attn_in['bkc'], 'L1_attn_wv': _L1_attn_in['wv'], 'L1_attn_bv': _L1_attn_in['bv'], 'L1_attn_wo': _L1_attn_in['wo'], 'L1_attn_bo': _L1_attn_in['bo'], 'L1_ffn_router_weight': _L1_ffn_in['router_weight'], 'L1_ffn_router_bias': _L1_ffn_in['router_bias'], 'L1_ffn_w_gate': _L1_ffn_in['w_gate'], 'L1_ffn_w_up': _L1_ffn_in['w_up'], 'L1_ffn_w_down': _L1_ffn_in['w_down']}

def reference(x, L0_tok_W1, L0_tok_b1, L0_tok_W2, L0_tok_b2, L0_attn_Wq, L0_attn_Wk, L0_attn_Wv, L0_attn_Wo, L0_ffn_sh_gate, L0_ffn_sh_up, L0_ffn_sh_down, L0_ffn_r_gate, L0_ffn_r_up, L0_ffn_r_down, L0_ffn_w_r, L0_ffn_b_r, L0_ffn_routing_bias, L1_attn_wq, L1_attn_bq, L1_attn_wqc, L1_attn_bqc, L1_attn_wqr, L1_attn_bqr, L1_attn_wkv, L1_attn_bkv, L1_attn_wkr, L1_attn_bkr, L1_attn_wkc, L1_attn_bkc, L1_attn_wv, L1_attn_bv, L1_attn_wo, L1_attn_bo, L1_ffn_router_weight, L1_ffn_router_bias, L1_ffn_w_gate, L1_ffn_w_up, L1_ffn_w_down):
    import jax
    import jax.numpy as jnp

    def _L0_tok_ref(x, W1, b1, W2, b2):
        import jax, jax.numpy as jnp
        import numpy as np
        P = 16
        C = 3
        D = 256

        def _patchify(x, p):
            B, Cc, H, W = x.shape
            gh, gw = (H // p, W // p)
            x = x.reshape(B, Cc, gh, p, gw, p)
            x = x.transpose(0, 2, 4, 1, 3, 5)
            return x.reshape(B, gh * gw, Cc * p * p)
        patches = _patchify(x, P)
        h = jax.nn.silu(jnp.einsum('blk,kd->bld', patches, W1) + b1)
        return jnp.einsum('bld,de->ble', h, W2) + b2

    def _L0_attn_ref(x, Wq, Wk, Wv, Wo):
        import jax, jax.numpy as jnp
        import numpy as np
        import math
        D_MODEL = 256
        D_K = 64
        D_V = 64
        N_HEADS = 16
        B, S, D = x.shape
        H, dk, dv = (N_HEADS, D_K, D_V)
        q = (x @ Wq).reshape(B, S, H, dk)
        k = (x @ Wk).reshape(B, S, H, dk)
        v = (x @ Wv).reshape(B, S, H, dv)
        scores = jnp.einsum('bqhd,bkhd->bhqk', q / math.sqrt(dk), k)
        causal = jnp.tril(jnp.ones((S, S), dtype=bool))
        scores = scores + jnp.where(causal, 0.0, -jnp.inf).astype(scores.dtype)
        attn = jax.nn.softmax(scores, axis=-1)
        out = jnp.einsum('bhqk,bkhd->bqhd', attn, v).reshape(B, S, H * dv)
        return x + out @ Wo

    def _L0_ffn_ref(x, sh_gate, sh_up, sh_down, r_gate, r_up, r_down, w_r, b_r, routing_bias):
        import jax, jax.numpy as jnp
        import numpy as np
        D = 256
        I = 128
        E = 7
        TOPK = 2
        B, S = (4, 1024)

        def _expert(xt, wg, wu, wd):
            return jax.nn.silu(xt @ wg) * (xt @ wu) @ wd
        Bx, Sx, Dx = x.shape
        T = Bx * Sx
        xt = x.reshape(T, Dx)
        shared_out = _expert(xt, sh_gate, sh_up, sh_down)
        logits = xt @ w_r + b_r + routing_bias
        probs = jax.nn.sigmoid(logits)
        top_p, top_i = jax.lax.top_k(probs, TOPK)
        top_p = top_p / jnp.sum(top_p, axis=-1, keepdims=True)
        comb = jnp.zeros((T, E), dtype=x.dtype).at[jnp.arange(T)[:, None], top_i].add(top_p)
        routed_out = jnp.zeros_like(xt)
        for e in range(E):
            y = _expert(xt, r_gate[e], r_up[e], r_down[e])
            routed_out = routed_out + y * comb[:, e:e + 1]
        return (shared_out + routed_out).reshape(Bx, Sx, Dx)

    def _L1_attn_ref(x, wq, bq, wqc, bqc, wqr, bqr, wkv, bkv, wkr, bkr, wkc, bkc, wv, bv, wo, bo):
        import jax, jax.numpy as jnp
        import numpy as np
        import math
        B, S, E = (2, 512, 256)
        H, DC, DR = (16, 64, 128)
        HD = E // H

        def _linear_params(key, din, dout):
            k1, k2 = jax.random.split(key)
            bound = 1.0 / math.sqrt(din)
            w = jax.random.uniform(k1, (din, dout), minval=-bound, maxval=bound, dtype=jnp.float32)
            b = jax.random.uniform(k2, (dout,), minval=-bound, maxval=bound, dtype=jnp.float32)
            return (w, b)

        def _gelu(x):
            return jax.nn.gelu(x, approximate=False)

        def _rope_cos_sin(seq_len, d_rope):
            inv_freq = 1.0 / 10000.0 ** (jnp.arange(0, d_rope, 2, dtype=jnp.float32) / d_rope)
            t = jnp.arange(seq_len, dtype=jnp.float32)
            freqs = t[:, None] * inv_freq[None, :]
            emb = jnp.concatenate([freqs, freqs], axis=-1)
            return (jnp.cos(emb), jnp.sin(emb))

        def _apply_rope(x, cos, sin):
            d = x.shape[-1]
            x1, x2 = (x[..., :d // 2], x[..., d // 2:])
            rot = jnp.concatenate([-x2, x1], axis=-1)
            return x * cos + rot * sin
        b, s, _ = x.shape
        cq = _gelu(x @ wq + bq)
        q_c = cq @ wqc + bqc
        q_r = x @ wqr + bqr
        ckv = _gelu(x @ wkv + bkv)
        k_r = x @ wkr + bkr
        k_c = ckv @ wkc + bkc
        v = (ckv @ wv + bv).reshape(b, s, H, HD).transpose(0, 2, 1, 3)
        cos, sin = _rope_cos_sin(s, DR)
        q_r = _apply_rope(q_r, cos, sin)
        k_r = _apply_rope(k_r, cos, sin)
        q = _gelu(jnp.concatenate([q_c, q_r], axis=-1)).reshape(b, s, H, HD).transpose(0, 2, 1, 3)
        k = _gelu(jnp.concatenate([k_c, k_r], axis=-1)).reshape(b, s, H, HD).transpose(0, 2, 1, 3)
        scale = 1.0 / math.sqrt(HD)
        scores = jnp.einsum('bhqd,bhkd->bhqk', q, k) * scale
        causal = jnp.triu(jnp.ones((s, s), dtype=bool), k=1)
        scores = jnp.where(causal[None, None], -jnp.inf, scores)
        attn = jax.nn.softmax(scores, axis=-1)
        out = jnp.einsum('bhqk,bhkd->bhqd', attn, v)
        out = out.transpose(0, 2, 1, 3).reshape(b, s, E)
        return out @ wo + bo

    def _L1_ffn_ref(x, router_weight, router_bias, w_gate, w_up, w_down):
        import jax, jax.numpy as jnp
        import numpy as np
        from jax import lax
        TOP_K = 4
        N_GROUP = 4
        TOPK_GROUP = 2
        ROUTED_SCALE = 2.5
        NEG_INF = -1000000000.0

        def _route(xf, router_weight, router_bias):
            T = xf.shape[0]
            E = router_weight.shape[0]
            logits = xf @ router_weight.T
            scores = jax.nn.sigmoid(logits)
            s_choice = scores + router_bias
            per_group = E // N_GROUP
            sg = s_choice.reshape(T, N_GROUP, per_group)
            group_scores = lax.top_k(sg, 2)[0].sum(-1)
            _, gidx = lax.top_k(group_scores, TOPK_GROUP)
            gmask = jnp.zeros((T, N_GROUP), dtype=bool).at[jnp.arange(T)[:, None], gidx].set(True)
            masked = jnp.where(gmask[:, :, None], sg, NEG_INF).reshape(T, E)
            _, topk_idx = lax.top_k(masked, TOP_K)
            w = jnp.take_along_axis(scores, topk_idx, axis=1)
            w = w / (w.sum(-1, keepdims=True) + 1e-20) * ROUTED_SCALE
            combine = jnp.zeros((T, E), dtype=xf.dtype).at[jnp.arange(T)[:, None], topk_idx].add(w)
            return combine
        B, S, H = x.shape
        E = w_gate.shape[0]
        xf = x.reshape(-1, H)
        combine = _route(xf, router_weight, router_bias)
        out = jnp.zeros_like(xf)
        for e in range(E):
            g = xf @ w_gate[e].T
            u = xf @ w_up[e].T
            y_e = jax.nn.silu(g) * u @ w_down[e].T
            out = out + combine[:, e:e + 1] * y_e
        return out.reshape(B, S, H)
    h = _L0_tok_ref(x, L0_tok_W1, L0_tok_b1, L0_tok_W2, L0_tok_b2)
    h = h + _L0_attn_ref(_layernorm(h, axis=-1), L0_attn_Wq, L0_attn_Wk, L0_attn_Wv, L0_attn_Wo)
    h = h + _L0_ffn_ref(_layernorm(h, axis=-1), L0_ffn_sh_gate, L0_ffn_sh_up, L0_ffn_sh_down, L0_ffn_r_gate, L0_ffn_r_up, L0_ffn_r_down, L0_ffn_w_r, L0_ffn_b_r, L0_ffn_routing_bias)
    h = h + _L1_attn_ref(_layernorm(h, axis=-1), L1_attn_wq, L1_attn_bq, L1_attn_wqc, L1_attn_bqc, L1_attn_wqr, L1_attn_bqr, L1_attn_wkv, L1_attn_bkv, L1_attn_wkr, L1_attn_bkr, L1_attn_wkc, L1_attn_bkc, L1_attn_wv, L1_attn_bv, L1_attn_wo, L1_attn_bo)
    h = h + _L1_ffn_ref(_layernorm(h, axis=-1), L1_ffn_router_weight, L1_ffn_router_bias, L1_ffn_w_gate, L1_ffn_w_up, L1_ffn_w_down)
    return h

_drawn_inputs = setup_inputs


def setup_inputs(seed=0):
    import zlib

    import numpy as np

    out = dict(_drawn_inputs(seed))
    spreads = {'L0_ffn_b_r': (0.0, 0.8),
     'L0_ffn_routing_bias': (0.0, 0.8),
     'L1_ffn_router_bias': (0.0, 0.765)}
    factors = {'L0_ffn_sh_gate': 6.951,
     'L0_ffn_sh_up': 6.806,
     'L0_ffn_sh_down': 6.768,
     'L0_ffn_r_gate': 8.0,
     'L0_ffn_r_up': 8.0,
     'L0_ffn_r_down': 8.0,
     'L0_ffn_w_r': 8.0,
     'L1_attn_wq': 8.0,
     'L1_attn_bq': 95.075,
     'L1_attn_wqc': 8.0,
     'L1_attn_bqc': 170.84,
     'L1_attn_wqr': 8.0,
     'L1_attn_bqr': 120.128,
     'L1_attn_bkv': 8.0,
     'L1_attn_wkr': 8.0,
     'L1_attn_bkr': 95.208,
     'L1_attn_wkc': 8.0,
     'L1_attn_bkc': 21.753,
     'L1_ffn_router_weight': 7.457,
     'L1_ffn_w_gate': 5.643,
     'L1_ffn_w_up': 5.566,
     'L1_ffn_w_down': 5.569}
    for name, (base, spread) in spreads.items():
        noise = np.random.default_rng([zlib.crc32(name.encode()), seed]).standard_normal(out[name].shape)
        drawn = base * np.exp(spread * noise) if base else spread * noise
        out[name] = jnp.asarray(drawn.astype(out[name].dtype))
    for name, factor in factors.items():
        out[name] = (out[name] * factor).astype(out[name].dtype)
    return out
```

```python
import math
from contextlib import ExitStack

import numpy as np
import concourse.bass as bass
from concourse import mybir

F32 = mybir.dt.float32
F32R = mybir.dt.float32r
BF16 = mybir.dt.bfloat16
ALU = mybir.AluOpType
ACT = mybir.ActivationFunctionType
AX = mybir.AxisListType

P = 128
D = 256
KD = D // P
IMAGES = 64
SEQ = 64
TOKENS = IMAGES * SEQ
TILE = 512
TILES = TOKENS // TILE
BLOCKS = TOKENS // P
CH = TILE // P
IMG_T = TILE // SEQ
PATCH = 3 * 16 * 16
KP = PATCH // P
EPS = 1e-5
NEG = -1e30

HEADS = 16
PAIRS = HEADS // 2
DK0 = 64
DK1 = D // HEADS
QKV0 = HEADS * DK0
HB0 = QKV0 // P

INNER = 128
WCOLS = 2 * D + D
E0, E1 = 8, 16
DVE_BN = 6


def at_least(eng, sem, value):
    if not isinstance(value, int) or value > 0:
        eng.wait_ge(sem, value)


def hold(eng, sem, value):
    eng.wait_ge(sem, value)
    eng.nop(nofuse=True)


def looped(eng, n, body):
    body(0)
    with eng.Fori(1, n - 1) as i:
        body(i)
    body(n - 1, last=True)


def row_statistics(dve, core, st, stats, step, block, count):
    for c in range(count):
        last = dve.bn_stats(st[:, c, :], core.h[:, bass.ds(block + c, 1), :].rearrange("p a n -> p (a n)"))
    last.then_inc(stats, 1)
    hold(dve, stats, 3 * step + 1)
    for c in range(count):
        last = dve.bn_aggr(st[:, c, 0:2], st[:, c, :])
    last.then_inc(stats, 1)
    dve.wait_ge(stats, 3 * step + 2)
    dve.tensor_scalar(core.mv[:, bass.ds(block, count), :], st[:, :, 0:2], 1.0, None, ALU.mult).then_inc(stats, 1)


def product3(eng, out, lhs, rhs, start=True, stop=True):
    terms = ((0, 0), (0, 1), (1, 0))
    for n, (a, b) in enumerate(terms):
        mm = eng.matmul(out, lhs[a], rhs[b], start=start and n == 0, stop=stop and n == len(terms) - 1)
    return mm


class Core:

    def __init__(self, nc, ctx, dram):
        self.nc, self.ctx, self.dram = nc, ctx, dram
        sb = self.sb
        self.h = sb(ctx, "h", [P, BLOCKS, D])
        self.mv = sb(ctx, "mv", [P, BLOCKS, 2])
        self.rstd = sb(ctx, "rstd", [P, BLOCKS])
        self.ident = sb(ctx, "ident", [P, P])
        self.ident_bf = sb(ctx, "ident_bf", [P, P], BF16)
        self.mask_bf = sb(ctx, "mask_bf", [P, TILE], BF16)

    def sb(self, ctx, name, shape, dt=F32):
        return ctx.enter_context(self.nc.sbuf_tensor(name, shape, dt))

    def ps(self, ctx, name, shape):
        return ctx.enter_context(self.nc.psum_tensor(name, shape, F32))

    def sem(self, name):
        return self.ctx.enter_context(self.nc.semaphore(name))


def patch_phase(core):
    nc, d = core.nc, core.dram
    with ExitStack() as ctx:
        sb = lambda name, shape, dt=F32: core.sb(ctx, "pa_" + name, shape, dt)
        sem = lambda name: core.sem("pa_" + name)
        w1_in, w2_in = sb("w1_in", [P, KP, D]), sb("w2_in", [P, KD, D])
        w1 = [sb("w1_hi", [P, KP, D], F32R), sb("w1_lo", [P, KP, D], F32R)]
        w2 = [sb("w2_hi", [P, KD, D], F32R), sb("w2_lo", [P, KD, D], F32R)]
        b1, b2 = sb("b1", [P, KD]), sb("b2", [P, D])
        mask_in = sb("mask_in", [P, SEQ])
        x = [sb(f"x{i}", [P, KP, TILE]) for i in range(2)]
        xs = [[sb(f"x_hi{i}", [P, KP, TILE], F32R), sb(f"x_lo{i}", [P, KP, TILE], F32R)] for i in range(2)]
        act = sb("act", [P, KD, TILE])
        acts = [sb("act_hi", [P, KD, TILE], F32R), sb("act_lo", [P, KD, TILE], F32R)]
        st = sb("st", [P, CH, DVE_BN])
        p_hid = [core.ps(ctx, f"pa_hid{i}", [P, KD, TILE]) for i in range(2)]
        p_out = [core.ps(ctx, f"pa_out{i}", [P, CH, D]) for i in range(2)]

        w_in, c_in = sem("w_in"), sem("c_in")
        x_in = [sem("x_in0"), sem("x_in1")]
        w_hi, w_split, consts = sem("w_hi"), sem("w_split"), sem("consts")
        x_hi, x_lo, hid, silu, act_hi, act_lo = (sem(n) for n in ("x_hi", "x_lo", "hid", "silu", "act_hi", "act_lo"))
        outp, h_done, stats = sem("outp"), sem("h_done"), sem("stats")

        block = ctx.enter_context(nc.Block())

        @block.sync
        def _(sp):
            sp.dma_start(w1_in[:], d["W1"]).then_inc(w_in, 16)
            sp.dma_start(x[0][:], d["x"][0]).then_inc(x_in[0], 16)
            sp.dma_start(w2_in[:], d["W2"]).then_inc(w_in, 16)
            sp.dma_start(x[1][:], d["x"][1]).then_inc(x_in[1], 16)
            with sp.Fori(1, TILES // 2) as t2:
                for u in range(2):
                    sp.wait_ge(x_lo, 2 * t2 + u - 1)
                    sp.dma_start(x[u][:], d["x"][bass.ds(2 * t2 + u, 1)].rearrange("a p k n -> (a p) k n"))\
                        .then_inc(x_in[u], 16)

        @block.scalar
        def _(act_e):
            act_e.dma_start(b1[:], d["b1"]).then_inc(c_in, 16)
            act_e.dma_start(b2[:], d["b2"].partition_broadcast(P)).then_inc(c_in, 16)
            act_e.dma_start(core.ident[:], d["ident"]).then_inc(c_in, 16)
            act_e.dma_start(mask_in[:], d["mask"]).then_inc(c_in, 16)
            act_e.wait_ge(w_in, 32)
            act_e.copy(w1[0][:], w1_in[:]).then_inc(w_hi, 1)
            act_e.copy(w2[0][:], w2_in[:]).then_inc(w_hi, 1)
            act_e.wait_ge(c_in, 64)

            def x_high(u, t2):
                act_e.wait_ge(x_in[u], 16 * t2 + 16)
                at_least(act_e, hid, 2 * t2 + u - 1)
                act_e.copy(xs[u][0][:], x[u][:]).then_inc(x_hi, 1)

            def pair(t2, last=False):
                for u in range(2):
                    t = 2 * t2 + u
                    if u == 0 or not last:
                        x_high(1 - u, t2 + u)
                    act_e.wait_ge(hid, t + 1)
                    at_least(act_e, act_lo, t)
                    for m in range(KD):
                        done = act_e.activation(act[:, m, :], p_hid[u][:, m, :], ACT.Silu, bias=b1[:, m:m + 1])
                    done.then_inc(silu, 1)
                    act_e.wait_ge(silu, t + 1)
                    at_least(act_e, outp, t)
                    act_e.copy(acts[0][:], act[:]).then_inc(act_hi, 1)

            x_high(0, 0)
            looped(act_e, TILES // 2, pair)

        @block.vector
        def _(dve):
            dve.wait_ge(w_hi, 2)
            dve.tensor_tensor(w1[1][:], w1_in[:], w1[0][:].bitcast(F32), ALU.subtract).then_inc(w_split, 1)
            dve.tensor_tensor(w2[1][:], w2_in[:], w2[0][:].bitcast(F32), ALU.subtract).then_inc(w_split, 1)

            def x_low(u, t):
                dve.wait_ge(x_hi, t + 1)
                dve.tensor_tensor(xs[u][1][:], x[u][:], xs[u][0][:].bitcast(F32), ALU.subtract).then_inc(x_lo, 1)

            def finish(u, t):
                dve.wait_ge(outp, t + 1)
                dve.tensor_tensor(core.h[:, bass.ds(CH * t, CH), :], p_out[u][:],
                                  b2[:].rearrange("p (c n) -> p c n", c=1).broadcast_to([P, CH, D]),
                                  ALU.add).then_inc(h_done, 1)
                hold(dve, h_done, t + 1)
                row_statistics(dve, core, st, stats, t, CH * t, CH)

            def pair(t2, last=False):
                for u in range(2):
                    t = 2 * t2 + u
                    if u == 0 or not last:
                        x_low(1 - u, t + 1)
                    dve.wait_ge(act_hi, t + 1)
                    dve.tensor_tensor(acts[1][:], act[:], acts[0][:].bitcast(F32), ALU.subtract).then_inc(act_lo, 1)
                    if not (isinstance(t, int) and t == 0):
                        finish(1 - u, t - 1)

            x_low(0, 0)
            dve.wait_ge(c_in, 64)
            dve.tensor_copy(core.ident_bf[:], core.ident[:])
            dve.tensor_copy(core.mask_bf[:].rearrange("p (i k) -> p i k", k=SEQ),
                            mask_in[:].rearrange("p (i k) -> p i k", i=1).broadcast_to([P, IMG_T, SEQ]))
            looped(dve, TILES // 2, pair)
            finish(1, TILES - 1)

        @block.tensor
        def _(pe):
            pe.wait_ge(w_split, 2)

            def hidden(u, t):
                pe.wait_ge(x_lo, t + 1)
                at_least(pe, silu, t - 1)
                for m in range(KD):
                    for k in range(KP):
                        last = product3(pe, p_hid[u][:, m, :], [w[:, k, m * P:(m + 1) * P] for w in w1],
                                        [v[:, k, :] for v in xs[u]], start=k == 0, stop=k == KP - 1)
                last.then_inc(hid, 1)

            def output(u, t):
                pe.wait_ge(act_lo, t + 1)
                at_least(pe, h_done, t - 1)
                for c in range(CH):
                    for k in range(KD):
                        last = product3(pe, p_out[u][:, c, :], [a[:, k, c * P:(c + 1) * P] for a in acts],
                                        [w[:, k, :] for w in w2], start=k == 0, stop=k == KD - 1)
                last.then_inc(outp, 1)

            def pair(t2, last=False):
                for u in range(2):
                    t = 2 * t2 + u
                    hidden(u, t)
                    if not (isinstance(t, int) and t == 0):
                        output(1 - u, t - 1)

            looped(pe, TILES // 2, pair)
            output(1, TILES - 1)


def statistics_phase(core):
    nc = core.nc
    with ExitStack() as ctx:
        st = core.sb(ctx, "ss_st", [P, BLOCKS, DVE_BN])
        stats = core.sem("ss_stats")
        block = ctx.enter_context(nc.Block())

        @block.vector
        def _(dve):
            row_statistics(dve, core, st, stats, 0, 0, BLOCKS)


def inverse_deviation(core, dve_or_act, who, var_eps, sems):
    eps_done, root_done, rstd_done = sems
    if who == "dve":
        dve_or_act.tensor_scalar(var_eps[:], core.mv[:, :, 1], EPS, None, ALU.add).then_inc(eps_done, 1)
        dve_or_act.wait_ge(root_done, 1)
        dve_or_act.reciprocal(core.rstd[:], var_eps[:]).then_inc(rstd_done, 1)
        dve_or_act.wait_ge(rstd_done, 1)
    else:
        dve_or_act.wait_ge(eps_done, 1)
        dve_or_act.activation(var_eps[:], var_eps[:], ACT.Sqrt).then_inc(root_done, 1)


def normalise(dve, core, xn, t):
    for c in range(CH):
        block = bass.ds(CH * t + c, 1)
        last = dve.tensor_scalar(xn[:, c, :], core.h[:, block, :].rearrange("p a n -> p (a n)"),
                                 core.mv[:, block, 0:1].rearrange("p a n -> p (a n)"), core.rstd[:, block],
                                 ALU.subtract, ALU.mult)
    return last


def turn(pe, core, out, xn):
    for k in range(KD):
        for c in range(CH):
            last = pe.transpose(out[:, k, c * P:(c + 1) * P], xn[:, c, k * P:(k + 1) * P], core.ident[:])
    return last


class Chain:

    def __init__(self, eng, sem):
        self.eng, self.sem, self.n = eng, sem, 0

    def __call__(self, instruction):
        self.n += 1
        instruction.then_inc(self.sem, 1)
        self.eng.wait_ge(self.sem, self.n)


def choose(dve, then, b, vals, top, width, k):
    for n in range(BLOCKS):
        last = dve.max(top[:, n, :], vals[:, n, :])
    then(last)
    shape = [P, BLOCKS, width]
    kth = top[:, :, k - 1:k].broadcast_to(shape)
    above, equal, rank, sel = (b[n][:, :, 0:width] for n in ("above", "equal", "rank", "sel"))
    dve.tensor_tensor(above, vals, kth, ALU.is_gt)
    then(dve.tensor_tensor(equal, vals, kth, ALU.is_equal))
    then(dve.tensor_reduce(b["count"][:], above, AX.X, ALU.add))
    flat = lambda a: a.rearrange("p b e -> p (b e)")
    then(dve.tensor_tensor_scan(flat(rank), flat(b["restart"][:]), flat(equal), 0.0, ALU.mult, ALU.add))
    then(dve.tensor_tensor(rank, rank, b["count"][:].rearrange("p (b e) -> p b e", e=1).broadcast_to(shape), ALU.add))
    then(dve.tensor_scalar(rank, rank, float(k), None, ALU.is_le))
    then(dve.tensor_tensor(equal, equal, rank, ALU.mult))
    then(dve.tensor_tensor(sel, equal, above, ALU.add))


def experts_phase(core, layer, experts, width, top_k, out=None):
    nc, d = core.nc, core.dram
    name = f"e{layer}_"
    with ExitStack() as ctx:
        sb = lambda n, shape, dt=F32: core.sb(ctx, name + n, shape, dt)
        sem = lambda n: core.sem(name + n)
        xt = [sb("xt_hi", [P, KD, TOKENS], F32R), sb("xt_lo", [P, KD, TOKENS], F32R)]
        xn = [sb(f"xn{i}", [P, CH, D]) for i in range(2)]
        var_eps = sb("var_eps", [P, BLOCKS])
        wr_in = sb("wr_in", [P, KD, width])
        wr = [sb("wr_hi", [P, KD, width], F32R), sb("wr_lo", [P, KD, width], F32R)]
        bias = [sb(f"bias{i}", [P, width]) for i in range(2)]
        lg_t = [sb(f"lg_t{i}", [width, TILE]) for i in range(2)]
        comb = sb("comb", [P, BLOCKS, width])
        scores = sb("scores", [P, BLOCKS, width])
        b = {n: sb(n, [P, BLOCKS, width]) for n in ("above", "equal", "rank", "sel", "restart", "vals")}
        b["count"] = sb("count", [P, BLOCKS])
        top = sb("top", [P, BLOCKS, 8])
        if layer == 1:
            group_b = {n: sb("g_" + n, [P, BLOCKS, 8]) for n in ("above", "equal", "rank", "sel", "restart", "vals")}
            group_b["count"] = sb("g_count", [P, BLOCKS])
            pick = [sb(f"pick{i}", [P, BLOCKS, 4]) for i in range(4)]
        w_in = [sb(f"w_in{i}", [P, WCOLS]) for i in range(2)]
        w = [[sb(f"w_hi{i}", [P, WCOLS], F32R), sb(f"w_lo{i}", [P, WCOLS], F32R)] for i in range(2)]
        gated = [sb(f"gated{i}", [P, TILE]) for i in range(2)]
        hid = [sb(f"hid{i}", [P, TILE]) for i in range(2)]
        hids = [[sb(f"hid_hi{i}", [P, TILE], F32R), sb(f"hid_lo{i}", [P, TILE], F32R)] for i in range(2)]
        p_gu = [core.ps(ctx, name + f"gu{i}", [P, 2, TILE]) for i in range(2)]
        p_dn = [core.ps(ctx, name + f"dn{i}", [P, CH, D]) for i in range(2)]

        s_in, s_split = sem("small_in"), sem("small_split")
        norm_sems = (sem("eps"), sem("root"), sem("rstd"))
        xn_done, turned, xt_hi, xt_lo = sem("xn_done"), sem("turned"), sem("xt_hi"), sem("xt_lo")
        lg_done, lg_out, lg_back, logits = sem("lg_done"), sem("lg_out"), sem("lg_back"), sem("logits")
        sig, route = sem("sig"), sem("route")
        w_here = [sem("w_here0"), sem("w_here1")]
        w_split = sem("w_split")
        gate, up, silu, gated_up, hid_hi, hid_lo = (sem(n) for n in ("gate", "up", "silu", "gated_up", "hid_hi", "hid_lo"))
        down, added, stored = sem("down"), sem("added"), sem("stored")

        def tile_loops(eng, pair, drain):
            def rest(e, par):
                with eng.Fori(1, TILES // 2) as t2:
                    pair(e, par, t2, par)

            pair(0, 0, 0, None)
            with eng.Fori(0, experts // 2 - 1) as e2:
                rest(2 * e2, 0)
                pair(2 * e2 + 1, 1, 0, 0)
                rest(2 * e2 + 1, 1)
                pair(2 * e2 + 2, 0, 0, 1)
            rest(experts - 2, 0)
            pair(experts - 1, 1, 0, 0)
            rest(experts - 1, 1)
            drain()

        block = ctx.enter_context(nc.Block())

        @block.sync
        def _(sp):
            w_d = d[f"we{layer}"]
            for e in range(2):
                sp.dma_start(w_in[e][:], w_d[e]).then_inc(w_here[e], 16)
            with sp.Fori(1, experts // 2) as e2:
                for par in range(2):
                    sp.wait_ge(w_split, 2 * (2 * e2 + par - 1))
                    sp.dma_start(w_in[par][:], w_d[bass.ds(2 * e2 + par, 1)].rearrange("a p n -> (a p) n"))\
                        .then_inc(w_here[par], 16)
            if out is not None:
                for t in range(TILES):
                    sp.wait_ge(added, (experts - 1) * TILES + t + 1)
                    rows = slice(CH * t, CH * (t + 1))
                    sp.dma_start(out[:, rows, :], core.h[:, rows, :]).then_inc(stored, 16)
                sp.wait_ge(stored, 16 * TILES)

        @block.gpsimd
        def _(pool):
            pool.wait_ge(s_in, 48)
            pool.tensor_copy(wr[0][:], wr_in[:]).then_inc(s_split, 1)
            pool.wait_ge(s_split, 1)
            pool.tensor_tensor(wr[1][:], wr_in[:], wr[0][:].bitcast(F32), ALU.subtract).then_inc(s_split, 1)
            for which in [b] + ([group_b] if layer == 1 else []):
                pool.memset(which["restart"][:], 1.0)
            pool.memset(b["vals"][:], -1.0).then_inc(s_split, 1)
            if layer == 1:
                pool.memset(group_b["vals"][:], NEG).then_inc(s_split, 1)
            pool.wait_ge(s_split, 4 if layer == 1 else 3)
            for which in [b] + ([group_b] if layer == 1 else []):
                pool.memset(which["restart"][:, :, 0:1], 0.0).then_inc(s_split, 1)

            def split_weights(e2, par):
                e = 2 * e2 + par
                hold(pool, w_here[par], 16 * e2 + 16)
                if not (isinstance(e2, int) and e2 == 0):
                    hold(pool, down, TILES * (e - 1))
                pool.tensor_copy(w[par][0][:], w_in[par][:]).then_inc(w_split, 1)
                hold(pool, w_split, 2 * e + 1)
                pool.tensor_tensor(w[par][1][:], w_in[par][:], w[par][0][:].bitcast(F32), ALU.subtract)\
                    .then_inc(w_split, 1)

            split_weights(0, 0)
            split_weights(0, 1)
            with pool.Fori(1, experts // 2) as e2:
                split_weights(e2, 0)
                split_weights(e2, 1)

        @block.scalar
        def _(act):
            act.dma_start(wr_in[:], d[f"wr{layer}"]).then_inc(s_in, 16)
            for i in range(2):
                act.dma_start(bias[i][:], d[f"rb{layer}"][i].partition_broadcast(P)).then_inc(s_in, 16)
            inverse_deviation(core, act, "act", var_eps, norm_sems)

            def norm_pair(t2, last=False):
                for u in range(2):
                    t = 2 * t2 + u
                    hold(act, turned, t + 1)
                    act.copy(xt[0][:, :, bass.ds(TILE * t, TILE)], p_gu[u][:]).then_inc(xt_hi, 1)
                    act.wait_ge(lg_done, t + 1)
                    at_least(act, lg_back, t - 1)
                    act.copy(lg_t[u][:], p_dn[0][0:width].rearrange("p c n -> p (c n)")[:, 0:TILE]).then_inc(lg_out, 1)

            looped(act, TILES // 2, norm_pair)
            act.wait_ge(logits, TILES + 1)
            act.activation(scores[:], comb[:], ACT.Sigmoid).then_inc(sig, 1)

            def pair(e, par, t2, prev):
                for u in range(2):
                    n = TILES * e + 2 * t2 + u
                    act.wait_ge(gate, n + 1)
                    at_least(act, gated_up, n - 1)
                    act.activation(gated[u][:], p_gu[u][:, 0, :], ACT.Silu).then_inc(silu, 1)
                    act.wait_ge(gated_up, n + 1)
                    at_least(act, down, n - 1)
                    act.copy(hids[u][0][:], hid[u][:]).then_inc(hid_hi, 1)

            tile_loops(act, pair, lambda: None)

        @block.vector
        def _(dve):
            inverse_deviation(core, dve, "dve", var_eps, norm_sems)
            dve.wait_ge(s_in, 48)

            def take(u, t):
                dve.wait_ge(xt_hi, t + 1)
                cols = bass.ds(TILE * t, TILE)
                dve.tensor_tensor(xt[1][:, :, cols], p_gu[u][:], xt[0][:, :, cols].bitcast(F32), ALU.subtract)\
                   .then_inc(xt_lo, 1)

            def take_logits(t):
                dve.wait_ge(lg_back, t + 1)
                dve.tensor_tensor(comb[:, bass.ds(CH * t, CH), :],
                                  p_dn[1][:].rearrange("p c n -> p (c n)")[:, 0:CH * width].rearrange("p (c n) -> p c n", n=width),
                                  bias[0][:].rearrange("p (c n) -> p c n", c=1).broadcast_to([P, CH, width]),
                                  ALU.add).then_inc(logits, 1)

            def norm_pair(t2, last=False):
                for u in range(2):
                    t = 2 * t2 + u
                    if u == 0 or not last:
                        if isinstance(t, int):
                            at_least(dve, turned, t)
                        else:
                            hold(dve, turned, t)
                        normalise(dve, core, xn[1 - u], t + 1).then_inc(xn_done, 1)
                    take(u, t)
                    if not (isinstance(t, int) and t == 0):
                        take_logits(t - 1)

            normalise(dve, core, xn[0], 0).then_inc(xn_done, 1)
            looped(dve, TILES // 2, norm_pair)
            take_logits(TILES - 1)
            dve.wait_ge(logits, TILES)
            if layer == 0:
                dve.tensor_tensor(comb[:], comb[:], bias[1][:].rearrange("p (c n) -> p c n", c=1).broadcast_to([P, BLOCKS, width]),
                                  ALU.add).then_inc(logits, 1)
            else:
                dve.tensor_scalar(comb[:], comb[:], 1.0, None, ALU.mult).then_inc(logits, 1)
            dve.wait_ge(sig, 1)
            dve.wait_ge(s_split, 6 if layer == 1 else 4)
            then = Chain(dve, route)
            if layer == 0:
                real = experts - 1
                then(dve.tensor_copy(b["vals"][:, :, 0:real], scores[:, :, 0:real]))
            else:
                shape = [P, BLOCKS, width]
                vals = b["vals"]
                then(dve.tensor_tensor(vals[:], scores[:], bias[1][:].rearrange("p (c n) -> p c n", c=1).broadcast_to(shape), ALU.add))
                member = lambda i: vals[:].rearrange("p b (g m) -> p b g m", m=4)[:, :, :, i]
                dve.tensor_tensor(pick[0][:], member(0), member(1), ALU.max)
                dve.tensor_tensor(pick[1][:], member(0), member(1), ALU.min)
                dve.tensor_tensor(pick[2][:], member(2), member(3), ALU.max)
                then(dve.tensor_tensor(pick[3][:], member(2), member(3), ALU.min))
                then(dve.tensor_tensor(pick[1][:], pick[1][:], pick[3][:], ALU.max))
                then(dve.tensor_tensor(pick[3][:], pick[0][:], pick[2][:], ALU.min))
                then(dve.tensor_tensor(pick[1][:], pick[1][:], pick[3][:], ALU.max))
                then(dve.tensor_tensor(pick[0][:], pick[0][:], pick[2][:], ALU.max))
                then(dve.tensor_tensor(group_b["vals"][:, :, 0:4], pick[0][:], pick[1][:], ALU.add))
                choose(dve, then, group_b, group_b["vals"][:], top, 8, 2)
                kept = group_b["sel"][:, :, 0:4]
                then(dve.tensor_scalar(pick[0][:], kept, -1.0, 1e9, ALU.add, ALU.mult))
                for g in range(4):
                    of_group = vals[:, :, 4 * g:4 * g + 4]
                    then(dve.tensor_tensor(of_group, of_group, kept[:, :, g:g + 1].broadcast_to([P, BLOCKS, 4]), ALU.mult))
                    then(dve.tensor_tensor(of_group, of_group, pick[0][:, :, g:g + 1].broadcast_to([P, BLOCKS, 4]), ALU.add))
            choose(dve, then, b, b["vals"][:], top, width, top_k)
            then(dve.tensor_tensor(comb[:], b["sel"][:], scores[:], ALU.mult))
            then(dve.tensor_reduce(b["count"][:], comb[:], AX.X, ALU.add))
            if layer == 1:
                then(dve.tensor_scalar(b["count"][:], b["count"][:], 1e-20, None, ALU.add))
            then(dve.reciprocal(b["count"][:], b["count"][:]))
            then(dve.tensor_tensor(comb[:], comb[:], b["count"][:].rearrange("p (b e) -> p b e", e=1).broadcast_to([P, BLOCKS, width]), ALU.mult))
            if layer == 0:
                then(dve.memset(comb[:, :, experts - 1:experts], 1.0))
            else:
                then(dve.tensor_scalar(comb[:], comb[:], 2.5, None, ALU.mult))

            def add(u, e, t):
                n = TILES * e + t
                dve.wait_ge(down, n + 1)
                for c in range(CH):
                    row = core.h[:, bass.ds(CH * t + c, 1), :].rearrange("p a n -> p (a n)")
                    weight = comb[:, bass.ds(CH * t + c, 1), bass.ds(e, 1)].rearrange("p a n -> p (a n)")
                    last = dve.scalar_tensor_tensor(row, p_dn[u][:, c, :], weight, row, ALU.mult, ALU.add)
                last.then_inc(added, 1)

            def pair(e, par, t2, prev):
                for u in range(2):
                    n = TILES * e + 2 * t2 + u
                    dve.wait_ge(silu, n + 1)
                    dve.wait_ge(up, n + 1)
                    at_least(dve, hid_hi, n - 1)
                    dve.tensor_tensor(hid[u][:], gated[u][:], p_gu[u][:, 1, :], ALU.mult).then_inc(gated_up, 1)
                    dve.wait_ge(hid_hi, n + 1)
                    at_least(dve, down, n - 1)
                    dve.tensor_tensor(hids[u][1][:], hid[u][:], hids[u][0][:].bitcast(F32), ALU.subtract).then_inc(hid_lo, 1)
                    if u == 1:
                        add(0, e, 2 * t2)
                    elif prev is not None:
                        same = not (isinstance(t2, int) and t2 == 0)
                        add(1, e if same else e - 1, 2 * t2 - 1 if same else TILES - 1)

            tile_loops(dve, pair, lambda: add(1, experts - 1, TILES - 1))

        @block.tensor
        def _(pe):
            pe.wait_ge(s_split, 2)

            def norm_pair(t2, last=False):
                for u in range(2):
                    t = 2 * t2 + u
                    pe.wait_ge(xn_done, t + 1)
                    at_least(pe, xt_lo, t - 1)
                    turn(pe, core, p_gu[u], xn[u]).then_inc(turned, 1)
                    if not (isinstance(t, int) and t == 0):
                        router_logits(t - 1)
                        logits_back(1 - u, t - 1)

            def router_logits(t):
                pe.wait_ge(xt_lo, t + 1)
                at_least(pe, lg_out, t)
                cols = bass.ds(TILE * t, TILE)
                for k in range(KD):
                    last = product3(pe, p_dn[0][0:width].rearrange("p c n -> p (c n)")[:, 0:TILE],
                                    [v[:, k, :] for v in wr], [v[:, k, cols] for v in xt], start=k == 0, stop=k == KD - 1)
                last.then_inc(lg_done, 1)

            def logits_back(u, t):
                at_least(pe, logits, t)
                hold(pe, lg_out, t + 1)
                for c in range(CH):
                    last = pe.transpose(p_dn[1][:].rearrange("p c n -> p (c n)")[:, c * width:(c + 1) * width],
                                        lg_t[u][:, c * P:(c + 1) * P], core.ident[0:width, 0:width])
                last.then_inc(lg_back, 1)

            looped(pe, TILES // 2, norm_pair)
            router_logits(TILES - 1)
            logits_back(1, TILES - 1)

            def projections(e, par, t, u, n):
                cols = bass.ds(TILE * t, TILE)
                at_least(pe, gated_up, n - 1)
                for m, done in ((0, gate), (1, up)):
                    for k in range(KD):
                        at = (m * KD + k) * P
                        last = product3(pe, p_gu[u][:, m, :], [v[:, at:at + P] for v in w[par]],
                                        [v[:, k, cols] for v in xt], start=k == 0, stop=k == KD - 1)
                    last.then_inc(done, 1)

            def down_product(prev, u, n):
                pe.wait_ge(hid_lo, n + 1)
                at_least(pe, added, n - 1)
                for c in range(CH):
                    last = product3(pe, p_dn[u][:, c, :], [v[:, c * P:(c + 1) * P] for v in hids[u]],
                                    [v[:, 2 * D:3 * D] for v in w[prev]])
                last.then_inc(down, 1)

            def pair(e, par, t2, prev):
                for u in range(2):
                    t = 2 * t2 + u
                    n = TILES * e + t
                    if isinstance(t2, int) and t2 == 0 and u == 0:
                        pe.wait_ge(w_split, 2 * (e + 1))
                        if prev is None:
                            pe.wait_ge(xt_lo, TILES)
                            pe.wait_ge(logits, TILES)
                    projections(e, par, t, u, n)
                    if u == 1:
                        down_product(par, 0, n - 1)
                    elif prev is not None:
                        down_product(prev, 1, n - 1)

            tile_loops(pe, pair, lambda: down_product(1, 1, experts * TILES - 1))


def attention_phase(core, layer):
    nc, d = core.nc, core.dram
    name = f"a{layer}_"
    nb = HB0 if layer == 0 else KD
    dk = DK0 if layer == 0 else DK1
    with ExitStack() as ctx:
        sb = lambda n, shape, dt=F32: core.sb(ctx, name + n, shape, dt)
        sem = lambda n: core.sem(name + n)
        PIECE = 1024
        pieces = 8 if layer == 0 else 4
        w_in = [sb(f"w_in{i}", [P, PIECE]) for i in range(2)]
        w = [sb("w_hi", [P, pieces * PIECE], F32R), sb("w_lo", [P, pieces * PIECE], F32R)]
        var_eps = sb("var_eps", [P, BLOCKS])
        xn = sb("xn", [P, CH, D])
        xt = [sb("xt_hi", [P, KD, TILE], F32R), sb("xt_lo", [P, KD, TILE], F32R)]
        kt = sb("kt", [P, nb, TILE])
        s = [sb(f"s{i}", [P, PAIRS, 2, SEQ]) for i in range(2)]
        mx, total = sb("mx", [P, 2 * PAIRS]), sb("total", [P, 2 * PAIRS])
        pt = sb("pt", [P, PAIRS, P])
        ot = [sb("ot_hi", [P, nb, 2, SEQ], F32R), sb("ot_lo", [P, nb, 2, SEQ], F32R)]
        st = sb("st", [P, CH, DVE_BN])
        if layer == 0:
            qt = sb("qt", [P, nb, TILE])
            v = sb("v", [P, CH, QKV0])
        else:
            qz = sb("qz", [P, KD, IMG_T, 2, SEQ])
            qg, kg = sb("qg", [P, KD, TILE]), sb("kg", [P, TILE])
            vz = sb("vz", [P, CH, PAIRS, 2, 2 * DK1])
            comp = sb("comp", [P, TILE])
            comps = [sb("comp_hi", [P, TILE], F32R), sb("comp_lo", [P, TILE], F32R)]
            rope = [sb(f"rope{i}", [P, TILE]) for i in range(4)]
            cos, sin = sb("cos", [P, SEQ]), sb("sin", [P, SEQ])
            head_mask = sb("head_mask", [P, 2])
            bias = sb("bias", [P, 9])
            bo = sb("bo", [P, D])
            out_b = sb("out_b", [P, nb, 2, SEQ])
            c_in, zeros = sem("c_in"), sem("zeros")
        p_s = core.ps(ctx, name + "S", [P, 2, TILE])
        p_t = core.ps(ctx, name + "T", [P, 2, TILE])
        p_o = core.ps(ctx, name + "O", [P, 2, TILE])
        p_j = core.ps(ctx, name + "J", [P, 2, TILE])

        norm_sems = (sem("eps"), sem("root"), sem("rstd"))
        w_here = [sem("w_here0"), sem("w_here1")]
        w_hi, w_lo = sem("w_hi_done"), sem("w_lo_done")
        xn_done, turned, xt_hi, xt_lo, residual = (sem(n) for n in ("xn_done", "turned", "xt_hi_done", "xt_lo_done", "residual"))
        q_mm, k_mm, v_mm, q_out, k_out, v_out = (sem(n) for n in ("q_mm", "k_mm", "v_mm", "q_out", "k_out", "v_out"))
        s_mm, max_done, s_out, exp_done, soft, p_done = (sem(n) for n in ("s_mm", "max", "s_out", "exp", "soft", "p_done"))
        t_mm, pt_out, o_mm, ot_hi, ot_lo, wo_mm, added, stats = (
            sem(n) for n in ("t_mm", "pt_out", "o_mm", "ot_hi_done", "ot_lo_done", "wo_mm", "added", "stats"))
        if layer == 1:
            comp_mm, comp_out, comp_hi, comp_lo = (sem(n) for n in ("comp_mm", "comp_out", "comp_hi_done", "comp_lo_done"))
            rope_mm, rope_out, rope_sum, q_gelu, out_bias, row_tile = (
                sem(n) for n in ("rope_mm", "rope_out", "rope_sum", "q_gelu", "out_bias", "row_tile"))

        if layer == 0:
            at_qk = lambda j, which, k: ((j * 2 + which) * KD + k) * P
            at_v = lambda k, half: 4 * PIECE + k * QKV0 + half * TILE
            at_o = lambda j: 6 * PIECE + j * D
        else:
            at_x = lambda i, k: (i * KD + k) * P
            at_qc, at_kc, at_v1 = 5 * D, 5 * D + P, 6 * D
            at_o = lambda j: 7 * D + j * D

        def weights(at, n):
            return [part[:, at:at + n] for part in w]

        block = ctx.enter_context(nc.Block())

        @block.sync
        def _(sp):
            for i in range(pieces):
                if i >= 2:
                    sp.wait_ge(w_lo, i - 1)
                sp.dma_start(w_in[i % 2][:], d[f"wa{layer}"][i]).then_inc(w_here[i % 2], 16)

        @block.gpsimd
        def _(pool):
            if layer == 1:
                pool.memset(vz[:], 0.0).then_inc(zeros, 1)
                pool.wait_ge(c_in, 80)

            def body(t):
                hold(pool, xn_done, t + 1)
                rows = core.h[:, bass.ds(CH * t, CH), :]
                other = xn[:] if layer == 0 else bo[:].rearrange("p (c n) -> p c n", c=1).broadcast_to([P, CH, D])
                pool.tensor_tensor(rows, rows, other, ALU.add).then_inc(residual, 1)

            with pool.Fori(0, TILES) as t:
                body(t)

        def wo_bank(c):
            return c % 2 if layer == 0 or c != 2 else 1

        def not_first(t):
            return not (isinstance(t, int) and t == 0)

        @block.scalar
        def _(act):
            if layer == 1:
                for dst, src in ((cos, "cos"), (sin, "sin"), (head_mask, "head_mask"), (bias, "bias1")):
                    act.dma_start(dst[:], d[src]).then_inc(c_in, 16)
                act.dma_start(bo[:], d["bo"].partition_broadcast(P)).then_inc(c_in, 16)
            inverse_deviation(core, act, "act", var_eps, norm_sems)
            for i in range(pieces):
                act.wait_ge(w_here[i % 2], 16 * (i // 2) + 16)
                act.copy(w[0][:, i * PIECE:(i + 1) * PIECE], w_in[i % 2][:]).then_inc(w_hi, 1)
            if layer == 1:
                act.wait_ge(c_in, 80)

            def exp(g, i):
                act.wait_ge(s_out, g + 1)
                buf = s[i]
                act.activation(buf[:], buf[:], ACT.Exp, scale=1.0 / math.sqrt(dk)).then_inc(exp_done, 1)

            def turned_out(g):
                act.wait_ge(t_mm, g + 1)
                act.copy(pt[:].rearrange("p j n -> p (j n)"), p_t[:].rearrange("p a n -> p (a n)")).then_inc(pt_out, 1)

            def output_high(g):
                if layer == 0:
                    act.wait_ge(o_mm, g + 1)
                    act.copy(ot[0][:], p_o[:].rearrange("p i (j q) -> p j i q", q=SEQ)).then_inc(ot_hi, 1)
                else:
                    act.wait_ge(out_bias, g + 1)
                    act.copy(ot[0][:], out_b[:]).then_inc(ot_hi, 1)

            def queries(t, lo, hi):
                for j in range(lo, hi):
                    act.wait_ge(q_mm, nb * t + j + 1)
                    act.copy(qt[:, j, :], p_j[:, 0, :]).then_inc(q_out, 1)

            def body(t, last=False):
                act.wait_ge(turned, t + 1)
                act.copy(xt[0][:].rearrange("p k n -> p (k n)"), p_t[:].rearrange("p a n -> p (a n)")).then_inc(xt_hi, 1)
                if layer == 0:
                    queries(t, 0, 4)
                else:
                    act.wait_ge(comp_mm, t + 1)
                    act.activation(comp[:], p_j[:, 0, :], ACT.Gelu, bias=bias[:, 0:1]).then_inc(comp_out, 1)
                    act.wait_ge(comp_out, t + 1)
                    act.copy(comps[0][:], comp[:]).then_inc(comp_hi, 1)
                    act.wait_ge(rope_sum, 2 * t + 1)
                    act.activation(qg[:, 1, :], rope[0][:], ACT.Gelu).then_inc(q_gelu, 1)
                    act.wait_ge(rope_sum, 2 * t + 2)
                    act.activation(kt[:, 1, :], rope[2][:], ACT.Gelu).then_inc(k_out, 1)
                if not_first(t):
                    turned_out(CH * t - 1)
                if layer == 0:
                    queries(t, 4, 8)
                else:
                    act.wait_ge(q_mm, t + 1)
                    act.activation(qg[:, 0, :], p_j[:, 0, :], ACT.Gelu, bias=bias[:, 5:6]).then_inc(q_gelu, 1)
                    act.wait_ge(k_mm, t + 1)
                    act.activation(kt[:, 0, :], p_j[:, 1, :], ACT.Gelu, bias=bias[:, 6:7]).then_inc(k_out, 1)
                if not_first(t):
                    output_high(CH * t - 1)
                if layer == 0:
                    for n in range(2 * CH):
                        act.wait_ge(v_mm, 2 * CH * t + n + 1)
                        act.copy(v[:, n // 2, (n % 2) * TILE:(n % 2 + 1) * TILE], p_j[:, n % 2, :]).then_inc(v_out, 1)
                else:
                    if not not_first(t):
                        act.wait_ge(zeros, 1)
                    for n in range(2):
                        act.wait_ge(v_mm, 2 * t + n + 1)
                        for c in range(2):
                            for par in range(2):
                                done = act.copy(vz[:, 2 * n + c, :, par, par * DK1:(par + 1) * DK1],
                                                p_j[:, n, c * D:(c + 1) * D].rearrange("p (j a f) -> p j a f", a=2, f=DK1)[:, :, par, :])
                        done.then_inc(v_out, 1)
                g = CH * t
                exp(g, 0)
                exp(g + 1, 1)
                turned_out(g)
                output_high(g)
                exp(g + 2, 0)
                turned_out(g + 1)
                output_high(g + 1)
                exp(g + 3, 1)
                turned_out(g + 2)
                output_high(g + 2)

            looped(act, TILES, body)
            turned_out(CH * TILES - 1)
            output_high(CH * TILES - 1)

        @block.vector
        def _(dve):
            inverse_deviation(core, dve, "dve", var_eps, norm_sems)
            normalise(dve, core, xn, 0).then_inc(xn_done, 1)
            for i in range(pieces):
                dve.wait_ge(w_hi, i + 1)
                part = slice(i * PIECE, (i + 1) * PIECE)
                dve.tensor_tensor(w[1][:, part], w_in[i % 2][:], w[0][:, part].bitcast(F32), ALU.subtract).then_inc(w_lo, 1)

            def keys(t, lo, hi):
                for j in range(lo, hi):
                    dve.wait_ge(k_mm, nb * t + j + 1)
                    dve.tensor_copy(kt[:, j, :], p_j[:, 1, :]).then_inc(k_out, 1)

            rows = lambda a: a[:].rearrange("p j i k -> p (j i) k")
            per_row = lambda a: a[:].rearrange("p (r k) -> p r k", k=1).broadcast_to([P, 2 * PAIRS, SEQ])

            def shift(g, i):
                scores = p_s[:].rearrange("p a (r k) -> p (a r) k", k=SEQ)
                if layer == 0:
                    dve.wait_ge(s_mm, g + 1)
                else:
                    dve.wait_ge(row_tile, 8 * g + 8)
                dve.tensor_reduce(mx[:], scores, AX.X, ALU.max).then_inc(max_done, 1)
                dve.wait_ge(max_done, g + 1)
                dve.tensor_tensor(rows(s[i]), scores, per_row(mx), ALU.subtract).then_inc(s_out, 1)

            def softmax(g, i):
                dve.wait_ge(exp_done, g + 1)
                dve.tensor_reduce(total[:], rows(s[i]), AX.X, ALU.add).then_inc(soft, 1)
                dve.wait_ge(soft, 2 * g + 1)
                dve.reciprocal(total[:], total[:]).then_inc(soft, 1)
                dve.wait_ge(soft, 2 * g + 2)
                dve.tensor_tensor(rows(s[i]), rows(s[i]), per_row(total), ALU.mult).then_inc(p_done, 1)

            def output_low(g):
                dve.wait_ge(ot_hi, g + 1)
                src = p_o[:].rearrange("p i (j q) -> p j i q", q=SEQ) if layer == 0 else out_b[:]
                dve.tensor_tensor(ot[1][:], src, ot[0][:].bitcast(F32), ALU.subtract).then_inc(ot_lo, 1)

            def output_bias(g):
                if layer == 1:
                    dve.wait_ge(o_mm, g + 1)
                    for j in range(nb):
                        done = dve.tensor_scalar(out_b[:, j], p_o[:, :, j * SEQ:(j + 1) * SEQ], bias[:, 7 + j:8 + j], None, ALU.add)
                    done.then_inc(out_bias, 1)

            def add(t, g, c):
                if c == 0:
                    dve.wait_ge(residual, t + 1)
                dve.wait_ge(wo_mm, g + 1)
                row = core.h[:, bass.ds(g, 1), :].rearrange("p a n -> p (a n)")
                dve.tensor_tensor(row, row, p_j[:, wo_bank(c), 0:D], ALU.add).then_inc(added, 1)

            def rotate(t, i):
                for m, (bank, table) in enumerate(((1, cos), (0, sin))):
                    dve.wait_ge(rope_mm, 4 * t + 2 * i + m + 1)
                    dve.scalar_tensor_tensor(rope[2 * i + m][:].rearrange("p (i n) -> p i n", n=SEQ),
                                             p_j[:, bank, :].rearrange("p (i n) -> p i n", n=SEQ),
                                             bias[:, 1 + 2 * i + m:2 + 2 * i + m],
                                             table[:].rearrange("p (i n) -> p i n", i=1).broadcast_to([P, IMG_T, SEQ]),
                                             ALU.add, ALU.mult).then_inc(rope_out, 1)
                dve.wait_ge(rope_out, 4 * t + 2 * i + 2)
                dve.tensor_tensor(rope[2 * i][:], rope[2 * i][:], rope[2 * i + 1][:], ALU.add).then_inc(rope_sum, 1)

            def spread(t, b, nth):
                dve.wait_ge(q_gelu, 2 * t + nth)
                for par in range(2):
                    done = dve.tensor_scalar(qz[:, b, :, par, :], qg[:, b, :].rearrange("p (i n) -> p i n", n=SEQ),
                                             head_mask[:, par:par + 1], None, ALU.mult)
                done.then_inc(q_out, 1)

            def body(t, last=False):
                dve.wait_ge(xt_hi, t + 1)
                dve.tensor_tensor(xt[1][:].rearrange("p k n -> p (k n)"), p_t[:].rearrange("p a n -> p (a n)"),
                                  xt[0][:].rearrange("p k n -> p (k n)").bitcast(F32), ALU.subtract).then_inc(xt_lo, 1)
                if layer == 0:
                    keys(t, 0, 4)
                else:
                    rotate(t, 0)
                    dve.wait_ge(comp_hi, t + 1)
                    dve.tensor_tensor(comps[1][:], comp[:], comps[0][:].bitcast(F32), ALU.subtract).then_inc(comp_lo, 1)
                    rotate(t, 1)
                    spread(t, 1, 1)
                if not_first(t):
                    add(t - 1, CH * t - 2, 2)
                if layer == 0:
                    keys(t, 4, 8)
                else:
                    spread(t, 0, 2)
                if not last:
                    hold(dve, residual, t + 1)
                    normalise(dve, core, xn, t + 1).then_inc(xn_done, 1)
                if not_first(t):
                    output_bias(CH * t - 1)
                    output_low(CH * t - 1)
                g = CH * t
                shift(g, 0)
                if not_first(t):
                    add(t - 1, g - 1, 3)
                    hold(dve, added, g)
                    row_statistics(dve, core, st, stats, t - 1, CH * (t - 1), CH)
                softmax(g, 0)
                shift(g + 1, 1)
                output_bias(g)
                softmax(g + 1, 1)
                output_low(g)
                shift(g + 2, 0)
                add(t, g, 0)
                output_bias(g + 1)
                softmax(g + 2, 0)
                output_low(g + 1)
                shift(g + 3, 1)
                add(t, g + 1, 1)
                output_bias(g + 2)
                softmax(g + 3, 1)
                output_low(g + 2)

            looped(dve, TILES, body)
            add(TILES - 1, CH * TILES - 2, 2)
            output_bias(CH * TILES - 1)
            output_low(CH * TILES - 1)
            add(TILES - 1, CH * TILES - 1, 3)
            dve.wait_ge(added, CH * TILES)
            row_statistics(dve, core, st, stats, TILES - 1, CH * (TILES - 1), CH)

        @block.tensor
        def _(pe):
            def project(bank, at, k_blocks=KD):
                for k in range(KD):
                    mm = product3(pe, p_j[:, bank, :], weights(at(k), P), [part[:, k, :] for part in xt],
                                  start=k == 0, stop=k == KD - 1)
                return mm

            def queries_keys(t, lo, hi):
                for j in range(lo, hi):
                    if j == 4 and not_first(t):
                        pe.wait_ge(added, CH * t - 1)
                        pe.wait_ge(k_out, nb * t + j)
                    elif j > 0:
                        pe.wait_ge(q_out, nb * t + j)
                        pe.wait_ge(k_out, nb * t + j)
                    project(0, lambda k: at_qk(j, 0, k)).then_inc(q_mm, 1)
                    project(1, lambda k: at_qk(j, 1, k)).then_inc(k_mm, 1)

            def first_part(t):
                pe.wait_ge(xn_done, t + 1)
                at_least(pe, pt_out, CH * t - 1)
                turn(pe, core, p_t, xn).then_inc(turned, 1)
                pe.wait_ge(xt_lo, t + 1)
                at_least(pe, added, CH * t - 2)
                if layer == 0:
                    queries_keys(t, 0, 4)
                else:
                    project(0, lambda k: at_x(0, k)).then_inc(comp_mm, 1)
                    project(1, lambda k: at_x(1, k)).then_inc(rope_mm, 1)
                    pe.wait_ge(comp_out, t + 1)
                    project(0, lambda k: at_x(2, k)).then_inc(rope_mm, 1)
                    pe.wait_ge(rope_out, 4 * t + 1)
                    project(1, lambda k: at_x(3, k)).then_inc(rope_mm, 1)
                    pe.wait_ge(rope_out, 4 * t + 2)
                    project(0, lambda k: at_x(4, k)).then_inc(rope_mm, 1)

            def second_part(t):
                if layer == 0:
                    queries_keys(t, 4, 8)
                else:
                    pe.wait_ge(comp_lo, t + 1)
                    pe.wait_ge(rope_out, 4 * t + 4)
                    product3(pe, p_j[:, 0, :], weights(at_qc, P), [c[:] for c in comps]).then_inc(q_mm, 1)
                    at_least(pe, added, CH * t - 1)
                    product3(pe, p_j[:, 1, :], weights(at_kc, P), [c[:] for c in comps]).then_inc(k_mm, 1)

            def value_part(t):
                if layer == 0:
                    for n in range(2 * CH):
                        c, half = n // 2, n % 2
                        if n < 2:
                            pe.wait_ge((q_out, k_out)[n], nb * (t + 1))
                        else:
                            pe.wait_ge(v_out, 2 * CH * t + n - 1)
                        for k in range(KD):
                            mm = product3(pe, p_j[:, half, :], [part[:, k, c * P:(c + 1) * P] for part in xt],
                                          weights(at_v(k, half), TILE), start=k == 0, stop=k == KD - 1)
                        mm.then_inc(v_mm, 1)
                else:
                    for n in range(2):
                        pe.wait_ge((q_gelu, k_out)[n], 2 * (t + 1))
                        for c in range(2):
                            rows = slice((2 * n + c) * P, (2 * n + c + 1) * P)
                            mm = product3(pe, p_j[:, n, c * D:(c + 1) * D], [part[:, rows] for part in comps], weights(at_v1, D))
                        mm.then_inc(v_mm, 1)

            def scores(t, g, c):
                if c == 0:
                    pe.wait_ge(q_out, nb * (t + 1))
                    pe.wait_ge(k_out, nb * (t + 1))
                at_least(pe, s_out, g)
                for bank in range(2):
                    pe.matmul(p_s[:, bank, :], core.ident_bf[:], core.mask_bf[:], start=True, stop=False, skip_group_check=True)
                if layer == 0:
                    for turn_of in range(2):
                        for n in range(8):
                            for bank in range(2):
                                head = (bank + turn_of) % 2
                                j, img = 4 * bank + n // 2, 2 * c + n % 2
                                rows, cols = slice(64 * head, 64 * head + 64), slice(img * SEQ, (img + 1) * SEQ)
                                mm = pe.matmul(p_s[rows, bank, n * SEQ:(n + 1) * SEQ], qt[rows, j, cols], kt[rows, j, cols],
                                               start=False, stop=True, skip_group_check=True)
                else:
                    for q in range(4):
                        rows = slice(32 * q, 32 * q + 32)
                        for bank in range(2):
                            if q > 0:
                                pe.wait_ge(row_tile, 8 * g + 2 * (q - 1) + bank + 1)
                            for i in range(2):
                                img, n = 2 * c + i, 2 * q + i
                                mm = pe.matmul(p_s[:, bank, n * SEQ:(n + 1) * SEQ],
                                               qz[rows, bank, img].rearrange("p a q -> p (a q)"),
                                               kt[rows, bank, img * SEQ:(img + 1) * SEQ], start=False, stop=True, skip_group_check=True)
                            mm.then_inc(row_tile, 1)
                    return
                mm.then_inc(s_mm, 1)

            def turn_probabilities(g, i):
                pe.wait_ge(p_done, g + 1)
                at_least(pe, pt_out, g)
                for j in range(PAIRS):
                    mm = pe.transpose(p_t[:, j // 4, (j % 4) * P:(j % 4 + 1) * P],
                                      s[i][:, j].rearrange("p i k -> p (i k)"), core.ident[:])
                mm.then_inc(t_mm, 1)

            def values(t, g, c):
                if c == 0:
                    pe.wait_ge(v_out, (2 * CH if layer == 0 else 2) * (t + 1))
                at_least(pe, ot_lo, g)
                hold(pe, pt_out, g + 1)
                if layer == 0:
                    for j in range(PAIRS):
                        for img in range(2):
                            for head in range(2):
                                rows = slice(64 * img, 64 * img + 64)
                                mm = pe.matmul(p_o[64 * head:64 * head + 64, img, j * SEQ:(j + 1) * SEQ],
                                               v[rows, c, (2 * j + head) * DK0:(2 * j + head + 1) * DK0],
                                               pt[rows, j, head * SEQ:(head + 1) * SEQ], start=True, stop=True)
                else:
                    for b in range(KD):
                        for head in range(2):
                            for q in range(4):
                                for img in range(2):
                                    rows = slice(64 * img, 64 * img + 64)
                                    mm = pe.matmul(p_o[32 * q:32 * q + 32, img, b * SEQ:(b + 1) * SEQ],
                                                   vz[rows, c, 4 * b + q, head, :], pt[rows, 4 * b + q, head * SEQ:(head + 1) * SEQ],
                                                   start=head == 0, stop=head == 1)
                mm.then_inc(o_mm, 1)

            def output(g, c):
                bank = wo_bank(c)
                pe.wait_ge(ot_lo, g + 1)
                for j in range(nb):
                    mm = product3(pe, p_j[:, bank, 0:D], [part[:, j].rearrange("p i q -> p (i q)") for part in ot],
                                  weights(at_o(j), D), start=j == 0, stop=j == nb - 1)
                mm.then_inc(wo_mm, 1)

            def body(t, last=False):
                g = CH * t
                first_part(t)
                if not_first(t):
                    turn_probabilities(g - 1, 1)
                    if layer == 0:
                        pe.wait_ge(q_out, nb * t + 4)
                    else:
                        pe.wait_ge(rope_out, 4 * t + 3)
                    output(g - 2, 2)
                second_part(t)
                if not_first(t):
                    values(t - 1, g - 1, 3)
                value_part(t)
                scores(t, g, 0)
                if not_first(t):
                    pe.wait_ge(v_out, (2 * CH if layer == 0 else 2) * (t + 1))
                    output(g - 1, 3)
                scores(t, g + 1, 1)
                turn_probabilities(g, 0)
                values(t, g, 0)
                scores(t, g + 2, 2)
                turn_probabilities(g + 1, 1)
                output(g, 0)
                values(t, g + 1, 1)
                scores(t, g + 3, 3)
                turn_probabilities(g + 2, 0)
                at_least(pe, added, g)
                output(g + 1, 1)
                values(t, g + 2, 2)

            pe.wait_ge(w_lo, pieces)
            looped(pe, TILES, body)
            g = CH * TILES
            turn_probabilities(g - 1, 1)
            pe.wait_ge(added, g - 2)
            output(g - 2, 2)
            values(TILES - 1, g - 1, 3)
            if layer == 1:
                pe.wait_ge(added, g - 1)
            output(g - 1, 3)



def rows_to_blocks(w):
    return w.reshape(w.shape[0] // P, P, w.shape[1]).transpose(1, 0, 2)


def pack_attention0(wq, wk, wv, wo):
    qk = np.stack([rows_to_blocks(w).reshape(P, KD, HB0, P) for w in (wq, wk)], axis=1)
    parts = [qk.transpose(0, 3, 1, 2, 4).reshape(P, -1), rows_to_blocks(wv).reshape(P, -1), rows_to_blocks(wo).reshape(P, -1)]
    flat = np.concatenate(parts, axis=1)
    return np.ascontiguousarray(flat.reshape(P, 8, 1024).transpose(1, 0, 2))


def swap_halves(w):
    half = w.shape[-1] // 2
    return np.concatenate([w[..., half:], w[..., :half]], axis=-1)


def rope_tables():
    inv = (1.0 / np.float32(10000.0) ** (np.arange(0, P, 2, dtype=np.float32) / np.float32(P))).astype(np.float32)
    freqs = np.arange(SEQ, dtype=np.float32)[:, None] * inv[None, :]
    emb = np.concatenate([freqs, freqs], axis=-1).T
    sign = np.where(np.arange(P) < P // 2, np.float32(-1), np.float32(1))[:, None]
    return np.ascontiguousarray(np.cos(emb)), np.ascontiguousarray(np.sin(emb) * sign)


def pack_attention1(w):
    comp = np.concatenate([w["wq"], w["wkv"]], axis=1)
    from_x = [comp, w["wqr"], swap_halves(w["wqr"]), w["wkr"], swap_halves(w["wkr"])]
    none = np.zeros_like
    parts = [rows_to_blocks(m).reshape(P, -1) for m in from_x]
    parts += [np.concatenate([w["wqc"], none(w["wqc"])]), np.concatenate([none(w["wkc"]), w["wkc"]]),
              np.concatenate([none(w["wv"]), w["wv"]]), rows_to_blocks(w["wo"]).reshape(P, -1)]
    flat = np.concatenate(parts, axis=1)
    flat = np.concatenate([flat, np.zeros((P, 4096 - flat.shape[1]), np.float32)], axis=1)
    bv = w["bv"].reshape(KD, P)
    bias = np.stack([np.concatenate([w["bq"], w["bkv"]]), w["bqr"], swap_halves(w["bqr"]), w["bkr"], swap_halves(w["bkr"]),
                     w["bqc"], w["bkc"], bv[0], bv[1]], axis=1)
    cos, sin = rope_tables()
    odd = (np.arange(P) // DK1) % 2
    return dict(wa1=np.ascontiguousarray(flat.reshape(P, 4, 1024).transpose(1, 0, 2)), bias1=np.ascontiguousarray(bias),
                bo=w["bo"].reshape(1, D), cos=cos, sin=sin,
                head_mask=np.stack([1 - odd, odd], axis=1).astype(np.float32))


def build(nc, dram, out):
    with ExitStack() as ctx:
        core = Core(nc, ctx, dram)
        patch_phase(core)
        attention_phase(core, 0)
        experts_phase(core, 0, E0, 8, 2)
        statistics_phase(core)
        attention_phase(core, 1)
        experts_phase(core, 1, E1, 16, 4, out=out)


def kernel(**inputs):
    from concourse import bacc
    from concourse.bass_utils import run_bass_kernel_spmd

    a = {k: np.asarray(v) for k, v in inputs.items()}
    arrays = {}
    x = a["x"].reshape(IMAGES, 3, 8, 16, 8, 16).transpose(1, 3, 5, 0, 2, 4).reshape(KP, P, TILES, TILE)
    arrays["x"] = x.transpose(2, 1, 0, 3)
    arrays["W1"], arrays["W2"] = rows_to_blocks(a["L0_tok_W1"]), rows_to_blocks(a["L0_tok_W2"])
    arrays["b1"], arrays["b2"] = a["L0_tok_b1"].reshape(KD, P).T, a["L0_tok_b2"]
    arrays["wa0"] = pack_attention0(*(a[f"L0_attn_W{n}"] for n in "qkvo"))
    arrays.update(pack_attention1({n: a[f"L1_attn_{n}"] for n in (
        "wq", "wqc", "wqr", "wkv", "wkr", "wkc", "wv", "wo", "bq", "bqc", "bqr", "bkv", "bkr", "bkc", "bv", "bo")}))
    arrays["bo"] = a["L1_attn_bo"]

    def pack_experts(gate, up, down):
        wide = [w.reshape(-1, KD, P, INNER).transpose(0, 2, 1, 3).reshape(-1, P, KD * INNER) for w in (gate, up)]
        return np.concatenate(wide + [down], axis=2)

    arrays["we0"] = pack_experts(*(np.concatenate([a[f"L0_ffn_r_{n}"], a[f"L0_ffn_sh_{n}"][None]]) for n in ("gate", "up", "down")))
    arrays["we1"] = pack_experts(*(a[f"L1_ffn_w_{n}"].transpose(0, 2, 1) for n in ("gate", "up", "down")))
    pad = lambda m: np.concatenate([m, np.zeros(m.shape[:-1] + (1,), m.dtype)], axis=-1)
    arrays["wr0"] = rows_to_blocks(pad(a["L0_ffn_w_r"]))
    arrays["rb0"] = np.stack([pad(a["L0_ffn_b_r"]), pad(a["L0_ffn_routing_bias"])])
    arrays["wr1"] = rows_to_blocks(a["L1_ffn_router_weight"].T)
    arrays["rb1"] = np.stack([np.zeros(E1, np.float32), a["L1_ffn_router_bias"]])
    arrays["ident"] = np.eye(P, dtype=np.float32)
    at = np.arange(SEQ)
    arrays["mask"] = np.tile(np.where(at[None, :] > at[:, None], np.float32(NEG), np.float32(0)), (2, 1))

    nc = bacc.Bacc("TRN2", target_bir_lowering=False, num_devices=1)
    arrays = {f"in_{k}": np.ascontiguousarray(v, dtype=np.float32) for k, v in arrays.items()}
    dram = {k[3:]: nc.dram_tensor(k, v.shape, F32, kind="ExternalInput").ap() for k, v in arrays.items()}
    out = nc.dram_tensor("out_h", (TOKENS, D), F32, kind="ExternalOutput").ap()
    build(nc, dram, out.rearrange("(b p) n -> p b n", p=P))
    r = run_bass_kernel_spmd(nc, [arrays], core_ids=[0])
    return r.results[0]["out_h"].reshape(IMAGES, SEQ, D)
```

```python
import math
from contextlib import ExitStack

import numpy as np
import concourse.bass as bass
from concourse import mybir

F32 = mybir.dt.float32
F32R = mybir.dt.float32r
BF16 = mybir.dt.bfloat16
ALU = mybir.AluOpType
ACT = mybir.ActivationFunctionType
AX = mybir.AxisListType

P = 128
D = 256
KD = D // P
IMAGES = 64
SEQ = 64
TOKENS = IMAGES * SEQ
TILE = 512
TILES = TOKENS // TILE
BLOCKS = TOKENS // P
CH = TILE // P
IMG_T = TILE // SEQ
PATCH = 3 * 16 * 16
KP = PATCH // P
EPS = 1e-5
NEG = -1e30

HEADS = 16
PAIRS = HEADS // 2
DK0 = 64
DK1 = D // HEADS
QKV0 = HEADS * DK0
HB0 = QKV0 // P

INNER = 128
WCOLS = 2 * D + D
E0, E1 = 8, 16
DVE_BN = 6


def at_least(eng, sem, value):
    if not isinstance(value, int) or value > 0:
        eng.wait_ge(sem, value)


def hold(eng, sem, value):
    eng.wait_ge(sem, value)
    eng.nop(nofuse=True)


def looped(eng, n, body):
    body(0)
    with eng.Fori(1, n - 1) as i:
        body(i)
    body(n - 1, last=True)


def row_statistics(dve, core, st, stats, step, block, count):
    for c in range(count):
        last = dve.bn_stats(st[:, c, :], core.h[:, bass.ds(block + c, 1), :].rearrange("p a n -> p (a n)"))
    last.then_inc(stats, 1)
    hold(dve, stats, 3 * step + 1)
    for c in range(count):
        last = dve.bn_aggr(st[:, c, 0:2], st[:, c, :])
    last.then_inc(stats, 1)
    dve.wait_ge(stats, 3 * step + 2)
    dve.tensor_scalar(core.mv[:, bass.ds(block, count), :], st[:, :, 0:2], 1.0, None, ALU.mult).then_inc(stats, 1)


def product3(eng, out, lhs, rhs, start=True, stop=True):
    terms = ((0, 0), (0, 1), (1, 0))
    for n, (a, b) in enumerate(terms):
        mm = eng.matmul(out, lhs[a], rhs[b], start=start and n == 0, stop=stop and n == len(terms) - 1)
    return mm


class Core:

    def __init__(self, nc, ctx, dram):
        self.nc, self.ctx, self.dram = nc, ctx, dram
        sb = self.sb
        self.h = sb(ctx, "h", [P, BLOCKS, D])
        self.mv = sb(ctx, "mv", [P, BLOCKS, 2])
        self.rstd = sb(ctx, "rstd", [P, BLOCKS])
        self.ident = sb(ctx, "ident", [P, P])
        self.ident_bf = sb(ctx, "ident_bf", [P, P], BF16)
        self.mask_bf = sb(ctx, "mask_bf", [P, TILE], BF16)

    def sb(self, ctx, name, shape, dt=F32):
        return ctx.enter_context(self.nc.sbuf_tensor(name, shape, dt))

    def ps(self, ctx, name, shape):
        return ctx.enter_context(self.nc.psum_tensor(name, shape, F32))

    def sem(self, name):
        return self.ctx.enter_context(self.nc.semaphore(name))


def patch_phase(core, stages, w_qk):
    nc, d = core.nc, core.dram
    with ExitStack() as ctx:
        sb = lambda name, shape, dt=F32: core.sb(ctx, "pa_" + name, shape, dt)
        sem = lambda name: core.sem("pa_" + name)
        w1_in, w2_in = sb("w1_in", [P, KP, D]), sb("w2_in", [P, KD, D])
        w1 = [sb("w1_hi", [P, KP, D], F32R), sb("w1_lo", [P, KP, D], F32R)]
        w2 = [sb("w2_hi", [P, KD, D], F32R), sb("w2_lo", [P, KD, D], F32R)]
        b1, b2 = sb("b1", [P, KD]), sb("b2", [P, D])
        mask_in = sb("mask_in", [P, SEQ])
        x = [sb(f"x{i}", [P, KP, TILE]) for i in range(2)]
        xs = [[sb(f"x_hi{i}", [P, KP, TILE], F32R), sb(f"x_lo{i}", [P, KP, TILE], F32R)] for i in range(2)]
        act = sb("act", [P, KD, TILE])
        acts = [sb("act_hi", [P, KD, TILE], F32R), sb("act_lo", [P, KD, TILE], F32R)]
        st = sb("st", [P, CH, DVE_BN])
        p_hid = [core.ps(ctx, f"pa_hid{i}", [P, KD, TILE]) for i in range(2)]
        p_out = [core.ps(ctx, f"pa_out{i}", [P, CH, D]) for i in range(2)]

        w_in, c_in = sem("w_in"), sem("c_in")
        x_in = [sem("x_in0"), sem("x_in1")]
        w_hi, w_split, consts = sem("w_hi"), sem("w_split"), sem("consts")
        x_hi, x_lo, hid, silu, act_hi, act_lo = (sem(n) for n in ("x_hi", "x_lo", "hid", "silu", "act_hi", "act_lo"))
        outp, h_done, stats = sem("outp"), sem("h_done"), sem("stats")
        qk_here, qk_split = [sem("qk_here0"), sem("qk_here1")], sem("qk_split")

        block = ctx.enter_context(nc.Block())

        @block.sync
        def _(sp):
            sp.dma_start(w1_in[:], d["W1"]).then_inc(w_in, 16)
            sp.dma_start(x[0][:], d["x"][0]).then_inc(x_in[0], 16)
            sp.dma_start(w2_in[:], d["W2"]).then_inc(w_in, 16)
            sp.dma_start(x[1][:], d["x"][1]).then_inc(x_in[1], 16)
            with sp.Fori(1, TILES // 2) as t2:
                for u in range(2):
                    sp.wait_ge(x_lo, 2 * t2 + u - 1)
                    sp.dma_start(x[u][:], d["x"][bass.ds(2 * t2 + u, 1)].rearrange("a p k n -> (a p) k n"))\
                        .then_inc(x_in[u], 16)

        @block.gpsimd
        def _(pool):
            split_pieces(pool, stages, w_qk, d["wa0"][0:4], 4, qk_here, qk_split)

        @block.scalar
        def _(act_e):
            act_e.dma_start(b1[:], d["b1"]).then_inc(c_in, 16)
            act_e.dma_start(b2[:], d["b2"].partition_broadcast(P)).then_inc(c_in, 16)
            act_e.dma_start(core.ident[:], d["ident"]).then_inc(c_in, 16)
            act_e.dma_start(mask_in[:], d["mask"]).then_inc(c_in, 16)
            act_e.wait_ge(w_in, 32)
            act_e.copy(w1[0][:], w1_in[:]).then_inc(w_hi, 1)
            act_e.copy(w2[0][:], w2_in[:]).then_inc(w_hi, 1)
            act_e.wait_ge(c_in, 64)

            def x_high(u, t2):
                act_e.wait_ge(x_in[u], 16 * t2 + 16)
                at_least(act_e, hid, 2 * t2 + u - 1)
                act_e.copy(xs[u][0][:], x[u][:]).then_inc(x_hi, 1)

            def pair(t2, last=False):
                for u in range(2):
                    t = 2 * t2 + u
                    if u == 0 or not last:
                        x_high(1 - u, t2 + u)
                    act_e.wait_ge(hid, t + 1)
                    at_least(act_e, act_lo, t)
                    for m in range(KD):
                        done = act_e.activation(act[:, m, :], p_hid[u][:, m, :], ACT.Silu, bias=b1[:, m:m + 1])
                    done.then_inc(silu, 1)
                    act_e.wait_ge(silu, t + 1)
                    at_least(act_e, outp, t)
                    act_e.copy(acts[0][:], act[:]).then_inc(act_hi, 1)

            x_high(0, 0)
            looped(act_e, TILES // 2, pair)

        @block.vector
        def _(dve):
            dve.wait_ge(w_hi, 2)
            dve.tensor_tensor(w1[1][:], w1_in[:], w1[0][:].bitcast(F32), ALU.subtract).then_inc(w_split, 1)
            dve.tensor_tensor(w2[1][:], w2_in[:], w2[0][:].bitcast(F32), ALU.subtract).then_inc(w_split, 1)

            def x_low(u, t):
                dve.wait_ge(x_hi, t + 1)
                dve.tensor_tensor(xs[u][1][:], x[u][:], xs[u][0][:].bitcast(F32), ALU.subtract).then_inc(x_lo, 1)

            def finish(u, t):
                dve.wait_ge(outp, t + 1)
                dve.tensor_tensor(core.h[:, bass.ds(CH * t, CH), :], p_out[u][:],
                                  b2[:].rearrange("p (c n) -> p c n", c=1).broadcast_to([P, CH, D]),
                                  ALU.add).then_inc(h_done, 1)
                hold(dve, h_done, t + 1)
                row_statistics(dve, core, st, stats, t, CH * t, CH)

            def pair(t2, last=False):
                for u in range(2):
                    t = 2 * t2 + u
                    if u == 0 or not last:
                        x_low(1 - u, t + 1)
                    dve.wait_ge(act_hi, t + 1)
                    dve.tensor_tensor(acts[1][:], act[:], acts[0][:].bitcast(F32), ALU.subtract).then_inc(act_lo, 1)
                    if not (isinstance(t, int) and t == 0):
                        finish(1 - u, t - 1)

            x_low(0, 0)
            dve.wait_ge(c_in, 64)
            dve.tensor_copy(core.ident_bf[:], core.ident[:])
            dve.tensor_copy(core.mask_bf[:].rearrange("p (i k) -> p i k", k=SEQ),
                            mask_in[:].rearrange("p (i k) -> p i k", i=1).broadcast_to([P, IMG_T, SEQ]))
            looped(dve, TILES // 2, pair)
            finish(1, TILES - 1)

        @block.tensor
        def _(pe):
            pe.wait_ge(w_split, 2)

            def hidden(u, t):
                pe.wait_ge(x_lo, t + 1)
                at_least(pe, silu, t - 1)
                for m in range(KD):
                    for k in range(KP):
                        last = product3(pe, p_hid[u][:, m, :], [w[:, k, m * P:(m + 1) * P] for w in w1],
                                        [v[:, k, :] for v in xs[u]], start=k == 0, stop=k == KP - 1)
                last.then_inc(hid, 1)

            def output(u, t):
                pe.wait_ge(act_lo, t + 1)
                at_least(pe, h_done, t - 1)
                for c in range(CH):
                    for k in range(KD):
                        last = product3(pe, p_out[u][:, c, :], [a[:, k, c * P:(c + 1) * P] for a in acts],
                                        [w[:, k, :] for w in w2], start=k == 0, stop=k == KD - 1)
                last.then_inc(outp, 1)

            def pair(t2, last=False):
                for u in range(2):
                    t = 2 * t2 + u
                    hidden(u, t)
                    if not (isinstance(t, int) and t == 0):
                        output(1 - u, t - 1)

            looped(pe, TILES // 2, pair)
            output(1, TILES - 1)


def inverse_deviation(core, dve_or_act, who, var_eps, sems):
    eps_done, root_done, rstd_done = sems
    if who == "dve":
        dve_or_act.tensor_scalar(var_eps[:], core.mv[:, :, 1], EPS, None, ALU.add).then_inc(eps_done, 1)
        dve_or_act.wait_ge(root_done, 1)
        dve_or_act.reciprocal(core.rstd[:], var_eps[:]).then_inc(rstd_done, 1)
        dve_or_act.wait_ge(rstd_done, 1)
    else:
        dve_or_act.wait_ge(eps_done, 1)
        dve_or_act.activation(var_eps[:], var_eps[:], ACT.Sqrt).then_inc(root_done, 1)


def normalise(dve, core, xn, t):
    for c in range(CH):
        block = bass.ds(CH * t + c, 1)
        last = dve.tensor_scalar(xn[:, c, :], core.h[:, block, :].rearrange("p a n -> p (a n)"),
                                 core.mv[:, block, 0:1].rearrange("p a n -> p (a n)"), core.rstd[:, block],
                                 ALU.subtract, ALU.mult)
    return last


def turn(pe, core, out, xn):
    for k in range(KD):
        for c in range(CH):
            last = pe.transpose(out[:, k, c * P:(c + 1) * P], xn[:, c, k * P:(k + 1) * P], core.ident[:])
    return last


class Chain:

    def __init__(self, eng, sem):
        self.eng, self.sem, self.n = eng, sem, 0

    def __call__(self, instruction):
        self.n += 1
        instruction.then_inc(self.sem, 1)
        self.eng.wait_ge(self.sem, self.n)


def choose(dve, then, b, vals, top, width, k):
    for n in range(BLOCKS):
        last = dve.max(top[:, n, :], vals[:, n, :])
    then(last)
    shape = [P, BLOCKS, width]
    kth = top[:, :, k - 1:k].broadcast_to(shape)
    above, equal, rank, sel = (b[n][:, :, 0:width] for n in ("above", "equal", "rank", "sel"))
    dve.tensor_tensor(above, vals, kth, ALU.is_gt)
    then(dve.tensor_tensor(equal, vals, kth, ALU.is_equal))
    then(dve.tensor_reduce(b["count"][:], above, AX.X, ALU.add))
    flat = lambda a: a.rearrange("p b e -> p (b e)")
    then(dve.tensor_tensor_scan(flat(rank), flat(b["restart"][:]), flat(equal), 0.0, ALU.mult, ALU.add))
    then(dve.tensor_tensor(rank, rank, b["count"][:].rearrange("p (b e) -> p b e", e=1).broadcast_to(shape), ALU.add))
    then(dve.tensor_scalar(rank, rank, float(k), None, ALU.is_le))
    then(dve.tensor_tensor(equal, equal, rank, ALU.mult))
    then(dve.tensor_tensor(sel, equal, above, ALU.add))


def experts_phase(core, layer, experts, width, top_k, out=None, next_w=None):
    nc, d = core.nc, core.dram
    name = f"e{layer}_"
    with ExitStack() as ctx:
        sb = lambda n, shape, dt=F32: core.sb(ctx, name + n, shape, dt)
        sem = lambda n: core.sem(name + n)
        xt = [sb("xt_hi", [P, KD, TOKENS], F32R), sb("xt_lo", [P, KD, TOKENS], F32R)]
        xn = [sb(f"xn{i}", [P, CH, D]) for i in range(2)]
        var_eps = sb("var_eps", [P, BLOCKS])
        wr_in = sb("wr_in", [P, KD, width])
        wr = [sb("wr_hi", [P, KD, width], F32R), sb("wr_lo", [P, KD, width], F32R)]
        bias = [sb(f"bias{i}", [P, width]) for i in range(2)]
        lg_t = [sb(f"lg_t{i}", [width, TILE]) for i in range(2)]
        comb = sb("comb", [P, BLOCKS, width])
        scores = sb("scores", [P, BLOCKS, width])
        b = {n: sb(n, [P, BLOCKS, width]) for n in ("above", "equal", "rank", "sel", "restart", "vals")}
        b["count"] = sb("count", [P, BLOCKS])
        top = sb("top", [P, BLOCKS, 8])
        if layer == 1:
            group_b = {n: sb("g_" + n, [P, BLOCKS, 8]) for n in ("above", "equal", "rank", "sel", "restart", "vals")}
            group_b["count"] = sb("g_count", [P, BLOCKS])
            pick = [sb(f"pick{i}", [P, BLOCKS, 4]) for i in range(4)]
        w_in = [sb(f"w_in{i}", [P, WCOLS]) for i in range(2)]
        w = [[sb(f"w_hi{i}", [P, WCOLS], F32R), sb(f"w_lo{i}", [P, WCOLS], F32R)] for i in range(2)]
        gated = [sb(f"gated{i}", [P, TILE]) for i in range(2)]
        hid = [sb(f"hid{i}", [P, TILE]) for i in range(2)]
        hids = [[sb(f"hid_hi{i}", [P, TILE], F32R), sb(f"hid_lo{i}", [P, TILE], F32R)] for i in range(2)]
        p_gu = [core.ps(ctx, name + f"gu{i}", [P, 2, TILE]) for i in range(2)]
        p_dn = [core.ps(ctx, name + f"dn{i}", [P, CH, D]) for i in range(2)]

        s_in, s_split = sem("small_in"), sem("small_split")
        norm_sems = (sem("eps"), sem("root"), sem("rstd"))
        xn_done, turned, xt_hi, xt_lo = sem("xn_done"), sem("turned"), sem("xt_hi"), sem("xt_lo")
        lg_done, lg_out, lg_back, logits = sem("lg_done"), sem("lg_out"), sem("lg_back"), sem("logits")
        sig, route = sem("sig"), sem("route")
        w_here = [sem("w_here0"), sem("w_here1")]
        w_split = sem("w_split")
        gate, up, silu, gated_up, hid_hi, hid_lo = (sem(n) for n in ("gate", "up", "silu", "gated_up", "hid_hi", "hid_lo"))
        down, added, stored = sem("down"), sem("added"), sem("stored")
        next_here, next_split, stats = [sem("next_here0"), sem("next_here1")], sem("next_split"), sem("stats")
        st = sb("st", [P, CH, DVE_BN])

        def tile_loops(eng, pair, drain):
            def rest(e, par):
                with eng.Fori(1, TILES // 2) as t2:
                    pair(e, par, t2, par)

            pair(0, 0, 0, None)
            with eng.Fori(0, experts // 2 - 1) as e2:
                rest(2 * e2, 0)
                pair(2 * e2 + 1, 1, 0, 0)
                rest(2 * e2 + 1, 1)
                pair(2 * e2 + 2, 0, 0, 1)
            rest(experts - 2, 0)
            pair(experts - 1, 1, 0, 0)
            rest(experts - 1, 1)
            drain()

        block = ctx.enter_context(nc.Block())

        @block.sync
        def _(sp):
            w_d = d[f"we{layer}"]
            for e in range(2):
                sp.dma_start(w_in[e][:], w_d[e]).then_inc(w_here[e], 16)
            with sp.Fori(1, experts // 2) as e2:
                for par in range(2):
                    sp.wait_ge(w_split, 2 * (2 * e2 + par - 1))
                    sp.dma_start(w_in[par][:], w_d[bass.ds(2 * e2 + par, 1)].rearrange("a p n -> (a p) n"))\
                        .then_inc(w_here[par], 16)
            if out is not None:
                for t in range(TILES):
                    sp.wait_ge(added, (experts - 1) * TILES + t + 1)
                    rows = slice(CH * t, CH * (t + 1))
                    sp.dma_start(out[:, rows, :], core.h[:, rows, :]).then_inc(stored, 16)
                sp.wait_ge(stored, 16 * TILES)

        @block.gpsimd
        def _(pool):
            pool.wait_ge(s_in, 48)
            pool.tensor_copy(wr[0][:], wr_in[:]).then_inc(s_split, 1)
            pool.wait_ge(s_split, 1)
            pool.tensor_tensor(wr[1][:], wr_in[:], wr[0][:].bitcast(F32), ALU.subtract).then_inc(s_split, 1)
            for which in [b] + ([group_b] if layer == 1 else []):
                pool.memset(which["restart"][:], 1.0)
            pool.memset(b["vals"][:], -1.0).then_inc(s_split, 1)
            if layer == 1:
                pool.memset(group_b["vals"][:], NEG).then_inc(s_split, 1)
            pool.wait_ge(s_split, 4 if layer == 1 else 3)
            for which in [b] + ([group_b] if layer == 1 else []):
                pool.memset(which["restart"][:, :, 0:1], 0.0).then_inc(s_split, 1)

            def split_weights(e2, par):
                e = 2 * e2 + par
                hold(pool, w_here[par], 16 * e2 + 16)
                if not (isinstance(e2, int) and e2 == 0):
                    hold(pool, down, TILES * (e - 1))
                pool.tensor_copy(w[par][0][:], w_in[par][:]).then_inc(w_split, 1)
                hold(pool, w_split, 2 * e + 1)
                pool.tensor_tensor(w[par][1][:], w_in[par][:], w[par][0][:].bitcast(F32), ALU.subtract)\
                    .then_inc(w_split, 1)

            split_weights(0, 0)
            split_weights(0, 1)
            if next_w is not None:
                split_pieces(pool, *next_w, d["wa1"], 4, next_here, next_split)
            with pool.Fori(1, experts // 2) as e2:
                split_weights(e2, 0)
                split_weights(e2, 1)

        @block.scalar
        def _(act):
            act.dma_start(wr_in[:], d[f"wr{layer}"]).then_inc(s_in, 16)
            for i in range(2):
                act.dma_start(bias[i][:], d[f"rb{layer}"][i].partition_broadcast(P)).then_inc(s_in, 16)
            inverse_deviation(core, act, "act", var_eps, norm_sems)

            def norm_pair(t2, last=False):
                for u in range(2):
                    t = 2 * t2 + u
                    hold(act, turned, t + 1)
                    act.copy(xt[0][:, :, bass.ds(TILE * t, TILE)], p_gu[u][:]).then_inc(xt_hi, 1)
                    act.wait_ge(lg_done, t + 1)
                    at_least(act, lg_back, t - 1)
                    act.copy(lg_t[u][:], p_dn[0][0:width].rearrange("p c n -> p (c n)")[:, 0:TILE]).then_inc(lg_out, 1)

            looped(act, TILES // 2, norm_pair)
            act.wait_ge(logits, TILES + 1)
            act.activation(scores[:], comb[:], ACT.Sigmoid).then_inc(sig, 1)

            def pair(e, par, t2, prev):
                for u in range(2):
                    n = TILES * e + 2 * t2 + u
                    act.wait_ge(gate, n + 1)
                    at_least(act, gated_up, n - 1)
                    act.activation(gated[u][:], p_gu[u][:, 0, :], ACT.Silu).then_inc(silu, 1)
                    act.wait_ge(gated_up, n + 1)
                    at_least(act, down, n - 1)
                    act.copy(hids[u][0][:], hid[u][:]).then_inc(hid_hi, 1)

            tile_loops(act, pair, lambda: None)

        @block.vector
        def _(dve):
            inverse_deviation(core, dve, "dve", var_eps, norm_sems)
            dve.wait_ge(s_in, 48)

            def take(u, t):
                dve.wait_ge(xt_hi, t + 1)
                cols = bass.ds(TILE * t, TILE)
                dve.tensor_tensor(xt[1][:, :, cols], p_gu[u][:], xt[0][:, :, cols].bitcast(F32), ALU.subtract)\
                   .then_inc(xt_lo, 1)

            def take_logits(t):
                dve.wait_ge(lg_back, t + 1)
                dve.tensor_tensor(comb[:, bass.ds(CH * t, CH), :],
                                  p_dn[1][:].rearrange("p c n -> p (c n)")[:, 0:CH * width].rearrange("p (c n) -> p c n", n=width),
                                  bias[0][:].rearrange("p (c n) -> p c n", c=1).broadcast_to([P, CH, width]),
                                  ALU.add).then_inc(logits, 1)

            def norm_pair(t2, last=False):
                for u in range(2):
                    t = 2 * t2 + u
                    if u == 0 or not last:
                        if isinstance(t, int):
                            at_least(dve, turned, t)
                        else:
                            hold(dve, turned, t)
                        normalise(dve, core, xn[1 - u], t + 1).then_inc(xn_done, 1)
                    take(u, t)
                    if not (isinstance(t, int) and t == 0):
                        take_logits(t - 1)

            normalise(dve, core, xn[0], 0).then_inc(xn_done, 1)
            looped(dve, TILES // 2, norm_pair)
            take_logits(TILES - 1)
            dve.wait_ge(logits, TILES)
            if layer == 0:
                dve.tensor_tensor(comb[:], comb[:], bias[1][:].rearrange("p (c n) -> p c n", c=1).broadcast_to([P, BLOCKS, width]),
                                  ALU.add).then_inc(logits, 1)
            else:
                dve.tensor_scalar(comb[:], comb[:], 1.0, None, ALU.mult).then_inc(logits, 1)
            dve.wait_ge(sig, 1)
            dve.wait_ge(s_split, 6 if layer == 1 else 4)
            then = Chain(dve, route)
            if layer == 0:
                real = experts - 1
                then(dve.tensor_copy(b["vals"][:, :, 0:real], scores[:, :, 0:real]))
            else:
                shape = [P, BLOCKS, width]
                vals = b["vals"]
                then(dve.tensor_tensor(vals[:], scores[:], bias[1][:].rearrange("p (c n) -> p c n", c=1).broadcast_to(shape), ALU.add))
                member = lambda i: vals[:].rearrange("p b (g m) -> p b g m", m=4)[:, :, :, i]
                dve.tensor_tensor(pick[0][:], member(0), member(1), ALU.max)
                dve.tensor_tensor(pick[1][:], member(0), member(1), ALU.min)
                dve.tensor_tensor(pick[2][:], member(2), member(3), ALU.max)
                then(dve.tensor_tensor(pick[3][:], member(2), member(3), ALU.min))
                then(dve.tensor_tensor(pick[1][:], pick[1][:], pick[3][:], ALU.max))
                then(dve.tensor_tensor(pick[3][:], pick[0][:], pick[2][:], ALU.min))
                then(dve.tensor_tensor(pick[1][:], pick[1][:], pick[3][:], ALU.max))
                then(dve.tensor_tensor(pick[0][:], pick[0][:], pick[2][:], ALU.max))
                then(dve.tensor_tensor(group_b["vals"][:, :, 0:4], pick[0][:], pick[1][:], ALU.add))
                choose(dve, then, group_b, group_b["vals"][:], top, 8, 2)
                kept = group_b["sel"][:, :, 0:4]
                then(dve.tensor_scalar(pick[0][:], kept, -1.0, 1e9, ALU.add, ALU.mult))
                for g in range(4):
                    of_group = vals[:, :, 4 * g:4 * g + 4]
                    then(dve.tensor_tensor(of_group, of_group, kept[:, :, g:g + 1].broadcast_to([P, BLOCKS, 4]), ALU.mult))
                    then(dve.tensor_tensor(of_group, of_group, pick[0][:, :, g:g + 1].broadcast_to([P, BLOCKS, 4]), ALU.add))
            choose(dve, then, b, b["vals"][:], top, width, top_k)
            then(dve.tensor_tensor(comb[:], b["sel"][:], scores[:], ALU.mult))
            then(dve.tensor_reduce(b["count"][:], comb[:], AX.X, ALU.add))
            if layer == 1:
                then(dve.tensor_scalar(b["count"][:], b["count"][:], 1e-20, None, ALU.add))
            then(dve.reciprocal(b["count"][:], b["count"][:]))
            then(dve.tensor_tensor(comb[:], comb[:], b["count"][:].rearrange("p (b e) -> p b e", e=1).broadcast_to([P, BLOCKS, width]), ALU.mult))
            if layer == 0:
                then(dve.memset(comb[:, :, experts - 1:experts], 1.0))
            else:
                then(dve.tensor_scalar(comb[:], comb[:], 2.5, None, ALU.mult))

            def add(u, e, t):
                n = TILES * e + t
                dve.wait_ge(down, n + 1)
                for c in range(CH):
                    row = core.h[:, bass.ds(CH * t + c, 1), :].rearrange("p a n -> p (a n)")
                    weight = comb[:, bass.ds(CH * t + c, 1), bass.ds(e, 1)].rearrange("p a n -> p (a n)")
                    last = dve.scalar_tensor_tensor(row, p_dn[u][:, c, :], weight, row, ALU.mult, ALU.add)
                last.then_inc(added, 1)
                if next_w is not None and isinstance(e, int) and e == experts - 1:
                    hold(dve, added, n + 1)
                    row_statistics(dve, core, st, stats, t, CH * t, CH)

            def pair(e, par, t2, prev):
                for u in range(2):
                    n = TILES * e + 2 * t2 + u
                    dve.wait_ge(silu, n + 1)
                    dve.wait_ge(up, n + 1)
                    at_least(dve, hid_hi, n - 1)
                    dve.tensor_tensor(hid[u][:], gated[u][:], p_gu[u][:, 1, :], ALU.mult).then_inc(gated_up, 1)
                    dve.wait_ge(hid_hi, n + 1)
                    at_least(dve, down, n - 1)
                    dve.tensor_tensor(hids[u][1][:], hid[u][:], hids[u][0][:].bitcast(F32), ALU.subtract).then_inc(hid_lo, 1)
                    if u == 1:
                        add(0, e, 2 * t2)
                    elif prev is not None:
                        same = not (isinstance(t2, int) and t2 == 0)
                        add(1, e if same else e - 1, 2 * t2 - 1 if same else TILES - 1)

            tile_loops(dve, pair, lambda: add(1, experts - 1, TILES - 1))

        @block.tensor
        def _(pe):
            pe.wait_ge(s_split, 2)

            def norm_pair(t2, last=False):
                for u in range(2):
                    t = 2 * t2 + u
                    pe.wait_ge(xn_done, t + 1)
                    at_least(pe, xt_lo, t - 1)
                    turn(pe, core, p_gu[u], xn[u]).then_inc(turned, 1)
                    if not (isinstance(t, int) and t == 0):
                        router_logits(t - 1)
                        logits_back(1 - u, t - 1)

            def router_logits(t):
                pe.wait_ge(xt_lo, t + 1)
                at_least(pe, lg_out, t)
                cols = bass.ds(TILE * t, TILE)
                for k in range(KD):
                    last = product3(pe, p_dn[0][0:width].rearrange("p c n -> p (c n)")[:, 0:TILE],
                                    [v[:, k, :] for v in wr], [v[:, k, cols] for v in xt], start=k == 0, stop=k == KD - 1)
                last.then_inc(lg_done, 1)

            def logits_back(u, t):
                at_least(pe, logits, t)
                hold(pe, lg_out, t + 1)
                for c in range(CH):
                    last = pe.transpose(p_dn[1][:].rearrange("p c n -> p (c n)")[:, c * width:(c + 1) * width],
                                        lg_t[u][:, c * P:(c + 1) * P], core.ident[0:width, 0:width])
                last.then_inc(lg_back, 1)

            looped(pe, TILES // 2, norm_pair)
            router_logits(TILES - 1)
            logits_back(1, TILES - 1)

            def projections(e, par, t, u, n):
                cols = bass.ds(TILE * t, TILE)
                at_least(pe, gated_up, n - 1)
                for m, done in ((0, gate), (1, up)):
                    for k in range(KD):
                        at = (m * KD + k) * P
                        last = product3(pe, p_gu[u][:, m, :], [v[:, at:at + P] for v in w[par]],
                                        [v[:, k, cols] for v in xt], start=k == 0, stop=k == KD - 1)
                    last.then_inc(done, 1)

            def down_product(prev, u, n):
                pe.wait_ge(hid_lo, n + 1)
                at_least(pe, added, n - 1)
                for c in range(CH):
                    last = product3(pe, p_dn[u][:, c, :], [v[:, c * P:(c + 1) * P] for v in hids[u]],
                                    [v[:, 2 * D:3 * D] for v in w[prev]])
                last.then_inc(down, 1)

            def pair(e, par, t2, prev):
                for u in range(2):
                    t = 2 * t2 + u
                    n = TILES * e + t
                    if isinstance(t2, int) and t2 == 0 and u == 0:
                        pe.wait_ge(w_split, 2 * (e + 1))
                        if prev is None:
                            pe.wait_ge(xt_lo, TILES)
                            pe.wait_ge(logits, TILES)
                    projections(e, par, t, u, n)
                    if u == 1:
                        down_product(par, 0, n - 1)
                    elif prev is not None:
                        down_product(prev, 1, n - 1)

            tile_loops(pe, pair, lambda: down_product(1, 1, experts * TILES - 1))


class Banks:

    def __init__(self, full, free, order, base=(0, 0), absent=()):
        self.full, self.free, self.order, self.base, self.absent = full, free, order, base, absent

    def before(self, t, place):
        bank = self.order[place]
        same = lambda places: sum(self.order[n] == bank for n in places)
        if isinstance(t, int) and t == 0:
            return self.base[bank] + same(n for n in range(place) if n not in self.absent)
        return t * same(range(len(self.order))) + self.base[bank] + same(range(place)) - same(self.absent)

    def wait_free(self, eng, t, place):
        at_least(eng, self.free[self.order[place]], self.before(t, place))

    def wait_full(self, eng, t, place):
        eng.wait_ge(self.full[self.order[place]], self.before(t, place) + 1)

    def wait_read(self, eng, t, place):
        eng.wait_ge(self.free[self.order[place]], self.before(t, place) + 1)


def row_groups(a):
    return a[:].rearrange("p j i k -> p (j i) k")


def per_row(a):
    return a[:].rearrange("p (r k) -> p r k", k=1).broadcast_to([P, 2 * PAIRS, SEQ])


def flat3(a):
    return a[:].rearrange("p a n -> p (a n)")


PIECE = 1024


def split_pieces(pool, w_in, w, src, pieces, here, done):
    for n in range(pieces):
        if n >= 2:
            pool.wait_ge(done, 2 * n - 2)
        pool.dma_start(w_in[n % 2][:], src[n]).then_inc(here[n % 2], 16)
        if n >= 1:
            split_piece(pool, w_in, w, n - 1, here, done)
    split_piece(pool, w_in, w, pieces - 1, here, done)


def split_piece(pool, w_in, w, n, here, done):
    cols = slice(n * PIECE, (n + 1) * PIECE)
    pool.wait_ge(here[n % 2], 16 * (n // 2) + 16)
    pool.tensor_copy(w[0][:, cols], w_in[n % 2][:]).then_inc(done, 1)
    pool.wait_ge(done, 2 * n + 1)
    pool.tensor_tensor(w[1][:, cols], w_in[n % 2][:], w[0][:, cols].bitcast(F32), ALU.subtract).then_inc(done, 1)


def attention0_phase(core, w_in, w_qk):
    nc, d = core.nc, core.dram
    nb = HB0
    with ExitStack() as ctx:
        sb = lambda n, shape, dt=F32: core.sb(ctx, "a0_" + n, shape, dt)
        sem = lambda n: core.sem("a0_" + n)
        w_vo = [sb("w_hi", [P, 4 * PIECE], F32R), sb("w_lo", [P, 4 * PIECE], F32R)]
        var_eps = sb("var_eps", [P, BLOCKS])
        xn = sb("xn", [P, CH, D])
        xt = [sb("xt_hi", [P, KD, TILE], F32R), sb("xt_lo", [P, KD, TILE], F32R)]
        qt, kt, v = sb("qt", [P, nb, TILE]), sb("kt", [P, nb, TILE]), sb("v", [P, CH, QKV0])
        s = [sb(f"s{i}", [P, PAIRS, 2, SEQ]) for i in range(CH)]
        mx, totals = sb("mx", [P, 2 * PAIRS]), [sb(f"total{i}", [P, 2 * PAIRS]) for i in range(CH)]
        pt = sb("pt", [P, PAIRS, P])
        ot = [sb("ot_hi", [P, nb, 2, SEQ], F32R), sb("ot_lo", [P, nb, 2, SEQ], F32R)]
        st = sb("st", [P, CH, DVE_BN])
        p_s, p_t, p_o, p_j = (core.ps(ctx, "a0_" + n, [P, 2, TILE]) for n in ("S", "T", "O", "J"))

        norm_sems = (sem("eps"), sem("root"), sem("rstd"))
        w_here, w_split = [sem("w_here0"), sem("w_here1")], sem("w_split")
        xn_done, turned, xt_hi, xt_lo, residual = (sem(n) for n in ("xn_done", "turned", "xt_hi_done", "xt_lo_done", "residual"))
        s_mm, max_done, s_out, exp_done, soft, p_done = (sem(n) for n in ("s_mm", "max", "s_out", "exp", "soft", "p_done"))
        t_mm, pt_out, o_mm, ot_hi, ot_lo, added, stats = (
            sem(n) for n in ("t_mm", "pt_out", "o_mm", "ot_hi_done", "ot_lo_done", "added", "stats"))

        Q = [0, 2, 5, 7, 10, 12, 15, 17]
        K = [n + 1 for n in Q]
        W = [4, 9, 14, 20]
        V = [19] + list(range(21, 28))
        j = Banks([sem("j_full0"), sem("j_full1")], [sem("j_free0"), sem("j_free1")],
                  [n % 2 for n in range(28)], absent=W)

        def tail_before(c):
            bank = j.order[W[c]]
            return j.before(TILES, j.order.index(bank)) + sum(j.order[place] == bank for place in W[:c])

        at_qk = lambda b, which, k: ((b * 2 + which) * KD + k) * P
        at_v = lambda k, half: k * QKV0 + half * TILE
        at_o = lambda b: 2 * PIECE + b * D

        def not_first(t):
            return not (isinstance(t, int) and t == 0)

        block = ctx.enter_context(nc.Block())

        @block.sync
        def _(sp):
            pass

        @block.gpsimd
        def _(pool):
            split_pieces(pool, w_in, w_vo, d["wa0"][4:8], 4, w_here, w_split)
            with pool.Fori(0, TILES) as t:
                hold(pool, xn_done, t + 1)
                rows = core.h[:, bass.ds(CH * t, CH), :]
                pool.tensor_tensor(rows, rows, xn[:], ALU.add).then_inc(residual, 1)

        @block.scalar
        def _(act):
            inverse_deviation(core, act, "act", var_eps, norm_sems)

            def projected(t, place, out):
                j.wait_full(act, t, place)
                bank = j.order[place]
                act.copy(out, p_j[:, bank, :]).then_inc(j.free[bank], 1)

            def exp(g, c):
                act.wait_ge(s_out, g + 1)
                act.activation(s[c][:], s[c][:], ACT.Exp, scale=1.0 / math.sqrt(DK0)).then_inc(exp_done, 1)

            def turned_out(g):
                act.wait_ge(t_mm, g + 1)
                act.copy(flat3(pt), flat3(p_t)).then_inc(pt_out, 1)

            def output_high(g):
                act.wait_ge(o_mm, g + 1)
                act.copy(ot[0][:], p_o[:].rearrange("p i (j q) -> p j i q", q=SEQ)).then_inc(ot_hi, 1)

            def body(t, last=False):
                act.wait_ge(turned, t + 1)
                act.copy(flat3(xt[0]), flat3(p_o)).then_inc(xt_hi, 1)
                for b in range(nb):
                    if not_first(t):
                        (turned_out, output_high)[b % 2](CH * (t - 1) + b // 2)
                    projected(t, Q[b], qt[:, b, :])
                    projected(t, K[b], kt[:, b, :])
                for c in range(CH):
                    for half in range(2):
                        projected(t, V[2 * c + half], v[:, c, half * TILE:(half + 1) * TILE])
                    exp(CH * t + c, c)

            looped(act, TILES, body)
            for c in range(CH):
                turned_out(CH * (TILES - 1) + c)
                output_high(CH * (TILES - 1) + c)

        @block.vector
        def _(dve):
            inverse_deviation(core, dve, "dve", var_eps, norm_sems)
            normalise(dve, core, xn, 0).then_inc(xn_done, 1)

            def shift(g, c):
                scores = p_s[:].rearrange("p a (r k) -> p (a r) k", k=SEQ)
                dve.wait_ge(s_mm, g + 1)
                dve.tensor_reduce(mx[:], scores, AX.X, ALU.max).then_inc(max_done, 1)
                dve.wait_ge(max_done, g + 1)
                dve.tensor_tensor(row_groups(s[c]), scores, per_row(mx), ALU.subtract).then_inc(s_out, 1)

            def softmax(g, c):
                total = totals[c]
                dve.wait_ge(exp_done, g + 1)
                dve.tensor_reduce(total[:], row_groups(s[c]), AX.X, ALU.add).then_inc(soft, 1)
                dve.wait_ge(soft, 2 * g + 1)
                dve.reciprocal(total[:], total[:]).then_inc(soft, 1)
                dve.wait_ge(soft, 2 * g + 2)
                dve.tensor_tensor(row_groups(s[c]), row_groups(s[c]), per_row(total), ALU.mult).then_inc(p_done, 1)

            def output_low(g):
                dve.wait_ge(ot_hi, g + 1)
                dve.tensor_tensor(ot[1][:], p_o[:].rearrange("p i (j q) -> p j i q", q=SEQ), ot[0][:].bitcast(F32), ALU.subtract)\
                   .then_inc(ot_lo, 1)

            def add(t, c, tail=False):
                bank = j.order[W[c]]
                if tail:
                    dve.wait_ge(j.full[bank], tail_before(c) + 1)
                else:
                    j.wait_full(dve, t, W[c])
                row = core.h[:, bass.ds(CH * (t - 1) + c, 1), :].rearrange("p a n -> p (a n)")
                dve.tensor_tensor(row, row, p_j[:, bank, 0:D], ALU.add).then_inc(j.free[bank], 1)

            def statistics(t):
                row_statistics(dve, core, st, stats, t, CH * t, CH)

            def body(t, last=False):
                dve.wait_ge(xt_hi, t + 1)
                dve.tensor_tensor(flat3(xt[1]), flat3(p_o), flat3(xt[0]).bitcast(F32), ALU.subtract).then_inc(xt_lo, 1)
                if not_first(t):
                    for c in (2, 3):
                        softmax(CH * (t - 1) + c, c)
                    output_low(CH * (t - 1))
                    dve.wait_ge(residual, t)
                    add(t, 0)
                    output_low(CH * (t - 1) + 1)
                if not last:
                    hold(dve, residual, t + 1)
                    normalise(dve, core, xn, t + 1).then_inc(xn_done, 1)
                if not_first(t):
                    add(t, 1)
                    output_low(CH * (t - 1) + 2)
                    add(t, 2)
                    output_low(CH * (t - 1) + 3)
                g = CH * t
                shift(g, 0)
                if not_first(t):
                    add(t, 3)
                shift(g + 1, 1)
                softmax(g, 0)
                shift(g + 2, 2)
                softmax(g + 1, 1)
                shift(g + 3, 3)
                if not_first(t):
                    bank = j.order[W[3]]
                    hold(dve, j.free[bank], j.before(t, W[3]) + 1)
                    statistics(t - 1)

            looped(dve, TILES, body)
            for c in (2, 3):
                softmax(CH * (TILES - 1) + c, c)
            dve.wait_ge(residual, TILES)
            for c in range(CH):
                output_low(CH * (TILES - 1) + c)
                add(TILES, c, tail=True)
            dve.wait_ge(j.free[j.order[W[1]]], tail_before(1) + 1)
            dve.wait_ge(j.free[j.order[W[3]]], tail_before(3) + 1)
            statistics(TILES - 1)

        @block.tensor
        def _(pe):
            def queries_keys(t, b):
                for which, place in enumerate((Q[b], K[b])):
                    bank = j.order[place]
                    j.wait_free(pe, t, place)
                    for k in range(KD):
                        at = at_qk(b, which, k)
                        mm = product3(pe, p_j[:, bank, :], [part[:, at:at + P] for part in w_qk], [part[:, k, :] for part in xt],
                                      start=k == 0, stop=k == KD - 1)
                    mm.then_inc(j.full[bank], 1)

            def values_in(t, n):
                c, half = n // 2, n % 2
                bank = j.order[V[n]]
                j.wait_free(pe, t, V[n])
                for k in range(KD):
                    at = at_v(k, half)
                    mm = product3(pe, p_j[:, bank, :], [part[:, k, c * P:(c + 1) * P] for part in xt],
                                  [part[:, at:at + TILE] for part in w_vo], start=k == 0, stop=k == KD - 1)
                mm.then_inc(j.full[bank], 1)

            def scores(t, g, c):
                if c == 0:
                    j.wait_read(pe, t, Q[-1])
                    j.wait_read(pe, t, K[-1])
                at_least(pe, s_out, g)
                for bank in range(2):
                    pe.matmul(p_s[:, bank, :], core.ident_bf[:], core.mask_bf[:], start=True, stop=False, skip_group_check=True)
                for turn_of in range(2):
                    for n in range(8):
                        for bank in range(2):
                            head = (bank + turn_of) % 2
                            b, img = 4 * bank + n // 2, 2 * c + n % 2
                            rows, cols = slice(64 * head, 64 * head + 64), slice(img * SEQ, (img + 1) * SEQ)
                            mm = pe.matmul(p_s[rows, bank, n * SEQ:(n + 1) * SEQ], qt[rows, b, cols], kt[rows, b, cols],
                                           start=False, stop=True, skip_group_check=True)
                mm.then_inc(s_mm, 1)

            def turn_probabilities(g, c):
                pe.wait_ge(p_done, g + 1)
                at_least(pe, pt_out, g)
                for b in range(PAIRS):
                    mm = pe.transpose(p_t[:, b // 4, (b % 4) * P:(b % 4 + 1) * P],
                                      s[c][:, b].rearrange("p i k -> p (i k)"), core.ident[:])
                mm.then_inc(t_mm, 1)

            def values(t, g, c):
                if c == 0:
                    j.wait_read(pe, t, V[-2])
                    j.wait_read(pe, t, V[-1])
                at_least(pe, ot_lo, g)
                hold(pe, pt_out, g + 1)
                for b in range(PAIRS):
                    for img in range(2):
                        for head in range(2):
                            rows = slice(64 * img, 64 * img + 64)
                            mm = pe.matmul(p_o[64 * head:64 * head + 64, img, b * SEQ:(b + 1) * SEQ],
                                           v[rows, c, (2 * b + head) * DK0:(2 * b + head + 1) * DK0],
                                           pt[rows, b, head * SEQ:(head + 1) * SEQ], start=True, stop=True)
                mm.then_inc(o_mm, 1)

            def output(t, c, tail=False):
                bank = j.order[W[c]]
                pe.wait_ge(ot_lo, CH * (t - 1) + c + 1)
                if tail:
                    pe.wait_ge(j.free[bank], tail_before(c))
                else:
                    j.wait_free(pe, t, W[c])
                for b in range(nb):
                    mm = product3(pe, p_j[:, bank, 0:D], [part[:, b].rearrange("p i q -> p (i q)") for part in ot],
                                  [part[:, at_o(b):at_o(b) + D] for part in w_vo], start=b == 0, stop=b == nb - 1)
                mm.then_inc(j.full[bank], 1)

            def body(t, last=False):
                g0 = CH * (t - 1)
                pe.wait_ge(xn_done, t + 1)
                at_least(pe, ot_lo, CH * t - CH)
                turn(pe, core, p_o, xn).then_inc(turned, 1)
                if not_first(t):
                    turn_probabilities(g0, 0)
                pe.wait_ge(xt_lo, t + 1)
                for b in range(nb):
                    queries_keys(t, b)
                    if not_first(t):
                        c = b // 2
                        if b % 2 == 0:
                            values(t - 1, g0 + c, c)
                        elif c < CH - 1:
                            output(t, c)
                            turn_probabilities(g0 + c + 1, c + 1)
                g = CH * t
                if not not_first(t):
                    pe.wait_ge(w_split, 8)
                values_in(t, 0)
                scores(t, g, 0)
                if not_first(t):
                    output(t, CH - 1)
                for c in range(CH):
                    if c > 0:
                        values_in(t, 2 * c)
                    values_in(t, 2 * c + 1)
                    if c < CH - 1:
                        scores(t, g + c + 1, c + 1)

            looped(pe, TILES, body)
            for c in range(CH):
                g = CH * (TILES - 1) + c
                turn_probabilities(g, c)
                values(TILES - 1, g, c)
                output(TILES, c, tail=True)


def attention1_phase(core, w):
    nc, d = core.nc, core.dram
    with ExitStack() as ctx:
        sb = lambda n, shape, dt=F32: core.sb(ctx, "a1_" + n, shape, dt)
        sem = lambda n: core.sem("a1_" + n)
        var_eps = sb("var_eps", [P, BLOCKS])
        xn = sb("xn", [P, CH, D])
        xt = [sb("xt_hi", [P, KD, TILE], F32R), sb("xt_lo", [P, KD, TILE], F32R)]
        comp = sb("comp", [P, TILE])
        comps = [sb("comp_hi", [P, IMG_T, 2, SEQ], F32R), sb("comp_lo", [P, IMG_T, 2, SEQ], F32R)]
        comp_twice = comp[:].rearrange("p (i a n) -> p i a n", a=1, n=SEQ).broadcast_to([P, IMG_T, 2, SEQ])
        rope = [sb(f"rope{i}", [P, TILE]) for i in range(4)]
        qt = [sb(f"qt{i}", [P, KD, TILE]) for i in range(2)]
        kz = [sb(f"kz{i}", [P, KD, IMG_T, 2, SEQ]) for i in range(2)]
        vz = [sb(f"vz{i}", [P, IMG_T, PAIRS, 2 * DK1]) for i in range(2)]
        s = [sb(f"s{i}", [P, PAIRS, 2, SEQ]) for i in range(CH)]
        mx, totals = sb("mx", [P, 2 * PAIRS]), [sb(f"total{i}", [P, 2 * PAIRS]) for i in range(CH)]
        pt = sb("pt", [P, PAIRS, P])
        ot = [sb("ot_hi", [P, KD, P], F32R), sb("ot_lo", [P, KD, P], F32R)]
        st = sb("st", [P, CH, DVE_BN])
        cos, sin, head_mask = sb("cos", [P, SEQ]), sb("sin", [P, SEQ]), sb("head_mask", [P, 2])
        bias = sb("bias", [P, 9])
        kc_bias = sb("kc_bias", [P, 2])
        bo = sb("bo", [P, D])
        p_s, p_t, p_j = (core.ps(ctx, "a1_" + n, [P, 2, TILE]) for n in ("S", "T", "J"))
        p_o, p_w = (core.ps(ctx, "a1_" + n, [P, TILE]) for n in ("O", "W"))

        norm_sems = (sem("eps"), sem("root"), sem("rstd"))
        c_in, zeros, kc_ready = sem("c_in"), sem("zeros"), sem("kc_bias_done")
        xn_done, turned, xt_hi, xt_lo, residual = (sem(n) for n in ("xn_done", "turned", "xt_hi_done", "xt_lo_done", "residual"))
        comp_hi, comp_lo, rope_sum, roped = (sem(n) for n in ("comp_hi_done", "comp_lo_done", "rope_sum", "roped"))
        row_tile, max_done, s_out, exp_done, summed, inverse, p_done = (
            sem(n) for n in ("row_tile", "max", "s_out", "exp", "summed", "inverse", "p_done"))
        t_mm, pt_out, o_mm, ot_hi, ot_lo, w_mm, added, stats = (
            sem(n) for n in ("t_mm", "pt_out", "o_mm", "ot_hi_done", "ot_lo_done", "w_mm", "added", "stats"))

        COMP, Q_ROPE, Q_SWAP, K_ROPE, K_SWAP, QC, KC = range(7)
        V = range(7, 11)
        j = Banks([sem("j_full0"), sem("j_full1")], [sem("j_free0"), sem("j_free1")], [n % 2 for n in range(11)])

        at_x = lambda i, k: (i * KD + k) * P
        at_qc, at_kc, at_v = 5 * D, 5 * D + P, 6 * D
        at_o = lambda b: 7 * D + b * D
        weights = lambda at, n: [part[:, at:at + n] for part in w]
        scored = lambda b, q: 4 * (q % 2) + 2 * (q // 2) + b

        def not_first(t):
            return not (isinstance(t, int) and t == 0)

        block = ctx.enter_context(nc.Block())

        @block.gpsimd
        def _(pool):
            for part in vz:
                done = pool.memset(part[:], 0.0)
            done.then_inc(zeros, 1)
            pool.wait_ge(c_in, 80)

            def add_bias(t):
                hold(pool, xn_done, t + 1)
                rows = core.h[:, bass.ds(CH * t, CH), :]
                pool.tensor_tensor(rows, rows, bo[:].rearrange("p (c n) -> p c n", c=1).broadcast_to([P, CH, D]), ALU.add)\
                    .then_inc(residual, 1)

            def probabilities(g, c):
                pool.wait_ge(inverse, g + 1)
                pool.tensor_tensor(row_groups(s[c]), row_groups(s[c]), per_row(totals[c]), ALU.mult).then_inc(p_done, 1)

            def rope_add(n, i, place):
                j.wait_read(pool, n, place - 1)
                j.wait_read(pool, n, place)
                pool.tensor_tensor(rope[i][:], rope[i][:], rope[i + 1][:], ALU.add).then_inc(rope_sum, 1)

            def pair(t2, last=False):
                for u in range(2):
                    t = 2 * t2 + u
                    g = CH * t
                    more = not (last and u == 1)
                    probabilities(g + 1, 1)
                    if more:
                        rope_add(t + 1, 0, Q_SWAP)
                    probabilities(g + 2, 2)
                    if more:
                        rope_add(t + 1, 2, K_SWAP)
                    probabilities(g + 3, 3)
                    if more:
                        add_bias(t + 1)
                        probabilities(g + 4, 0)

            add_bias(0)
            rope_add(0, 0, Q_SWAP)
            rope_add(0, 2, K_SWAP)
            probabilities(0, 0)
            looped(pool, TILES // 2, pair)

        @block.scalar
        def _(act):
            for dst, src in ((cos, "cos"), (sin, "sin"), (head_mask, "head_mask"), (bias, "bias1")):
                act.dma_start(dst[:], d[src]).then_inc(c_in, 16)
            act.dma_start(bo[:], d["bo"].partition_broadcast(P)).then_inc(c_in, 16)
            inverse_deviation(core, act, "act", var_eps, norm_sems)

            def turned_high(n):
                act.wait_ge(turned, n + 1)
                act.copy(flat3(xt[0]), flat3(p_j)).then_inc(xt_hi, 1)

            def compressed(n):
                j.wait_full(act, n, COMP)
                at_least(act, comp_lo, n)
                act.activation(comp[:], p_j[:, 0, :], ACT.Gelu, bias=bias[:, 0:1]).then_inc(j.free[0], 1)
                j.wait_read(act, n, COMP)
                act.copy(comps[0][:], comp_twice).then_inc(comp_hi, 1)

            def queries_keys(n, u):
                by_image = lambda a: a.rearrange("p (i n) -> p i n", n=SEQ)
                act.wait_ge(rope_sum, 2 * n + 2)
                act.activation(qt[u][:, 1, :], rope[0][:], ACT.Gelu)
                for head in range(2):
                    done = act.activation(kz[u][:, 1, :, head, :], by_image(rope[2][:]), ACT.Gelu, scale=head_mask[:, head:head + 1])
                done.then_inc(roped, 1)
                j.wait_full(act, n, QC)
                act.activation(qt[u][:, 0, :], p_j[:, 1, :], ACT.Gelu, bias=bias[:, 5:6]).then_inc(j.free[1], 1)
                j.wait_full(act, n, KC)
                for head in range(2):
                    done = act.activation(kz[u][:, 0, :, head, :], by_image(p_j[:, 0, :]), ACT.Gelu,
                                          scale=head_mask[:, head:head + 1], bias=kc_bias[:, head:head + 1])
                done.then_inc(j.free[0], 1)

            def values_out(n, u):
                for i, place in enumerate(V):
                    bank = j.order[place]
                    j.wait_full(act, n, place)
                    for head in range(2):
                        rows, cols = slice(SEQ * head, SEQ * (head + 1)), slice(head * DK1, (head + 1) * DK1)
                        done = act.copy(vz[u][rows, 2 * i:2 * i + 2, :, cols],
                                        p_j[rows, bank, :].rearrange("p (i j f) -> p i j f", i=2, f=2 * DK1)[:, :, :, cols])
                    done.then_inc(j.free[bank], 1)

            def exp(g, c):
                act.wait_ge(s_out, g + 1)
                act.activation(s[c][:], s[c][:], ACT.Exp, scale=1.0 / math.sqrt(DK1)).then_inc(exp_done, 1)

            def turned_out(g):
                act.wait_ge(t_mm, g + 1)
                act.copy(flat3(pt), flat3(p_t)).then_inc(pt_out, 1)

            def output_high(g):
                act.wait_ge(o_mm, g + 1)
                at_least(act, w_mm, g)
                for b in range(KD):
                    done = act.activation(ot[0][:, b], p_o[:, b * P:(b + 1) * P], ACT.Identity, bias=bias[:, 7 + b:8 + b])
                done.then_inc(ot_hi, 1)

            def pair(t2, last=False):
                for u in range(2):
                    t = 2 * t2 + u
                    g, n = CH * t, t + 1
                    more = not (last and u == 1)
                    turned_out(g)
                    output_high(g)
                    exp(g + 2, 2)

                    turned_out(g + 1)
                    if more:
                        queries_keys(n, 1 - u)
                    output_high(g + 1)

                    turned_out(g + 2)
                    exp(g + 3, 3)
                    if more:
                        values_out(n, 1 - u)
                        exp(g + 4, 0)
                    output_high(g + 2)

                    if not last:
                        turned_high(n + 1)
                    turned_out(g + 3)
                    output_high(g + 3)
                    if more:
                        exp(g + 5, 1)
                    if not last:
                        compressed(n + 1)

            turned_high(0)
            act.wait_ge(c_in, 80)
            compressed(0)
            act.wait_ge(kc_ready, 1)
            queries_keys(0, 0)
            act.wait_ge(zeros, 1)
            values_out(0, 0)
            exp(0, 0)
            turned_high(1)
            exp(1, 1)
            compressed(1)
            looped(act, TILES // 2, pair)

        @block.vector
        def _(dve):
            inverse_deviation(core, dve, "dve", var_eps, norm_sems)
            normalise(dve, core, xn, 0).then_inc(xn_done, 1)

            def turned_low(n):
                dve.wait_ge(xt_hi, n + 1)
                dve.tensor_tensor(flat3(xt[1]), flat3(p_j), flat3(xt[0]).bitcast(F32), ALU.subtract).then_inc(xt_lo, 1)

            def compressed_low(n):
                dve.wait_ge(comp_hi, n + 1)
                dve.tensor_tensor(comps[1][:], comp_twice, comps[0][:].bitcast(F32), ALU.subtract).then_inc(comp_lo, 1)

            def rotate(n, i):
                place = Q_ROPE + i
                bank, table = j.order[place], (cos, sin)[i % 2]
                j.wait_full(dve, n, place)
                at_least(dve, roped, n)
                dve.scalar_tensor_tensor(rope[i][:].rearrange("p (i n) -> p i n", n=SEQ),
                                         p_j[:, bank, :].rearrange("p (i n) -> p i n", n=SEQ), bias[:, 1 + i:2 + i],
                                         table[:].rearrange("p (i n) -> p i n", i=1).broadcast_to([P, IMG_T, SEQ]),
                                         ALU.add, ALU.mult).then_inc(j.free[bank], 1)

            def shift(g, c):
                scores = p_s[:].rearrange("p a (r k) -> p (a r) k", k=SEQ)
                dve.wait_ge(row_tile, 4 * g + 4)
                dve.tensor_reduce(mx[:], scores, AX.X, ALU.max).then_inc(max_done, 1)
                dve.wait_ge(max_done, g + 1)
                dve.tensor_tensor(row_groups(s[c]), scores, per_row(mx), ALU.subtract).then_inc(s_out, 1)

            def row_sums(g, c):
                dve.wait_ge(exp_done, g + 1)
                dve.tensor_reduce(totals[c][:], row_groups(s[c]), AX.X, ALU.add).then_inc(summed, 1)
                dve.wait_ge(summed, g + 1)
                dve.reciprocal(totals[c][:], totals[c][:]).then_inc(inverse, 1)

            def output_low(g):
                dve.wait_ge(ot_hi, g + 1)
                for b in range(KD):
                    done = dve.scalar_tensor_tensor(ot[1][:, b], p_o[:, b * P:(b + 1) * P], bias[:, 7 + b:8 + b],
                                                    ot[0][:, b].bitcast(F32), ALU.add, ALU.subtract)
                done.then_inc(ot_lo, 1)

            def add(t, g, c):
                if c == 0:
                    dve.wait_ge(residual, t + 1)
                dve.wait_ge(w_mm, g + 1)
                row = core.h[:, bass.ds(g, 1), :].rearrange("p a n -> p (a n)")
                dve.tensor_tensor(row, row, p_w[:, 0:D], ALU.add).then_inc(added, 1)

            def statistics(t):
                hold(dve, added, CH * t + CH)
                row_statistics(dve, core, st, stats, t, CH * t, CH)

            def normalised(n):
                hold(dve, turned, n)
                normalise(dve, core, xn, n).then_inc(xn_done, 1)

            def pair(t2, last=False):
                for u in range(2):
                    t = 2 * t2 + u
                    g, n = CH * t, t + 1
                    more = not (last and u == 1)
                    row_sums(g + 1, 1)
                    if not_first(t):
                        add(t - 1, g - 1, 3)
                    shift(g + 2, 2)
                    if more:
                        compressed_low(n)
                        rotate(n, 0)
                    output_low(g)
                    if more:
                        rotate(n, 1)
                        rotate(n, 2)

                    row_sums(g + 2, 2)
                    add(t, g, 0)
                    if more:
                        rotate(n, 3)
                    if not last:
                        normalised(n + 1)
                    shift(g + 3, 3)
                    output_low(g + 1)

                    add(t, g + 1, 1)
                    if more:
                        shift(g + 4, 0)
                    row_sums(g + 3, 3)
                    if not_first(t):
                        statistics(t - 1)
                    output_low(g + 2)

                    if not last:
                        turned_low(n + 1)
                    add(t, g + 2, 2)
                    if more:
                        row_sums(g + 4, 0)
                        shift(g + 5, 1)
                    output_low(g + 3)

            turned_low(0)
            normalised(1)
            dve.wait_ge(c_in, 80)
            dve.tensor_scalar(kc_bias[:], head_mask[:], bias[:, 6:7], None, ALU.mult).then_inc(kc_ready, 1)
            rotate(0, 0)
            compressed_low(0)
            for i in range(1, 4):
                rotate(0, i)
            shift(0, 0)
            turned_low(1)
            row_sums(0, 0)
            shift(1, 1)
            looped(dve, TILES // 2, pair)
            add(TILES - 1, CH * TILES - 1, 3)
            statistics(TILES - 1)

        @block.tensor
        def _(pe):
            def turn_rows(n):
                pe.wait_ge(xn_done, n + 1)
                if not_first(n):
                    j.wait_read(pe, n - 1, V[2])
                    j.wait_read(pe, n - 1, V[3])
                turn(pe, core, p_j, xn).then_inc(turned, 1)

            def from_rows(n, i):
                place = COMP + i
                bank = j.order[place]
                if i == 0:
                    pe.wait_ge(xt_lo, n + 1)
                j.wait_free(pe, n, place)
                for k in range(KD):
                    mm = product3(pe, p_j[:, bank, :], weights(at_x(i, k), P), [part[:, k, :] for part in xt],
                                  start=k == 0, stop=k == KD - 1)
                mm.then_inc(j.full[bank], 1)

            def from_compressed(n):
                pe.wait_ge(comp_lo, n + 1)
                for place, at in ((QC, at_qc), (KC, at_kc)):
                    bank = j.order[place]
                    j.wait_free(pe, n, place)
                    product3(pe, p_j[:, bank, :], weights(at, P), [part[:, :, 0, :] for part in comps]).then_inc(j.full[bank], 1)

            def values_in(n):
                for half, place in enumerate(V):
                    bank = j.order[place]
                    j.wait_free(pe, n, place)
                    for i in range(2):
                        twice = [part[:, 2 * half + i].rearrange("p a n -> p (a n)") for part in comps]
                        mm = product3(pe, p_j[:, bank, i * D:(i + 1) * D], twice, weights(at_v, D))
                    mm.then_inc(j.full[bank], 1)

            def scores(n, u, g, c):
                if c == 0:
                    j.wait_read(pe, n, QC)
                    j.wait_read(pe, n, KC)
                at_least(pe, s_out, g)
                for bank in range(2):
                    pe.matmul(p_s[:, bank, :], core.ident_bf[:], core.mask_bf[:], start=True, stop=False, skip_group_check=True)
                for q in range(4):
                    rows, bank = slice(32 * q, 32 * q + 32), q % 2
                    if q >= 2:
                        pe.wait_ge(row_tile, 4 * g + q - 1)
                    for b in range(KD):
                        for i in range(2):
                            img, at = 2 * c + i, (scored(b, q) % 4) * P
                            mm = pe.matmul(p_s[SEQ * i:SEQ * (i + 1), bank, at:at + P], qt[u][rows, b, img * SEQ:(img + 1) * SEQ],
                                           kz[u][rows, b, img].rearrange("p a k -> p (a k)"), start=False, stop=True, skip_group_check=True)
                    mm.then_inc(row_tile, 1)

            def turn_probabilities(g, c):
                pe.wait_ge(p_done, g + 1)
                at_least(pe, pt_out, g)
                for b in range(PAIRS):
                    mm = pe.transpose(p_t[:, b // 4, (b % 4) * P:(b % 4 + 1) * P],
                                      s[c][:, b].rearrange("p i k -> p (i k)"), core.ident[:])
                mm.then_inc(t_mm, 1)

            def values(t, u, g, c):
                if c == 0:
                    j.wait_read(pe, t, V[2])
                    j.wait_read(pe, t, V[3])
                at_least(pe, ot_lo, g)
                hold(pe, pt_out, g + 1)
                for b in range(KD):
                    for i in range(2):
                        for q in range(4):
                            mm = pe.matmul(p_o[32 * q:32 * q + 32, b * P + i * SEQ:b * P + (i + 1) * SEQ],
                                           vz[u][:, 2 * c + i, 4 * b + q, :], pt[:, scored(b, q), i * SEQ:(i + 1) * SEQ],
                                           start=True, stop=True)
                mm.then_inc(o_mm, 1)

            def output(g):
                at_least(pe, added, g)
                pe.wait_ge(ot_lo, g + 1)
                for b in range(KD):
                    mm = product3(pe, p_w[:, 0:D], [part[:, b] for part in ot],
                                  weights(at_o(b), D), start=b == 0, stop=b == KD - 1)
                mm.then_inc(w_mm, 1)

            def pair(t2, last=False):
                for u in range(2):
                    t = 2 * t2 + u
                    g, n = CH * t, t + 1
                    more = not (last and u == 1)
                    turn_probabilities(g, 0)
                    if not_first(t):
                        output(g - 1)
                    scores(t, u, g + 2, 2)
                    if more:
                        from_rows(n, 1)
                    values(t, u, g, 0)
                    if more:
                        from_rows(n, 2)
                        from_rows(n, 3)

                    turn_probabilities(g + 1, 1)
                    output(g)
                    if more:
                        from_rows(n, 4)
                        from_compressed(n)
                    scores(t, u, g + 3, 3)
                    values(t, u, g + 1, 1)

                    turn_probabilities(g + 2, 2)
                    output(g + 1)
                    if more:
                        scores(n, 1 - u, g + 4, 0)
                        values_in(n)
                    values(t, u, g + 2, 2)

                    if not last:
                        turn_rows(n + 1)
                    output(g + 2)
                    turn_probabilities(g + 3, 3)
                    if more:
                        scores(n, 1 - u, g + 5, 1)
                    values(t, u, g + 3, 3)
                    if not last:
                        from_rows(n + 1, 0)

            turn_rows(0)
            for i in range(5):
                from_rows(0, i)
            from_compressed(0)
            values_in(0)
            scores(0, 0, 0, 0)
            turn_rows(1)
            scores(0, 0, 1, 1)
            from_rows(1, 0)
            looped(pe, TILES // 2, pair)
            output(CH * TILES - 1)




def rows_to_blocks(w):
    return w.reshape(w.shape[0] // P, P, w.shape[1]).transpose(1, 0, 2)


def pack_attention0(wq, wk, wv, wo):
    qk = np.stack([rows_to_blocks(w).reshape(P, KD, HB0, P) for w in (wq, wk)], axis=1)
    parts = [qk.transpose(0, 3, 1, 2, 4).reshape(P, -1), rows_to_blocks(wv).reshape(P, -1), rows_to_blocks(wo).reshape(P, -1)]
    flat = np.concatenate(parts, axis=1)
    return np.ascontiguousarray(flat.reshape(P, 8, 1024).transpose(1, 0, 2))


def swap_halves(w):
    half = w.shape[-1] // 2
    return np.concatenate([w[..., half:], w[..., :half]], axis=-1)


def rope_tables():
    inv = (1.0 / np.float32(10000.0) ** (np.arange(0, P, 2, dtype=np.float32) / np.float32(P))).astype(np.float32)
    freqs = np.arange(SEQ, dtype=np.float32)[:, None] * inv[None, :]
    emb = np.concatenate([freqs, freqs], axis=-1).T
    sign = np.where(np.arange(P) < P // 2, np.float32(-1), np.float32(1))[:, None]
    return np.ascontiguousarray(np.cos(emb)), np.ascontiguousarray(np.sin(emb) * sign)


def pack_attention1(w):
    comp = np.concatenate([w["wq"], w["wkv"]], axis=1)
    from_x = [comp, w["wqr"], swap_halves(w["wqr"]), w["wkr"], swap_halves(w["wkr"])]
    none = np.zeros_like
    parts = [rows_to_blocks(m).reshape(P, -1) for m in from_x]
    parts += [np.concatenate([w["wqc"], none(w["wqc"])]), np.concatenate([none(w["wkc"]), w["wkc"]]),
              np.concatenate([none(w["wv"]), w["wv"]]), rows_to_blocks(w["wo"]).reshape(P, -1)]
    flat = np.concatenate(parts, axis=1)
    flat = np.concatenate([flat, np.zeros((P, 4096 - flat.shape[1]), np.float32)], axis=1)
    bv = w["bv"].reshape(KD, P)
    bias = np.stack([np.concatenate([w["bq"], w["bkv"]]), w["bqr"], swap_halves(w["bqr"]), w["bkr"], swap_halves(w["bkr"]),
                     w["bqc"], w["bkc"], bv[0], bv[1]], axis=1)
    cos, sin = rope_tables()
    odd = (np.arange(P) // DK1) % 2
    return dict(wa1=np.ascontiguousarray(flat.reshape(P, 4, 1024).transpose(1, 0, 2)), bias1=np.ascontiguousarray(bias),
                bo=w["bo"].reshape(1, D), cos=cos, sin=sin,
                head_mask=np.stack([1 - odd, odd], axis=1).astype(np.float32))


def build(nc, dram, out):
    with ExitStack() as ctx:
        core = Core(nc, ctx, dram)

        def attention_weights(sub, name):
            return ([core.sb(sub, f"{name}_in{i}", [P, PIECE]) for i in range(2)],
                    [core.sb(sub, f"{name}_{part}", [P, 4 * PIECE], F32R) for part in ("hi", "lo")])

        with ExitStack() as sub:
            w_in, w_qk = attention_weights(sub, "w_qk")
            patch_phase(core, w_in, w_qk)
            attention0_phase(core, w_in, w_qk)
        with ExitStack() as sub:
            w_in, w = attention_weights(sub, "w_attention1")
            experts_phase(core, 0, E0, 8, 2, next_w=(w_in, w))
            attention1_phase(core, w)
        experts_phase(core, 1, E1, 16, 4, out=out)


def kernel(**inputs):
    from concourse import bacc
    from concourse.bass_utils import run_bass_kernel_spmd

    a = {k: np.asarray(v) for k, v in inputs.items()}
    arrays = {}
    x = a["x"].reshape(IMAGES, 3, 8, 16, 8, 16).transpose(1, 3, 5, 0, 2, 4).reshape(KP, P, TILES, TILE)
    arrays["x"] = x.transpose(2, 1, 0, 3)
    arrays["W1"], arrays["W2"] = rows_to_blocks(a["L0_tok_W1"]), rows_to_blocks(a["L0_tok_W2"])
    arrays["b1"], arrays["b2"] = a["L0_tok_b1"].reshape(KD, P).T, a["L0_tok_b2"]
    arrays["wa0"] = pack_attention0(*(a[f"L0_attn_W{n}"] for n in "qkvo"))
    arrays.update(pack_attention1({n: a[f"L1_attn_{n}"] for n in (
        "wq", "wqc", "wqr", "wkv", "wkr", "wkc", "wv", "wo", "bq", "bqc", "bqr", "bkv", "bkr", "bkc", "bv", "bo")}))
    arrays["bo"] = a["L1_attn_bo"]

    def pack_experts(gate, up, down):
        wide = [w.reshape(-1, KD, P, INNER).transpose(0, 2, 1, 3).reshape(-1, P, KD * INNER) for w in (gate, up)]
        return np.concatenate(wide + [down], axis=2)

    arrays["we0"] = pack_experts(*(np.concatenate([a[f"L0_ffn_r_{n}"], a[f"L0_ffn_sh_{n}"][None]]) for n in ("gate", "up", "down")))
    arrays["we1"] = pack_experts(*(a[f"L1_ffn_w_{n}"].transpose(0, 2, 1) for n in ("gate", "up", "down")))
    pad = lambda m: np.concatenate([m, np.zeros(m.shape[:-1] + (1,), m.dtype)], axis=-1)
    arrays["wr0"] = rows_to_blocks(pad(a["L0_ffn_w_r"]))
    arrays["rb0"] = np.stack([pad(a["L0_ffn_b_r"]), pad(a["L0_ffn_routing_bias"])])
    arrays["wr1"] = rows_to_blocks(a["L1_ffn_router_weight"].T)
    arrays["rb1"] = np.stack([np.zeros(E1, np.float32), a["L1_ffn_router_bias"]])
    arrays["ident"] = np.eye(P, dtype=np.float32)
    at = np.arange(SEQ)
    arrays["mask"] = np.tile(np.where(at[None, :] > at[:, None], np.float32(NEG), np.float32(0)), (2, 1))

    nc = bacc.Bacc("TRN2", target_bir_lowering=False, num_devices=1)
    arrays = {f"in_{k}": np.ascontiguousarray(v, dtype=np.float32) for k, v in arrays.items()}
    dram = {k[3:]: nc.dram_tensor(k, v.shape, F32, kind="ExternalInput").ap() for k, v in arrays.items()}
    out = nc.dram_tensor("out_h", (TOKENS, D), F32, kind="ExternalOutput").ap()
    build(nc, dram, out.rearrange("(b p) n -> p b n", p=P))
    r = run_bass_kernel_spmd(nc, [arrays], core_ids=[0])
    return r.results[0]["out_h"].reshape(IMAGES, SEQ, D)
```

```python
import math
from contextlib import ExitStack

import numpy as np
import concourse.bass as bass
from concourse import mybir

F32 = mybir.dt.float32
F32R = mybir.dt.float32r
BF16 = mybir.dt.bfloat16
ALU = mybir.AluOpType
ACT = mybir.ActivationFunctionType
AX = mybir.AxisListType

P = 128
D = 256
KD = D // P
IMAGES = 64
SEQ = 64
TOKENS = IMAGES * SEQ
TILE = 512
TILES = TOKENS // TILE
BLOCKS = TOKENS // P
CH = TILE // P
IMG_T = TILE // SEQ
PATCH = 3 * 16 * 16
KP = PATCH // P
EPS = 1e-5
NEG = -1e30

HEADS = 16
PAIRS = HEADS // 2
DK0 = 64
DK1 = D // HEADS
QKV0 = HEADS * DK0
HB0 = QKV0 // P

INNER = 128
WCOLS = 2 * D + D
E0, E1 = 8, 16
GROUPS = 4
DVE_BN = 6


def is_first(i):
    return isinstance(i, int) and i == 0


def at_least(eng, sem, value):
    if not isinstance(value, int) or value > 0:
        eng.wait_ge(sem, value)


def hold(eng, sem, value):
    eng.wait_ge(sem, value)
    eng.nop(nofuse=True)


def looped(eng, n, body):
    body(0)
    with eng.Fori(1, n - 1) as i:
        body(i)
    body(n - 1, last=True)


def row_statistics(dve, core, st, stats, step, block, count):
    for c in range(count):
        last = dve.bn_stats(st[:, c, :], core.h[:, bass.ds(block + c, 1), :].rearrange("p a n -> p (a n)"))
    last.then_inc(stats, 1)
    hold(dve, stats, 3 * step + 1)
    for c in range(count):
        last = dve.bn_aggr(st[:, c, 0:2], st[:, c, :])
    last.then_inc(stats, 1)
    dve.wait_ge(stats, 3 * step + 2)
    dve.tensor_scalar(core.mv[:, bass.ds(block, count), :], st[:, :, 0:2], 1.0, None, ALU.mult).then_inc(stats, 1)


def product3(eng, out, lhs, rhs, start=True, stop=True):
    terms = ((0, 0), (0, 1), (1, 0))
    for n, (a, b) in enumerate(terms):
        mm = eng.matmul(out, lhs[a], rhs[b], start=start and n == 0, stop=stop and n == len(terms) - 1)
    return mm


class Core:

    def __init__(self, nc, ctx, dram):
        self.nc, self.ctx, self.dram = nc, ctx, dram
        sb = self.sb
        self.h = sb(ctx, "h", [P, BLOCKS, D])
        self.mv = sb(ctx, "mv", [P, BLOCKS, 2])
        self.var_eps, self.rstd = sb(ctx, "var_eps", [P, BLOCKS]), sb(ctx, "rstd", [P, BLOCKS])
        self.xn0 = sb(ctx, "xn0", [P, CH, D])
        self.ident = sb(ctx, "ident", [P, P])
        self.ident_bf = sb(ctx, "ident_bf", [P, P], BF16)
        self.mask = sb(ctx, "mask", [P, SEQ])
        self.mask_bf = sb(ctx, "mask_bf", [P, TILE], BF16)

        self.norm = Norm(self)

    def sb(self, ctx, name, shape, dt=F32):
        return ctx.enter_context(self.nc.sbuf_tensor(name, shape, dt))

    def ps(self, ctx, name, shape):
        return ctx.enter_context(self.nc.psum_tensor(name, shape, F32))

    def sem(self, name):
        return self.ctx.enter_context(self.nc.semaphore(name))


def patch_phase(core, stages, w_qk):
    nc, d = core.nc, core.dram
    with ExitStack() as ctx:
        sb = lambda name, shape, dt=F32: core.sb(ctx, "pa_" + name, shape, dt)
        sem = lambda name: core.sem("pa_" + name)
        w1_in, w2_in = sb("w1_in", [P, KP, D]), sb("w2_in", [P, KD, D])
        w1 = [sb("w1_hi", [P, KP, D], F32R), sb("w1_lo", [P, KP, D], F32R)]
        w2 = [sb("w2_hi", [P, KD, D], F32R), sb("w2_lo", [P, KD, D], F32R)]
        b1, b2 = sb("b1", [P, KD]), sb("b2", [P, D])
        x = [sb(f"x{i}", [P, KP, TILE]) for i in range(2)]
        xs = [[sb(f"x_hi{i}", [P, KP, TILE], F32R), sb(f"x_lo{i}", [P, KP, TILE], F32R)] for i in range(2)]
        act = sb("act", [P, KD, TILE])
        acts = [sb("act_hi", [P, KD, TILE], F32R), sb("act_lo", [P, KD, TILE], F32R)]
        st = sb("st", [P, CH, DVE_BN])
        p_hid = [core.ps(ctx, f"pa_hid{i}", [P, KD, TILE]) for i in range(2)]
        p_out = [core.ps(ctx, f"pa_out{i}", [P, CH, D]) for i in range(2)]

        w_in, c_in = sem("w_in"), sem("c_in")
        x_in = [sem("x_in0"), sem("x_in1")]
        first_in, first_hi, first_lo = [sem(f"first_in{k}") for k in range(KP)], sem("first_hi"), sem("first_lo")
        w_hi, w_split = sem("w_hi"), sem("w_split")
        x_hi, x_lo, hid, silu, act_hi, act_lo = (sem(n) for n in ("x_hi", "x_lo", "hid", "silu", "act_hi", "act_lo"))
        outp, h_done, stats = sem("outp"), sem("h_done"), sem("stats")
        qk_here, qk_split = [sem("qk_here0"), sem("qk_here1")], sem("qk_split")
        norm = core.norm

        block = ctx.enter_context(nc.Block())

        @block.sync
        def _(sp):
            for k in range(KP):
                sp.dma_start(w1_in[:, k, :], d["W1"][:, k, :]).then_inc(first_in[k], 16)
                sp.dma_start(x[0][:, k, :], d["x"][0][:, k, :]).then_inc(first_in[k], 16)
            sp.dma_start(w2_in[:], d["W2"]).then_inc(w_in, 16)
            sp.dma_start(x[1][:], d["x"][1]).then_inc(x_in[1], 16)

            def load(u, t):
                sp.wait_ge(x_lo, t - 2)
                sp.dma_start(x[u][:], d["x"][bass.ds(t, 1)].rearrange("a p k n -> (a p) k n")).then_inc(x_in[u], 16)

            sp.wait_ge(first_lo, KP)
            sp.dma_start(x[0][:], d["x"][2]).then_inc(x_in[0], 16)
            with sp.Fori(1, TILES // 2 - 1) as t2:
                load(1, 2 * t2 + 1)
                load(0, 2 * t2 + 2)
            load(1, TILES - 1)

        @block.gpsimd
        def _(pool):
            pool.wait_ge(x_in[1], 16)
            split_pieces(pool, stages, w_qk, d["wa0"][0:4], 4, qk_here, qk_split)

        @block.scalar
        def _(act_e):
            act_e.dma_start(b1[:], d["b1"]).then_inc(c_in, 16)
            act_e.dma_start(b2[:], d["b2"].partition_broadcast(P)).then_inc(c_in, 16)
            act_e.dma_start(core.ident[:], d["ident"]).then_inc(c_in, 16)
            act_e.dma_start(core.mask[:], d["mask"]).then_inc(c_in, 16)
            for k in range(KP):
                act_e.wait_ge(first_in[k], 32)
                act_e.copy(w1[0][:, k, :], w1_in[:, k, :])
                act_e.copy(xs[0][0][:, k, :], x[0][:, k, :]).then_inc(first_hi, 1)
            act_e.wait_ge(w_in, 16)
            act_e.copy(w2[0][:], w2_in[:]).then_inc(w_hi, 1)
            act_e.wait_ge(c_in, 64)

            def x_high(u, t2):
                act_e.wait_ge(x_in[u], 16 * (t2 + u))
                at_least(act_e, hid, 2 * t2 + u - 1)
                act_e.copy(xs[u][0][:], x[u][:]).then_inc(x_hi, 1)

            def pair(t2, last=False):
                for u in range(2):
                    t = 2 * t2 + u
                    if u == 0 or not last:
                        x_high(1 - u, t2 + u)
                    act_e.wait_ge(hid, t + 1)
                    at_least(act_e, act_lo, t)
                    for m in range(KD):
                        done = act_e.activation(act[:, m, :], p_hid[u][:, m, :], ACT.Silu, bias=b1[:, m:m + 1])
                    done.then_inc(silu, 1)
                    act_e.wait_ge(silu, t + 1)
                    at_least(act_e, outp, t)
                    act_e.copy(acts[0][:], act[:]).then_inc(act_hi, 1)

            looped(act_e, TILES // 2, pair)
            norm.root(act_e, norm.EARLY)

        @block.vector
        def _(dve):
            for k in range(KP):
                dve.wait_ge(first_hi, k + 1)
                dve.tensor_tensor(w1[1][:, k, :], w1_in[:, k, :], w1[0][:, k, :].bitcast(F32), ALU.subtract)
                dve.tensor_tensor(xs[0][1][:, k, :], x[0][:, k, :], xs[0][0][:, k, :].bitcast(F32), ALU.subtract).then_inc(first_lo, 1)
            dve.wait_ge(w_hi, 1)
            dve.tensor_tensor(w2[1][:], w2_in[:], w2[0][:].bitcast(F32), ALU.subtract).then_inc(w_split, 1)

            def x_low(u, t):
                dve.wait_ge(x_hi, t)
                dve.tensor_tensor(xs[u][1][:], x[u][:], xs[u][0][:].bitcast(F32), ALU.subtract).then_inc(x_lo, 1)

            def finish(u, t):
                dve.wait_ge(outp, t + 1)
                dve.tensor_tensor(core.h[:, bass.ds(CH * t, CH), :], p_out[u][:],
                                  b2[:].rearrange("p (c n) -> p c n", c=1).broadcast_to([P, CH, D]),
                                  ALU.add).then_inc(h_done, 1)
                if isinstance(t, int) and t >= TILES - 2:
                    return
                hold(dve, h_done, t + 1)
                row_statistics(dve, core, st, stats, t, CH * t, CH)

            def pair(t2, last=False):
                for u in range(2):
                    t = 2 * t2 + u
                    if u == 0 or not last:
                        x_low(1 - u, t + 1)
                    dve.wait_ge(act_hi, t + 1)
                    dve.tensor_tensor(acts[1][:], act[:], acts[0][:].bitcast(F32), ALU.subtract).then_inc(act_lo, 1)
                    if not is_first(t):
                        finish(1 - u, t - 1)

            dve.wait_ge(c_in, 64)
            dve.tensor_copy(core.ident_bf[:], core.ident[:])
            dve.tensor_copy(core.mask_bf[:].rearrange("p (i k) -> p i k", k=SEQ),
                            core.mask[:].rearrange("p (i k) -> p i k", i=1).broadcast_to([P, IMG_T, SEQ]))
            looped(dve, TILES // 2, pair)
            dve.wait_ge(stats, 3 * (TILES - 2))
            norm.request(dve, norm.EARLY)
            norm.first_rows(dve)
            finish(1, TILES - 1)

        @block.tensor
        def _(pe):
            def hidden(u, t):
                if is_first(t):
                    for k in range(KP):
                        pe.wait_ge(first_lo, k + 1)
                        for m in range(KD):
                            last = product3(pe, p_hid[u][:, m, :], [w[:, k, m * P:(m + 1) * P] for w in w1],
                                            [v[:, k, :] for v in xs[u]], start=k == 0, stop=k == KP - 1)
                    last.then_inc(hid, 1)
                    return
                pe.wait_ge(x_lo, t)
                at_least(pe, silu, t - 1)
                for m in range(KD):
                    for k in range(KP):
                        last = product3(pe, p_hid[u][:, m, :], [w[:, k, m * P:(m + 1) * P] for w in w1],
                                        [v[:, k, :] for v in xs[u]], start=k == 0, stop=k == KP - 1)
                last.then_inc(hid, 1)

            def output(u, t):
                if is_first(t):
                    pe.wait_ge(w_split, 1)
                pe.wait_ge(act_lo, t + 1)
                for c in range(CH):
                    for k in range(KD):
                        last = product3(pe, p_out[u][:, c, :], [a[:, k, c * P:(c + 1) * P] for a in acts],
                                        [w[:, k, :] for w in w2], start=k == 0, stop=k == KD - 1)
                last.then_inc(outp, 1)

            def pair(t2, last=False):
                for u in range(2):
                    t = 2 * t2 + u
                    hidden(u, t)
                    if not is_first(t):
                        output(1 - u, t - 1)

            looped(pe, TILES // 2, pair)
            output(1, TILES - 1)


class Norm:

    SPLIT = BLOCKS - 2 * CH
    EARLY, LATE = (0, SPLIT), (SPLIT, BLOCKS)

    def __init__(self, core):
        self.core = core
        self.eps_done, self.root_done, self.inverted, self.last_stats = (
            core.sem(f"norm_{n}") for n in ("eps", "root", "rstd", "last_stats"))
        self.roots = self.inversions = self.last_tile_count = 0

    def request(self, dve, blocks):
        var = self.core.mv[:, blocks[0]:blocks[1], 1]
        dve.tensor_scalar(self.core.var_eps[:, blocks[0]:blocks[1]], var, EPS, None, ALU.add).then_inc(self.eps_done, 1)

    def root(self, act, blocks):
        part = self.core.var_eps[:, blocks[0]:blocks[1]]
        self.roots += 1
        act.wait_ge(self.eps_done, self.roots)
        act.activation(part, part, ACT.Sqrt).then_inc(self.root_done, 1)

    def invert(self, dve, blocks):
        cols = slice(*blocks)
        self.inversions += 1
        dve.wait_ge(self.root_done, self.inversions)
        dve.reciprocal(self.core.rstd[:, cols], self.core.var_eps[:, cols]).then_inc(self.inverted, 1)
        dve.wait_ge(self.inverted, self.inversions)

    def first_rows(self, dve):
        self.invert(dve, self.EARLY)
        normalise(dve, self.core, self.core.xn0, 0)

    def last_tiles(self, dve, st, count=2):
        for block in range(BLOCKS - count * CH, BLOCKS, CH):
            row_statistics(dve, self.core, st, self.last_stats, self.last_tile_count, block, CH)
            self.last_tile_count += 1
            dve.wait_ge(self.last_stats, 3 * self.last_tile_count)
        self.request(dve, self.LATE)


def normalise(dve, core, xn, t):
    for c in range(CH):
        block = bass.ds(CH * t + c, 1)
        last = dve.tensor_scalar(xn[:, c, :], core.h[:, block, :].rearrange("p a n -> p (a n)"),
                                 core.mv[:, block, 0:1].rearrange("p a n -> p (a n)"), core.rstd[:, block],
                                 ALU.subtract, ALU.mult)
    return last


def turn(pe, core, out, xn):
    for k in range(KD):
        for c in range(CH):
            last = pe.transpose(out[:, k, c * P:(c + 1) * P], xn[:, c, k * P:(k + 1) * P], core.ident[:])
    return last


class Chain:

    def __init__(self, eng, sem):
        self.eng, self.sem, self.n = eng, sem, 0

    def __call__(self, instruction):
        self.n += 1
        instruction.then_inc(self.sem, 1)
        self.eng.wait_ge(self.sem, self.n)


def choose(dve, then, b, vals, top, width, k):
    for n in range(BLOCKS):
        last = dve.max(top[:, n, :], vals[:, n, :])
    then(last)
    shape = [P, BLOCKS, width]
    kth = top[:, :, k - 1:k].broadcast_to(shape)
    above, equal, rank, sel = (b[n][:, :, 0:width] for n in ("above", "equal", "rank", "sel"))
    dve.tensor_tensor(above, vals, kth, ALU.is_gt)
    then(dve.tensor_tensor(equal, vals, kth, ALU.is_equal))
    then(dve.tensor_reduce(b["count"][:], above, AX.X, ALU.add))
    flat = lambda a: a.rearrange("p b e -> p (b e)")
    then(dve.tensor_tensor_scan(flat(rank), flat(b["restart"][:]), flat(equal), 0.0, ALU.mult, ALU.add))
    then(dve.tensor_tensor(rank, rank, b["count"][:].rearrange("p (b e) -> p b e", e=1).broadcast_to(shape), ALU.add))
    then(dve.tensor_scalar(rank, rank, float(k), None, ALU.is_le))
    then(dve.tensor_tensor(equal, equal, rank, ALU.mult))
    then(dve.tensor_tensor(sel, equal, above, ALU.add))


def experts_phase(core, layer, experts, width, top_k, out=None, next_w=None):
    nc, d = core.nc, core.dram
    name = f"e{layer}_"
    with ExitStack() as ctx:
        sb = lambda n, shape, dt=F32: core.sb(ctx, name + n, shape, dt)
        sem = lambda n: core.sem(name + n)
        xt = [sb("xt_hi", [P, KD, TOKENS], F32R), sb("xt_lo", [P, KD, TOKENS], F32R)]
        xn = [sb(f"xn{i}", [P, CH, D]) for i in range(2)]
        wr_in = sb("wr_in", [P, KD, width])
        wr = [sb("wr_hi", [P, KD, width], F32R), sb("wr_lo", [P, KD, width], F32R)]
        bias = [sb(f"bias{i}", [P, width]) for i in range(2)]
        lg_t = [sb(f"lg_t{i}", [width, TILE]) for i in range(2)]
        comb = sb("comb", [P, BLOCKS, width])
        scores = sb("scores", [P, BLOCKS, width])
        b = {n: sb(n, [P, BLOCKS, width]) for n in ("above", "equal", "rank", "sel", "restart", "vals")}
        b["count"] = sb("count", [P, BLOCKS])
        vals = b["vals"]
        top = sb("top", [P, BLOCKS, 8])
        if layer == 1:
            pick = [sb(f"pick{i}", [P, BLOCKS, GROUPS]) for i in range(4)]
            wins = sb("wins", [P, BLOCKS, GROUPS])
        w_in = [sb(f"w_in{i}", [P, WCOLS]) for i in range(2)]
        w = [[sb(f"w_hi{i}", [P, WCOLS], F32R), sb(f"w_lo{i}", [P, WCOLS], F32R)] for i in range(2)]
        gated = [sb(f"gated{i}", [P, TILE]) for i in range(2)]
        hid = [sb(f"hid{i}", [P, TILE]) for i in range(2)]
        hids = [[sb(f"hid_hi{i}", [P, TILE], F32R), sb(f"hid_lo{i}", [P, TILE], F32R)] for i in range(2)]
        p_gu = [core.ps(ctx, name + f"gu{i}", [P, 2, TILE]) for i in range(2)]
        p_dn = [core.ps(ctx, name + f"dn{i}", [P, CH, D]) for i in range(2)]

        p_logits = p_dn[0][0:width].rearrange("p c n -> p (c n)")
        p_back = p_dn[1][:].rearrange("p c n -> p (c n)")

        s_in, s_split = sem("small_in"), sem("small_split")
        norm = core.norm
        xn_done, turned, xt_hi, xt_lo = sem("xn_done"), sem("turned"), sem("xt_hi"), sem("xt_lo")
        lg_done, lg_out, lg_back, logits = sem("lg_done"), sem("lg_out"), sem("lg_back"), sem("logits")
        sig, route = sem("sig"), sem("route")
        w_here = [sem("w_here0"), sem("w_here1")]
        w_split = sem("w_split")
        gate, up, silu, gated_up, hid_hi, hid_lo = (sem(n) for n in ("gate", "up", "silu", "gated_up", "hid_hi", "hid_lo"))
        down, added, stored = sem("down"), sem("added"), sem("stored")
        if next_w is not None:
            next_here, next_split, stats = [sem("next_here0"), sem("next_here1")], sem("next_split"), sem("stats")
        st = sb("st", [P, CH, DVE_BN])

        def tile_loops(eng, pair, drain):
            def rest(e, par):
                with eng.Fori(1, TILES // 2) as t2:
                    pair(e, par, t2, par)

            pair(0, 0, 0, None)
            with eng.Fori(0, experts // 2 - 1) as e2:
                rest(2 * e2, 0)
                pair(2 * e2 + 1, 1, 0, 0)
                rest(2 * e2 + 1, 1)
                pair(2 * e2 + 2, 0, 0, 1)
            rest(experts - 2, 0)
            pair(experts - 1, 1, 0, 0)
            rest(experts - 1, 1)
            drain()

        def hidden_low(eng, u, n):
            eng.wait_ge(hid_hi, n + 1)
            at_least(eng, down, n - 1)
            eng.tensor_tensor(hids[u][1][:], hid[u][:], hids[u][0][:].bitcast(F32), ALU.subtract).then_inc(hid_lo, 1)

        block = ctx.enter_context(nc.Block())

        @block.sync
        def _(sp):
            w_d = d[f"we{layer}"]
            for e in range(2):
                sp.dma_start(w_in[e][:], w_d[e]).then_inc(w_here[e], 16)
            with sp.Fori(1, experts // 2) as e2:
                for par in range(2):
                    sp.wait_ge(w_split, 2 * (2 * e2 + par - 1))
                    sp.dma_start(w_in[par][:], w_d[bass.ds(2 * e2 + par, 1)].rearrange("a p n -> (a p) n"))\
                        .then_inc(w_here[par], 16)
            if out is not None:
                for t in range(TILES):
                    sp.wait_ge(added, (experts - 1) * TILES + t + 2)
                    rows = slice(CH * t, CH * (t + 1))
                    sp.dma_start(out[:, rows, :], core.h[:, rows, :]).then_inc(stored, 16)
                sp.wait_ge(stored, 16 * TILES)

        @block.gpsimd
        def _(pool):
            pool.wait_ge(s_in, 48)
            pool.tensor_copy(wr[0][:], wr_in[:]).then_inc(s_split, 1)
            pool.wait_ge(s_split, 1)
            pool.tensor_tensor(wr[1][:], wr_in[:], wr[0][:].bitcast(F32), ALU.subtract).then_inc(s_split, 1)
            pool.memset(b["restart"][:], 1.0).then_inc(added, 1)
            if layer == 1:
                for g in range(GROUPS):
                    pool.memset(wins[:, :, g:g + 1], float(g))
            pool.memset(vals[:], -1.0).then_inc(s_split, 1)
            pool.wait_ge(s_split, 3)
            pool.memset(b["restart"][:, :, 0:1], 0.0).then_inc(s_split, 1)

            def split_weights(e2, par):
                e = 2 * e2 + par
                hold(pool, w_here[par], 16 * e2 + 16)
                if not (isinstance(e2, int) and e2 == 0):
                    hold(pool, down, TILES * (e - 1))
                pool.tensor_copy(w[par][0][:], w_in[par][:]).then_inc(w_split, 1)
                hold(pool, w_split, 2 * e + 1)
                pool.tensor_tensor(w[par][1][:], w_in[par][:], w[par][0][:].bitcast(F32), ALU.subtract)\
                    .then_inc(w_split, 1)

            split_weights(0, 0)
            split_weights(0, 1)
            if next_w is not None:
                split_pieces(pool, *next_w, d["wa1"], 4, next_here, next_split)
            with pool.Fori(1, experts // 2) as e2:
                split_weights(e2, 0)
                split_weights(e2, 1)
            if next_w is not None:
                for t in range(TILES):
                    hidden_low(pool, t % 2, TILES * (experts - 1) + t)

        @block.scalar
        def _(act):
            act.dma_start(wr_in[:], d[f"wr{layer}"]).then_inc(s_in, 16)
            for i in range(2):
                act.dma_start(bias[i][:], d[f"rb{layer}"][i].partition_broadcast(P)).then_inc(s_in, 16)

            def take_high(u, t):
                hold(act, turned, t + 1)
                act.copy(xt[0][:, :, bass.ds(TILE * t, TILE)], p_gu[u][:]).then_inc(xt_hi, 1)

            def norm_pair(t2, last=False):
                for u in range(2):
                    t = 2 * t2 + u
                    if u == 0 or not last:
                        take_high(1 - u, t + 1)
                    act.wait_ge(lg_done, t + 1)
                    at_least(act, lg_back, t - 1)
                    act.copy(lg_t[u][:], p_logits[:, u * TILE:(u + 1) * TILE]).then_inc(lg_out, 1)
                if is_first(t2):
                    norm.root(act, norm.LATE)

            take_high(0, 0)
            looped(act, TILES // 2, norm_pair)
            act.wait_ge(logits, TILES + 1)
            act.activation(scores[:], comb[:], ACT.Sigmoid).then_inc(sig, 1)

            def pair(e, par, t2, prev):
                for u in range(2):
                    n = TILES * e + 2 * t2 + u
                    act.wait_ge(gate, n + 1)
                    at_least(act, gated_up, n - 1)
                    act.activation(gated[u][:], p_gu[u][:, 0, :], ACT.Silu).then_inc(silu, 1)
                    act.wait_ge(gated_up, n + 1)
                    at_least(act, down, n - 1)
                    act.copy(hids[u][0][:], hid[u][:]).then_inc(hid_hi, 1)

            tile_loops(act, pair, lambda: None)
            if next_w is not None:
                norm.root(act, norm.EARLY)

        @block.vector
        def _(dve):
            normalise(dve, core, xn[1], 1).then_inc(xn_done, 1)

            def take(u, t):
                dve.wait_ge(xt_hi, t + 1)
                cols = bass.ds(TILE * t, TILE)
                dve.tensor_tensor(xt[1][:, :, cols], p_gu[u][:], xt[0][:, :, cols].bitcast(F32), ALU.subtract)\
                   .then_inc(xt_lo, 1)

            def take_logits(u, t):
                dve.wait_ge(lg_back, t + 1)
                dve.tensor_tensor(comb[:, bass.ds(CH * t, CH), :],
                                  p_back[:, u * TILE:u * TILE + CH * width].rearrange("p (c n) -> p c n", n=width),
                                  bias[0][:].rearrange("p (c n) -> p c n", c=1).broadcast_to([P, CH, width]),
                                  ALU.add).then_inc(logits, 1)

            def norm_pair(t2, last=False):
                for u in range(2):
                    t = 2 * t2 + u
                    if not last:
                        hold(dve, turned, t + 1)
                        normalise(dve, core, xn[u], t + 2).then_inc(xn_done, 1)
                    if u == 0 or not last:
                        take(1 - u, t + 1)
                    if not is_first(t):
                        take_logits(1 - u, t - 1)
                if is_first(t2):
                    norm.invert(dve, norm.LATE)

            take(0, 0)
            norm.last_tiles(dve, st, count=1)
            dve.wait_ge(s_in, 48)
            looped(dve, TILES // 2, norm_pair)
            take_logits(1, TILES - 1)
            dve.wait_ge(logits, TILES)
            if layer == 0:
                dve.tensor_tensor(comb[:], comb[:], bias[1][:].rearrange("p (c n) -> p c n", c=1).broadcast_to([P, BLOCKS, width]),
                                  ALU.add).then_inc(logits, 1)
            else:
                dve.tensor_scalar(comb[:], comb[:], 1.0, None, ALU.mult).then_inc(logits, 1)
            dve.wait_ge(sig, 1)
            dve.wait_ge(s_split, 4)
            then = Chain(dve, route)
            shape = [P, BLOCKS, width]

            def group_scores():
                then(dve.tensor_tensor(vals[:], scores[:], bias[1][:].rearrange("p (c n) -> p c n", c=1).broadcast_to(shape), ALU.add))
                member = lambda i: vals[:].rearrange("p b (g m) -> p b g m", g=GROUPS)[:, :, :, i]
                dve.tensor_tensor(pick[0][:], member(0), member(1), ALU.max)
                dve.tensor_tensor(pick[1][:], member(0), member(1), ALU.min)
                dve.tensor_tensor(pick[2][:], member(2), member(3), ALU.max)
                then(dve.tensor_tensor(pick[3][:], member(2), member(3), ALU.min))
                then(dve.tensor_tensor(pick[1][:], pick[1][:], pick[3][:], ALU.max))
                then(dve.tensor_tensor(pick[3][:], pick[0][:], pick[2][:], ALU.min))
                then(dve.tensor_tensor(pick[1][:], pick[1][:], pick[3][:], ALU.max))
                then(dve.tensor_tensor(pick[0][:], pick[0][:], pick[2][:], ALU.max))
                then(dve.tensor_tensor(pick[0][:], pick[0][:], pick[1][:], ALU.add))

            def compare_groups():
                scored = pick[0]
                pairs = [(slice(0, GROUPS - far), slice(far, GROUPS), pick[far]) for far in range(1, GROUPS)]
                for low, high, won in pairs:
                    last = dve.tensor_tensor(won[:, :, low], scored[:, :, low], scored[:, :, high], ALU.is_ge)
                then(last)
                for low, high, won in pairs:
                    then(dve.tensor_tensor(wins[:, :, low], wins[:, :, low], won[:, :, low], ALU.add))
                    then(dve.tensor_tensor(wins[:, :, high], wins[:, :, high], won[:, :, low], ALU.subtract))

            def choose_groups():
                kept, outside = pick[1], pick[2]
                then(dve.tensor_scalar(kept[:], wins[:], float(GROUPS - 2), None, ALU.is_ge))
                then(dve.tensor_scalar(outside[:], kept[:], -1.0, 1e9, ALU.add, ALU.mult))
                by_group = vals[:].rearrange("p b (g m) -> p (b g) m", g=GROUPS)
                of_member = lambda a: a[:].rearrange("p b (g m) -> p (b g) m", m=1).broadcast_to([P, BLOCKS * GROUPS, width // GROUPS])
                then(dve.tensor_tensor(by_group, by_group, of_member(kept), ALU.mult))
                then(dve.tensor_tensor(by_group, by_group, of_member(outside), ALU.add))

            def combine_weights():
                then(dve.tensor_tensor(comb[:], b["sel"][:], scores[:], ALU.mult))
                then(dve.tensor_reduce(b["count"][:], comb[:], AX.X, ALU.add))
                if layer == 1:
                    then(dve.tensor_scalar(b["count"][:], b["count"][:], 1e-20, None, ALU.add))
                then(dve.reciprocal(b["count"][:], b["count"][:]))
                then(dve.tensor_tensor(comb[:], comb[:], b["count"][:].rearrange("p (b e) -> p b e", e=1).broadcast_to(shape), ALU.mult))
                if layer == 0:
                    then(dve.memset(comb[:, :, experts - 1:experts], 1.0))
                else:
                    then(dve.tensor_scalar(comb[:], comb[:], 2.5, None, ALU.mult))

            def add(u, e, t):
                n = TILES * e + t
                dve.wait_ge(down, n + 1)
                if layer == 0 and isinstance(e, int) and e == experts - 1:
                    rows = core.h[:, bass.ds(CH * t, CH), :]
                    dve.tensor_tensor(rows, rows, p_dn[u][:], ALU.add).then_inc(added, 1)
                    return
                for c in range(CH):
                    row = core.h[:, bass.ds(CH * t + c, 1), :].rearrange("p a n -> p (a n)")
                    weight = comb[:, bass.ds(CH * t + c, 1), bass.ds(e, 1)].rearrange("p a n -> p (a n)")
                    last = dve.scalar_tensor_tensor(row, p_dn[u][:, c, :], weight, row, ALU.mult, ALU.add)
                last.then_inc(added, 1)

            def statistics(t):
                hold(dve, added, TILES * (experts - 1) + t + 2)
                row_statistics(dve, core, st, stats, t, CH * t, CH)

            def hidden_values(u, n):
                dve.wait_ge(silu, n + 1)
                dve.wait_ge(up, n + 1)
                at_least(dve, hid_hi, n - 1)
                dve.tensor_tensor(hid[u][:], gated[u][:], p_gu[u][:, 1, :], ALU.mult).then_inc(gated_up, 1)

            def pair(e, par, t2, prev):
                if prev is None:
                    if layer == 0:
                        real = experts - 1
                        then(dve.tensor_copy(vals[:, :, 0:real], scores[:, :, 0:real]))
                    else:
                        group_scores()
                    hidden_values(0, 0)
                    if layer == 1:
                        compare_groups()
                    hidden_low(dve, 0, 0)
                    hidden_values(1, 1)
                    if layer == 1:
                        choose_groups()
                    choose(dve, then, b, vals[:], top, width, top_k)
                    hidden_low(dve, 1, 1)
                    combine_weights()
                    add(0, 0, 0)
                    return
                for u in range(2):
                    n = TILES * e + 2 * t2 + u
                    hidden_values(u, n)
                    if not (next_w is not None and isinstance(e, int) and e == experts - 1):
                        hidden_low(dve, u, n)
                    elif not is_first(t2):
                        statistics(2 * t2 + u - 2)
                    if u == 1:
                        add(0, e, 2 * t2)
                    elif prev is not None:
                        same = not is_first(t2)
                        add(1, e if same else e - 1, 2 * t2 - 1 if same else TILES - 1)

            def drain():
                if next_w is not None:
                    dve.wait_ge(stats, 3 * (TILES - 2))
                    norm.request(dve, norm.EARLY)
                    norm.first_rows(dve)
                add(1, experts - 1, TILES - 1)

            tile_loops(dve, pair, drain)

        @block.tensor
        def _(pe):
            def turn_rows(u, t):
                at_least(pe, xn_done, t)
                at_least(pe, xt_lo, t - 1)
                turn(pe, core, p_gu[u], core.xn0 if is_first(t) else xn[u]).then_inc(turned, 1)

            def norm_pair(t2, last=False):
                for u in range(2):
                    t = 2 * t2 + u
                    router_logits(u, t)
                    if not is_first(t):
                        logits_back(1 - u, t - 1)
                    if not last:
                        turn_rows(u, t + 2)

            def router_logits(u, t):
                if is_first(t):
                    pe.wait_ge(s_split, 2)
                pe.wait_ge(xt_lo, t + 1)
                at_least(pe, lg_out, t - 1)
                cols = bass.ds(TILE * t, TILE)
                for k in range(KD):
                    last = product3(pe, p_logits[:, u * TILE:(u + 1) * TILE],
                                    [v[:, k, :] for v in wr], [v[:, k, cols] for v in xt], start=k == 0, stop=k == KD - 1)
                last.then_inc(lg_done, 1)

            def logits_back(u, t):
                hold(pe, lg_out, t + 1)
                for c in range(CH):
                    last = pe.transpose(p_back[:, u * TILE + c * width:u * TILE + (c + 1) * width],
                                        lg_t[u][:, c * P:(c + 1) * P], core.ident[0:width, 0:width])
                last.then_inc(lg_back, 1)

            turn_rows(0, 0)
            turn_rows(1, 1)
            looped(pe, TILES // 2, norm_pair)
            pe.wait_ge(logits, TILES - 2)
            logits_back(1, TILES - 1)

            def projections(e, par, t, u, n):
                cols = bass.ds(TILE * t, TILE)
                at_least(pe, gated_up, n - 1)
                for m, done in ((0, gate), (1, up)):
                    for k in range(KD):
                        at = (m * KD + k) * P
                        last = product3(pe, p_gu[u][:, m, :], [v[:, at:at + P] for v in w[par]],
                                        [v[:, k, cols] for v in xt], start=k == 0, stop=k == KD - 1)
                    last.then_inc(done, 1)

            def down_product(prev, u, n):
                pe.wait_ge(hid_lo, n + 1)
                at_least(pe, added, n)
                for c in range(CH):
                    last = product3(pe, p_dn[u][:, c, :], [v[:, c * P:(c + 1) * P] for v in hids[u]],
                                    [v[:, 2 * D:3 * D] for v in w[prev]])
                last.then_inc(down, 1)

            def pair(e, par, t2, prev):
                for u in range(2):
                    t = 2 * t2 + u
                    n = TILES * e + t
                    if is_first(t2) and u == 0:
                        pe.wait_ge(w_split, 2 * (e + 1))
                        if prev is None:
                            pe.wait_ge(xt_lo, TILES)
                    projections(e, par, t, u, n)
                    if u == 1:
                        if prev is None:
                            pe.wait_ge(logits, TILES)
                        down_product(par, 0, n - 1)
                    elif prev is not None:
                        down_product(prev, 1, n - 1)

            tile_loops(pe, pair, lambda: down_product(1, 1, experts * TILES - 1))


class Banks:

    def __init__(self, full, free, order, base=(0, 0), absent=()):
        self.full, self.free, self.order, self.base, self.absent = full, free, order, base, absent

    def before(self, t, place):
        bank = self.order[place]
        same = lambda places: sum(self.order[n] == bank for n in places)
        if is_first(t):
            return self.base[bank] + same(n for n in range(place) if n not in self.absent)
        return t * same(range(len(self.order))) + self.base[bank] + same(range(place)) - same(self.absent)

    def wait_free(self, eng, t, place):
        at_least(eng, self.free[self.order[place]], self.before(t, place))

    def wait_full(self, eng, t, place):
        eng.wait_ge(self.full[self.order[place]], self.before(t, place) + 1)

    def wait_read(self, eng, t, place):
        eng.wait_ge(self.free[self.order[place]], self.before(t, place) + 1)


def row_groups(a):
    return a[:].rearrange("p j i k -> p (j i) k")


def per_row(a):
    return a[:].rearrange("p (r k) -> p r k", k=1).broadcast_to([P, 2 * PAIRS, SEQ])


def flat3(a):
    return a[:].rearrange("p a n -> p (a n)")


PIECE = 1024


def split_pieces(pool, w_in, w, src, pieces, here, done):
    for n in range(pieces):
        if n >= 2:
            pool.wait_ge(done, 2 * n - 2)
        pool.dma_start(w_in[n % 2][:], src[n]).then_inc(here[n % 2], 16)
        if n >= 1:
            split_piece(pool, w_in, w, n - 1, here, done)
    split_piece(pool, w_in, w, pieces - 1, here, done)


def split_piece(pool, w_in, w, n, here, done):
    cols = slice(n * PIECE, (n + 1) * PIECE)
    pool.wait_ge(here[n % 2], 16 * (n // 2) + 16)
    pool.tensor_copy(w[0][:, cols], w_in[n % 2][:]).then_inc(done, 1)
    pool.wait_ge(done, 2 * n + 1)
    pool.tensor_tensor(w[1][:, cols], w_in[n % 2][:], w[0][:, cols].bitcast(F32), ALU.subtract).then_inc(done, 1)


def attention0_phase(core, w_in, w_qk):
    nc, d = core.nc, core.dram
    nb = HB0
    with ExitStack() as ctx:
        sb = lambda n, shape, dt=F32: core.sb(ctx, "a0_" + n, shape, dt)
        sem = lambda n: core.sem("a0_" + n)
        w_vo = [sb("w_hi", [P, 4 * PIECE], F32R), sb("w_lo", [P, 4 * PIECE], F32R)]
        xn = sb("xn", [P, CH, D])
        xt = [sb("xt_hi", [P, KD, TILE], F32R), sb("xt_lo", [P, KD, TILE], F32R)]
        qt, kt, v = sb("qt", [P, nb, TILE]), sb("kt", [P, nb, TILE]), sb("v", [P, CH, QKV0])
        s = [sb(f"s{i}", [P, PAIRS, 2, SEQ]) for i in range(CH)]
        mx, totals = sb("mx", [P, 2 * PAIRS]), [sb(f"total{i}", [P, 2 * PAIRS]) for i in range(CH)]
        pt = sb("pt", [P, PAIRS, P])
        ot = [sb("ot_hi", [P, nb, 2, SEQ], F32R), sb("ot_lo", [P, nb, 2, SEQ], F32R)]
        st = sb("st", [P, CH, DVE_BN])
        p_s, p_t, p_o, p_j = (core.ps(ctx, "a0_" + n, [P, 2, TILE]) for n in ("S", "T", "O", "J"))

        norm = core.norm
        w_here, w_split = [sem("w_here0"), sem("w_here1")], sem("w_split")
        xn_done, turned, xt_hi, xt_lo, residual = (sem(n) for n in ("xn_done", "turned", "xt_hi_done", "xt_lo_done", "residual"))
        s_mm, masked, max_done, s_out, exp_done, soft, p_done = (sem(n) for n in ("s_mm", "masked", "max", "s_out", "exp", "soft", "p_done"))
        t_mm, pt_out, o_mm, ot_hi, ot_lo, added, stats = (
            sem(n) for n in ("t_mm", "pt_out", "o_mm", "ot_hi_done", "ot_lo_done", "added", "stats"))

        Q = [0, 2, 5, 7, 10, 12, 15, 17]
        K = [n + 1 for n in Q]
        W = [4, 9, 14, 20]
        V = [19] + list(range(21, 28))
        j = Banks([sem("j_full0"), sem("j_full1")], [sem("j_free0"), sem("j_free1")],
                  [n % 2 for n in range(28)], absent=W)

        def tail_before(c):
            bank = j.order[W[c]]
            return j.before(TILES, j.order.index(bank)) + sum(j.order[place] == bank for place in W[:c])

        at_qk = lambda b, which, k: ((b * 2 + which) * KD + k) * P
        at_v = lambda k, half: k * QKV0 + half * TILE
        at_o = lambda b: 2 * PIECE + b * D

        block = ctx.enter_context(nc.Block())

        @block.gpsimd
        def _(pool):
            split_pieces(pool, w_in, w_vo, d["wa0"][4:8], 4, w_here, w_split)
            first = core.h[:, 0:CH, :]
            pool.tensor_tensor(first, first, core.xn0[:], ALU.add).then_inc(residual, 1)
            with pool.Fori(1, TILES) as t:
                hold(pool, xn_done, t)
                rows = core.h[:, bass.ds(CH * t, CH), :]
                pool.tensor_tensor(rows, rows, xn[:], ALU.add).then_inc(residual, 1)

        @block.scalar
        def _(act):

            def projected(t, place, out):
                j.wait_full(act, t, place)
                bank = j.order[place]
                act.copy(out, p_j[:, bank, :]).then_inc(j.free[bank], 1)

            def exp(g, c):
                act.wait_ge(s_out, g + 1)
                act.activation(s[c][:], s[c][:], ACT.Exp, scale=1.0 / math.sqrt(DK0)).then_inc(exp_done, 1)

            def turned_out(g):
                act.wait_ge(t_mm, g + 1)
                act.copy(flat3(pt), flat3(p_t)).then_inc(pt_out, 1)

            def output_high(g):
                act.wait_ge(o_mm, g + 1)
                act.copy(ot[0][:], p_o[:].rearrange("p i (j q) -> p j i q", q=SEQ)).then_inc(ot_hi, 1)

            def body(t, last=False):
                act.wait_ge(turned, t + 1)
                act.copy(flat3(xt[0]), flat3(p_o)).then_inc(xt_hi, 1)
                for b in range(nb):
                    if not is_first(t):
                        (turned_out, output_high)[b % 2](CH * (t - 1) + b // 2)
                    projected(t, Q[b], qt[:, b, :])
                    projected(t, K[b], kt[:, b, :])
                    if b == 1 and not is_first(t):
                        exp(CH * t - 1, CH - 1)
                    if b == 4 and is_first(t):
                        norm.root(act, norm.LATE)
                for c in range(CH):
                    for half in range(2):
                        projected(t, V[2 * c + half], v[:, c, half * TILE:(half + 1) * TILE])
                    if c < CH - 1:
                        exp(CH * t + c, c)

            looped(act, TILES, body)
            for c in range(CH):
                turned_out(CH * (TILES - 1) + c)
                if c == 0:
                    exp(CH * TILES - 1, CH - 1)
                output_high(CH * (TILES - 1) + c)
                if c == 0:
                    norm.root(act, norm.EARLY)

        @block.vector
        def _(dve):
            def shift(g, c):
                scores = p_s[:].rearrange("p a (r k) -> p (a r) k", k=SEQ)
                masks = core.mask[:].rearrange("p (r k) -> p r k", r=1).broadcast_to([P, 2 * PAIRS, SEQ])
                dve.wait_ge(s_mm, g + 1)
                dve.tensor_tensor(row_groups(s[c]), scores, masks, ALU.add).then_inc(masked, 1)
                dve.wait_ge(masked, g + 1)
                dve.tensor_reduce(mx[:], row_groups(s[c]), AX.X, ALU.max).then_inc(max_done, 1)
                dve.wait_ge(max_done, g + 1)
                dve.tensor_tensor(row_groups(s[c]), row_groups(s[c]), per_row(mx), ALU.subtract).then_inc(s_out, 1)

            def softmax(g, c):
                total = totals[c]
                dve.wait_ge(exp_done, g + 1)
                dve.tensor_reduce(total[:], row_groups(s[c]), AX.X, ALU.add).then_inc(soft, 1)
                dve.wait_ge(soft, 2 * g + 1)
                dve.reciprocal(total[:], total[:]).then_inc(soft, 1)
                dve.wait_ge(soft, 2 * g + 2)
                dve.tensor_tensor(row_groups(s[c]), row_groups(s[c]), per_row(total), ALU.mult).then_inc(p_done, 1)

            def output_low(g):
                dve.wait_ge(ot_hi, g + 1)
                dve.tensor_tensor(ot[1][:], p_o[:].rearrange("p i (j q) -> p j i q", q=SEQ), ot[0][:].bitcast(F32), ALU.subtract)\
                   .then_inc(ot_lo, 1)

            def add(t, c, tail=False):
                bank = j.order[W[c]]
                if tail:
                    dve.wait_ge(j.full[bank], tail_before(c) + 1)
                else:
                    j.wait_full(dve, t, W[c])
                row = core.h[:, bass.ds(CH * (t - 1) + c, 1), :].rearrange("p a n -> p (a n)")
                dve.tensor_tensor(row, row, p_j[:, bank, 0:D], ALU.add).then_inc(j.free[bank], 1)

            def statistics(t):
                row_statistics(dve, core, st, stats, t, CH * t, CH)

            def body(t, last=False):
                dve.wait_ge(xt_hi, t + 1)
                dve.tensor_tensor(flat3(xt[1]), flat3(p_o), flat3(xt[0]).bitcast(F32), ALU.subtract).then_inc(xt_lo, 1)
                if is_first(t):
                    norm.last_tiles(dve, st)
                else:
                    shift(CH * t - 1, 3)
                    softmax(CH * t - 3, 1)
                    output_low(CH * (t - 1))
                    softmax(CH * t - 2, 2)
                    dve.wait_ge(residual, t)
                    add(t, 0)
                    output_low(CH * (t - 1) + 1)
                    softmax(CH * t - 1, 3)
                if not last:
                    hold(dve, residual, t + 1)
                    normalise(dve, core, xn, t + 1).then_inc(xn_done, 1)
                if is_first(t):
                    norm.invert(dve, norm.LATE)
                if not is_first(t):
                    add(t, 1)
                    output_low(CH * (t - 1) + 2)
                    add(t, 2)
                    output_low(CH * (t - 1) + 3)
                g = CH * t
                shift(g, 0)
                if not is_first(t):
                    add(t, 3)
                shift(g + 1, 1)
                softmax(g, 0)
                shift(g + 2, 2)
                if not is_first(t) and not last:
                    bank = j.order[W[3]]
                    hold(dve, j.free[bank], j.before(t, W[3]) + 1)
                    statistics(t - 1)

            looped(dve, TILES, body)
            dve.wait_ge(stats, 3 * (TILES - 2))
            norm.request(dve, norm.EARLY)
            shift(CH * TILES - 1, 3)
            softmax(CH * TILES - 3, 1)
            dve.wait_ge(residual, TILES)
            for c in range(CH):
                output_low(CH * (TILES - 1) + c)
                if c == 0:
                    softmax(CH * TILES - 2, 2)
                    softmax(CH * TILES - 1, 3)
                if c == 1:
                    norm.first_rows(dve)
                if c == 2:
                    bank = j.order[W[3]]
                    dve.wait_ge(j.free[bank], j.before(TILES - 1, W[3]) + 1)
                    statistics(TILES - 2)
                add(TILES, c, tail=True)

        @block.tensor
        def _(pe):
            def queries_keys(t, b):
                for which, place in enumerate((Q[b], K[b])):
                    bank = j.order[place]
                    j.wait_free(pe, t, place)
                    for k in range(KD):
                        at = at_qk(b, which, k)
                        mm = product3(pe, p_j[:, bank, :], [part[:, at:at + P] for part in w_qk], [part[:, k, :] for part in xt],
                                      start=k == 0, stop=k == KD - 1)
                    mm.then_inc(j.full[bank], 1)

            def values_in(t, n):
                c, half = n // 2, n % 2
                bank = j.order[V[n]]
                j.wait_free(pe, t, V[n])
                for k in range(KD):
                    at = at_v(k, half)
                    mm = product3(pe, p_j[:, bank, :], [part[:, k, c * P:(c + 1) * P] for part in xt],
                                  [part[:, at:at + TILE] for part in w_vo], start=k == 0, stop=k == KD - 1)
                mm.then_inc(j.full[bank], 1)

            def scores(t, g, c):
                if c == 0:
                    j.wait_read(pe, t, Q[-1])
                    j.wait_read(pe, t, K[-1])
                if not is_first(g):
                    hold(pe, masked, g)
                for turn_of in range(2):
                    for n in range(8):
                        for bank in range(2):
                            head = (bank + turn_of) % 2
                            b, img = 4 * bank + n // 2, 2 * c + n % 2
                            rows, cols = slice(64 * head, 64 * head + 64), slice(img * SEQ, (img + 1) * SEQ)
                            mm = pe.matmul(p_s[rows, bank, n * SEQ:(n + 1) * SEQ], qt[rows, b, cols], kt[rows, b, cols],
                                           start=True, stop=True)
                mm.then_inc(s_mm, 1)

            def turn_probabilities(g, c):
                pe.wait_ge(p_done, g + 1)
                for b in range(PAIRS):
                    mm = pe.transpose(p_t[:, b // 4, (b % 4) * P:(b % 4 + 1) * P],
                                      s[c][:, b].rearrange("p i k -> p (i k)"), core.ident[:])
                mm.then_inc(t_mm, 1)

            def values(t, g, c):
                if c == 0:
                    j.wait_read(pe, t, V[-2])
                    j.wait_read(pe, t, V[-1])
                hold(pe, pt_out, g + 1)
                for b in range(PAIRS):
                    for img in range(2):
                        for head in range(2):
                            rows = slice(64 * img, 64 * img + 64)
                            mm = pe.matmul(p_o[64 * head:64 * head + 64, img, b * SEQ:(b + 1) * SEQ],
                                           v[rows, c, (2 * b + head) * DK0:(2 * b + head + 1) * DK0],
                                           pt[rows, b, head * SEQ:(head + 1) * SEQ], start=True, stop=True)
                mm.then_inc(o_mm, 1)

            def output(t, c, tail=False):
                bank = j.order[W[c]]
                pe.wait_ge(ot_lo, CH * (t - 1) + c + 1)
                if tail:
                    pe.wait_ge(j.free[bank], tail_before(c))
                else:
                    j.wait_free(pe, t, W[c])
                for b in range(nb):
                    mm = product3(pe, p_j[:, bank, 0:D], [part[:, b].rearrange("p i q -> p (i q)") for part in ot],
                                  [part[:, at_o(b):at_o(b) + D] for part in w_vo], start=b == 0, stop=b == nb - 1)
                mm.then_inc(j.full[bank], 1)

            def body(t, last=False):
                g0 = CH * (t - 1)
                at_least(pe, xn_done, t)
                turn(pe, core, p_o, core.xn0 if is_first(t) else xn).then_inc(turned, 1)
                if not is_first(t):
                    scores(t - 1, g0 + CH - 1, CH - 1)
                    turn_probabilities(g0, 0)
                pe.wait_ge(xt_lo, t + 1)
                for b in range(nb):
                    queries_keys(t, b)
                    if not is_first(t):
                        c = b // 2
                        if b % 2 == 0:
                            values(t - 1, g0 + c, c)
                        elif c < CH - 1:
                            output(t, c)
                            turn_probabilities(g0 + c + 1, c + 1)
                g = CH * t
                if is_first(t):
                    pe.wait_ge(w_split, 8)
                values_in(t, 0)
                scores(t, g, 0)
                if not is_first(t):
                    output(t, CH - 1)
                for c in range(CH):
                    if c > 0:
                        values_in(t, 2 * c)
                    values_in(t, 2 * c + 1)
                    if c < CH - 2:
                        scores(t, g + c + 1, c + 1)

            looped(pe, TILES, body)
            scores(TILES - 1, CH * TILES - 1, CH - 1)
            turn_probabilities(CH * (TILES - 1), 0)
            for c in range(CH):
                g = CH * (TILES - 1) + c
                values(TILES - 1, g, c)
                if c < CH - 1:
                    turn_probabilities(g + 1, c + 1)
                output(TILES, c, tail=True)


def attention1_phase(core, w):
    nc, d = core.nc, core.dram
    with ExitStack() as ctx:
        sb = lambda n, shape, dt=F32: core.sb(ctx, "a1_" + n, shape, dt)
        sem = lambda n: core.sem("a1_" + n)
        xn = sb("xn", [P, CH, D])
        xt = [sb("xt_hi", [P, KD, TILE], F32R), sb("xt_lo", [P, KD, TILE], F32R)]
        comp = sb("comp", [P, TILE])
        comps = [sb("comp_hi", [P, IMG_T, 2, SEQ], F32R), sb("comp_lo", [P, IMG_T, 2, SEQ], F32R)]
        comp_twice = comp[:].rearrange("p (i a n) -> p i a n", a=1, n=SEQ).broadcast_to([P, IMG_T, 2, SEQ])
        rope = [sb(f"rope{i}", [P, TILE]) for i in range(4)]
        qt = [sb(f"qt{i}", [P, KD, TILE]) for i in range(2)]
        kz = [sb(f"kz{i}", [P, KD, IMG_T, 2, SEQ]) for i in range(2)]
        vz = [sb(f"vz{i}", [P, IMG_T, PAIRS, 2 * DK1]) for i in range(2)]
        s = [sb(f"s{i}", [P, PAIRS, 2, SEQ]) for i in range(CH)]
        mx, totals = sb("mx", [P, 2 * PAIRS]), [sb(f"total{i}", [P, 2 * PAIRS]) for i in range(CH)]
        pt = sb("pt", [P, PAIRS, P])
        ot = [sb("ot_hi", [P, KD, P], F32R), sb("ot_lo", [P, KD, P], F32R)]
        st = sb("st", [P, CH, DVE_BN])
        cos, sin, head_mask = sb("cos", [P, SEQ]), sb("sin", [P, SEQ]), sb("head_mask", [P, 2])
        bias = sb("bias", [P, 9])
        kc_bias = sb("kc_bias", [P, 2])
        bo = sb("bo", [P, D])
        p_s, p_t, p_j = (core.ps(ctx, "a1_" + n, [P, 2, TILE]) for n in ("S", "T", "J"))
        p_o, p_w = (core.ps(ctx, "a1_" + n, [P, TILE]) for n in ("O", "W"))

        norm = core.norm
        c_in, zeros, kc_ready = sem("c_in"), sem("zeros"), sem("kc_bias_done")
        xn_done, turned, xt_hi, xt_lo, residual = (sem(n) for n in ("xn_done", "turned", "xt_hi_done", "xt_lo_done", "residual"))
        comp_hi, comp_lo, rope_sum, roped = (sem(n) for n in ("comp_hi_done", "comp_lo_done", "rope_sum", "roped"))
        row_tile, max_done, s_out, exp_done, summed, inverse, p_done = (
            sem(n) for n in ("row_tile", "max", "s_out", "exp", "summed", "inverse", "p_done"))
        t_mm, pt_out, o_mm, ot_hi, ot_lo, w_mm, added, stats = (
            sem(n) for n in ("t_mm", "pt_out", "o_mm", "ot_hi_done", "ot_lo_done", "w_mm", "added", "stats"))

        COMP, Q_ROPE, Q_SWAP, K_ROPE, K_SWAP, QC, KC = range(7)
        V = range(7, 11)
        j = Banks([sem("j_full0"), sem("j_full1")], [sem("j_free0"), sem("j_free1")], [n % 2 for n in range(11)])

        at_x = lambda i, k: (i * KD + k) * P
        at_qc, at_kc, at_v = 5 * D, 5 * D + P, 6 * D
        at_o = lambda b: 7 * D + b * D
        weights = lambda at, n: [part[:, at:at + n] for part in w]
        scored = lambda b, q: 4 * (q % 2) + 2 * (q // 2) + b

        block = ctx.enter_context(nc.Block())

        @block.gpsimd
        def _(pool):
            for part in vz:
                done = pool.memset(part[:], 0.0)
            done.then_inc(zeros, 1)
            pool.wait_ge(c_in, 80)

            def add_bias(t):
                if not is_first(t):
                    hold(pool, xn_done, t)
                rows = core.h[:, bass.ds(CH * t, CH), :]
                pool.tensor_tensor(rows, rows, bo[:].rearrange("p (c n) -> p c n", c=1).broadcast_to([P, CH, D]), ALU.add)\
                    .then_inc(residual, 1)

            def probabilities(g, c):
                pool.wait_ge(inverse, g + 1)
                pool.tensor_tensor(row_groups(s[c]), row_groups(s[c]), per_row(totals[c]), ALU.mult).then_inc(p_done, 1)

            def rope_add(n, i, place):
                j.wait_read(pool, n, place - 1)
                j.wait_read(pool, n, place)
                pool.tensor_tensor(rope[i][:], rope[i][:], rope[i + 1][:], ALU.add).then_inc(rope_sum, 1)

            def pair(t2, last=False):
                for u in range(2):
                    t = 2 * t2 + u
                    g = CH * t
                    more = not (last and u == 1)
                    probabilities(g + 1, 1)
                    if more:
                        rope_add(t + 1, 0, Q_SWAP)
                    if more:
                        rope_add(t + 1, 2, K_SWAP)
                    probabilities(g + 2, 2)
                    probabilities(g + 3, 3)
                    if more:
                        add_bias(t + 1)
                        probabilities(g + 4, 0)

            add_bias(0)
            rope_add(0, 0, Q_SWAP)
            rope_add(0, 2, K_SWAP)
            probabilities(0, 0)
            looped(pool, TILES // 2, pair)

        @block.scalar
        def _(act):
            for dst, src in ((cos, "cos"), (sin, "sin"), (head_mask, "head_mask"), (bias, "bias1")):
                act.dma_start(dst[:], d[src]).then_inc(c_in, 16)
            act.dma_start(bo[:], d["bo"].partition_broadcast(P)).then_inc(c_in, 16)

            def turned_high(n):
                act.wait_ge(turned, n + 1)
                act.copy(flat3(xt[0]), flat3(p_j)).then_inc(xt_hi, 1)

            def compressed(n):
                j.wait_full(act, n, COMP)
                at_least(act, comp_lo, n)
                act.activation(comp[:], p_j[:, 0, :], ACT.Gelu, bias=bias[:, 0:1]).then_inc(j.free[0], 1)
                j.wait_read(act, n, COMP)
                act.copy(comps[0][:], comp_twice).then_inc(comp_hi, 1)

            def queries_keys(n, u):
                by_image = lambda a: a.rearrange("p (i n) -> p i n", n=SEQ)
                act.wait_ge(rope_sum, 2 * n + 2)
                act.activation(qt[u][:, 1, :], rope[0][:], ACT.Gelu)
                for head in range(2):
                    done = act.activation(kz[u][:, 1, :, head, :], by_image(rope[2][:]), ACT.Gelu, scale=head_mask[:, head:head + 1])
                done.then_inc(roped, 1)
                j.wait_full(act, n, QC)
                act.activation(qt[u][:, 0, :], p_j[:, 1, :], ACT.Gelu, bias=bias[:, 5:6]).then_inc(j.free[1], 1)
                j.wait_full(act, n, KC)
                for head in range(2):
                    done = act.activation(kz[u][:, 0, :, head, :], by_image(p_j[:, 0, :]), ACT.Gelu,
                                          scale=head_mask[:, head:head + 1], bias=kc_bias[:, head:head + 1])
                done.then_inc(j.free[0], 1)

            def values_out(n, u):
                for i, place in enumerate(V):
                    bank = j.order[place]
                    j.wait_full(act, n, place)
                    for head in range(2):
                        rows, cols = slice(SEQ * head, SEQ * (head + 1)), slice(head * DK1, (head + 1) * DK1)
                        done = act.copy(vz[u][rows, 2 * i:2 * i + 2, :, cols],
                                        p_j[rows, bank, :].rearrange("p (i j f) -> p i j f", i=2, f=2 * DK1)[:, :, :, cols])
                    done.then_inc(j.free[bank], 1)

            def exp(g, c):
                act.wait_ge(s_out, g + 1)
                act.activation(s[c][:], s[c][:], ACT.Exp, scale=1.0 / math.sqrt(DK1)).then_inc(exp_done, 1)

            def turned_out(g):
                act.wait_ge(t_mm, g + 1)
                act.copy(flat3(pt), flat3(p_t)).then_inc(pt_out, 1)

            def output_high(g):
                act.wait_ge(o_mm, g + 1)
                at_least(act, w_mm, g)
                for b in range(KD):
                    done = act.activation(ot[0][:, b], p_o[:, b * P:(b + 1) * P], ACT.Identity, bias=bias[:, 7 + b:8 + b])
                done.then_inc(ot_hi, 1)

            def pair(t2, last=False):
                for u in range(2):
                    t = 2 * t2 + u
                    g, n = CH * t, t + 1
                    more = not (last and u == 1)
                    turned_out(g)
                    output_high(g)
                    exp(g + 2, 2)

                    turned_out(g + 1)
                    if more:
                        queries_keys(n, 1 - u)
                    output_high(g + 1)

                    turned_out(g + 2)
                    exp(g + 3, 3)
                    if more:
                        values_out(n, 1 - u)
                        exp(g + 4, 0)
                    else:
                        norm.root(act, norm.EARLY)
                    output_high(g + 2)

                    if not last:
                        turned_high(n + 1)
                    turned_out(g + 3)
                    output_high(g + 3)
                    if more:
                        exp(g + 5, 1)
                    if not last:
                        compressed(n + 1)

            turned_high(0)
            act.wait_ge(c_in, 80)
            compressed(0)
            act.wait_ge(kc_ready, 1)
            queries_keys(0, 0)
            act.wait_ge(zeros, 1)
            values_out(0, 0)
            exp(0, 0)
            turned_high(1)
            exp(1, 1)
            norm.root(act, norm.LATE)
            compressed(1)
            looped(act, TILES // 2, pair)

        @block.vector
        def _(dve):
            normalise(dve, core, xn, 1).then_inc(xn_done, 1)
            def turned_low(n):
                dve.wait_ge(xt_hi, n + 1)
                dve.tensor_tensor(flat3(xt[1]), flat3(p_j), flat3(xt[0]).bitcast(F32), ALU.subtract).then_inc(xt_lo, 1)

            def compressed_low(n):
                dve.wait_ge(comp_hi, n + 1)
                dve.tensor_tensor(comps[1][:], comp_twice, comps[0][:].bitcast(F32), ALU.subtract).then_inc(comp_lo, 1)

            def rotate(n, i):
                place = Q_ROPE + i
                bank, table = j.order[place], (cos, sin)[i % 2]
                j.wait_full(dve, n, place)
                at_least(dve, roped, n)
                dve.scalar_tensor_tensor(rope[i][:].rearrange("p (i n) -> p i n", n=SEQ),
                                         p_j[:, bank, :].rearrange("p (i n) -> p i n", n=SEQ), bias[:, 1 + i:2 + i],
                                         table[:].rearrange("p (i n) -> p i n", i=1).broadcast_to([P, IMG_T, SEQ]),
                                         ALU.add, ALU.mult).then_inc(j.free[bank], 1)

            def shift(g, c):
                scores = p_s[:].rearrange("p a (r k) -> p (a r) k", k=SEQ)
                dve.wait_ge(row_tile, 4 * g + 4)
                dve.tensor_reduce(mx[:], scores, AX.X, ALU.max).then_inc(max_done, 1)
                dve.wait_ge(max_done, g + 1)
                dve.tensor_tensor(row_groups(s[c]), scores, per_row(mx), ALU.subtract).then_inc(s_out, 1)

            def row_sums(g, c):
                dve.wait_ge(exp_done, g + 1)
                dve.tensor_reduce(totals[c][:], row_groups(s[c]), AX.X, ALU.add).then_inc(summed, 1)
                dve.wait_ge(summed, g + 1)
                dve.reciprocal(totals[c][:], totals[c][:]).then_inc(inverse, 1)

            def output_low(g):
                dve.wait_ge(ot_hi, g + 1)
                for b in range(KD):
                    done = dve.scalar_tensor_tensor(ot[1][:, b], p_o[:, b * P:(b + 1) * P], bias[:, 7 + b:8 + b],
                                                    ot[0][:, b].bitcast(F32), ALU.add, ALU.subtract)
                done.then_inc(ot_lo, 1)

            def add(t, g, c):
                if c == 0:
                    dve.wait_ge(residual, t + 1)
                dve.wait_ge(w_mm, g + 1)
                row = core.h[:, bass.ds(g, 1), :].rearrange("p a n -> p (a n)")
                dve.tensor_tensor(row, row, p_w[:, 0:D], ALU.add).then_inc(added, 1)

            def statistics(t):
                hold(dve, added, CH * t + CH)
                row_statistics(dve, core, st, stats, t, CH * t, CH)

            def normalised(n):
                hold(dve, turned, n)
                normalise(dve, core, xn, n).then_inc(xn_done, 1)

            def pair(t2, last=False):
                for u in range(2):
                    t = 2 * t2 + u
                    g, n = CH * t, t + 1
                    more = not (last and u == 1)
                    row_sums(g + 1, 1)
                    if not is_first(t):
                        add(t - 1, g - 1, 3)
                    shift(g + 2, 2)
                    if more:
                        rotate(n, 0)
                    output_low(g)
                    if more:
                        compressed_low(n)
                        rotate(n, 1)
                        rotate(n, 2)
                        rotate(n, 3)

                    row_sums(g + 2, 2)
                    add(t, g, 0)
                    if not last:
                        normalised(n + 1)
                    shift(g + 3, 3)
                    output_low(g + 1)

                    add(t, g + 1, 1)
                    row_sums(g + 3, 3)
                    if more:
                        shift(g + 4, 0)
                    if not more:
                        dve.wait_ge(stats, 3 * (TILES - 2))
                        norm.request(dve, norm.EARLY)
                    if not is_first(t):
                        statistics(t - 1)
                    output_low(g + 2)

                    if not last:
                        turned_low(n + 1)
                    if more:
                        row_sums(g + 4, 0)
                        shift(g + 5, 1)
                    add(t, g + 2, 2)
                    output_low(g + 3)

            turned_low(0)
            dve.wait_ge(c_in, 80)
            dve.tensor_scalar(kc_bias[:], head_mask[:], bias[:, 6:7], None, ALU.mult).then_inc(kc_ready, 1)
            norm.last_tiles(dve, st)
            rotate(0, 0)
            compressed_low(0)
            for i in range(1, 4):
                rotate(0, i)
            shift(0, 0)
            turned_low(1)
            row_sums(0, 0)
            shift(1, 1)
            norm.invert(dve, norm.LATE)
            looped(dve, TILES // 2, pair)
            norm.first_rows(dve)
            add(TILES - 1, CH * TILES - 1, 3)

        @block.tensor
        def _(pe):
            def turn_rows(n):
                at_least(pe, xn_done, n)
                if not is_first(n):
                    j.wait_read(pe, n - 1, V[2])
                    j.wait_read(pe, n - 1, V[3])
                turn(pe, core, p_j, core.xn0 if is_first(n) else xn).then_inc(turned, 1)

            def from_rows(n, i):
                place = COMP + i
                bank = j.order[place]
                if i == 0:
                    pe.wait_ge(xt_lo, n + 1)
                j.wait_free(pe, n, place)
                for k in range(KD):
                    mm = product3(pe, p_j[:, bank, :], weights(at_x(i, k), P), [part[:, k, :] for part in xt],
                                  start=k == 0, stop=k == KD - 1)
                mm.then_inc(j.full[bank], 1)

            def from_compressed(n):
                pe.wait_ge(comp_lo, n + 1)
                for place, at in ((QC, at_qc), (KC, at_kc)):
                    bank = j.order[place]
                    j.wait_free(pe, n, place)
                    product3(pe, p_j[:, bank, :], weights(at, P), [part[:, :, 0, :] for part in comps]).then_inc(j.full[bank], 1)

            def values_in(n):
                for half, place in enumerate(V):
                    bank = j.order[place]
                    j.wait_free(pe, n, place)
                    for i in range(2):
                        twice = [part[:, 2 * half + i].rearrange("p a n -> p (a n)") for part in comps]
                        mm = product3(pe, p_j[:, bank, i * D:(i + 1) * D], twice, weights(at_v, D))
                    mm.then_inc(j.full[bank], 1)

            def scores(n, u, g, c):
                if c == 0:
                    j.wait_read(pe, n, QC)
                    j.wait_read(pe, n, KC)
                at_least(pe, s_out, g)
                for bank in range(2):
                    pe.matmul(p_s[:, bank, :], core.ident_bf[:], core.mask_bf[:], start=True, stop=False, skip_group_check=True)
                for q in range(4):
                    rows, bank = slice(32 * q, 32 * q + 32), q % 2
                    if q >= 2:
                        pe.wait_ge(row_tile, 4 * g + q - 1)
                    for b in range(KD):
                        for i in range(2):
                            img, at = 2 * c + i, (scored(b, q) % 4) * P
                            mm = pe.matmul(p_s[SEQ * i:SEQ * (i + 1), bank, at:at + P], qt[u][rows, b, img * SEQ:(img + 1) * SEQ],
                                           kz[u][rows, b, img].rearrange("p a k -> p (a k)"), start=False, stop=True, skip_group_check=True)
                    mm.then_inc(row_tile, 1)

            def turn_probabilities(g, c):
                pe.wait_ge(p_done, g + 1)
                for b in range(PAIRS):
                    mm = pe.transpose(p_t[:, b // 4, (b % 4) * P:(b % 4 + 1) * P],
                                      s[c][:, b].rearrange("p i k -> p (i k)"), core.ident[:])
                mm.then_inc(t_mm, 1)

            def values(t, u, g, c):
                if c == 0:
                    j.wait_read(pe, t, V[2])
                    j.wait_read(pe, t, V[3])
                hold(pe, pt_out, g + 1)
                for b in range(KD):
                    for i in range(2):
                        for q in range(4):
                            mm = pe.matmul(p_o[32 * q:32 * q + 32, b * P + i * SEQ:b * P + (i + 1) * SEQ],
                                           vz[u][:, 2 * c + i, 4 * b + q, :], pt[:, scored(b, q), i * SEQ:(i + 1) * SEQ],
                                           start=True, stop=True)
                mm.then_inc(o_mm, 1)

            def output(g):
                at_least(pe, added, g)
                pe.wait_ge(ot_lo, g + 1)
                for b in range(KD):
                    mm = product3(pe, p_w[:, 0:D], [part[:, b] for part in ot],
                                  weights(at_o(b), D), start=b == 0, stop=b == KD - 1)
                mm.then_inc(w_mm, 1)

            def pair(t2, last=False):
                for u in range(2):
                    t = 2 * t2 + u
                    g, n = CH * t, t + 1
                    more = not (last and u == 1)
                    turn_probabilities(g, 0)
                    if not is_first(t):
                        output(g - 1)
                    scores(t, u, g + 2, 2)
                    if more:
                        from_rows(n, 1)
                    values(t, u, g, 0)
                    if more:
                        from_rows(n, 2)
                        from_rows(n, 3)

                    turn_probabilities(g + 1, 1)
                    output(g)
                    if more:
                        from_rows(n, 4)
                        from_compressed(n)
                    scores(t, u, g + 3, 3)
                    values(t, u, g + 1, 1)

                    turn_probabilities(g + 2, 2)
                    output(g + 1)
                    if more:
                        scores(n, 1 - u, g + 4, 0)
                        values_in(n)
                    values(t, u, g + 2, 2)

                    if not last:
                        turn_rows(n + 1)
                    turn_probabilities(g + 3, 3)
                    if more:
                        scores(n, 1 - u, g + 5, 1)
                    output(g + 2)
                    values(t, u, g + 3, 3)
                    if not last:
                        from_rows(n + 1, 0)

            turn_rows(0)
            for i in range(5):
                from_rows(0, i)
            from_compressed(0)
            values_in(0)
            scores(0, 0, 0, 0)
            turn_rows(1)
            scores(0, 0, 1, 1)
            from_rows(1, 0)
            looped(pe, TILES // 2, pair)
            output(CH * TILES - 1)




def rows_to_blocks(w):
    return w.reshape(w.shape[0] // P, P, w.shape[1]).transpose(1, 0, 2)


def pack_attention0(wq, wk, wv, wo):
    qk = np.stack([rows_to_blocks(w).reshape(P, KD, HB0, P) for w in (wq, wk)], axis=1)
    parts = [qk.transpose(0, 3, 1, 2, 4).reshape(P, -1), rows_to_blocks(wv).reshape(P, -1), rows_to_blocks(wo).reshape(P, -1)]
    flat = np.concatenate(parts, axis=1)
    return np.ascontiguousarray(flat.reshape(P, 8, 1024).transpose(1, 0, 2))


def swap_halves(w):
    half = w.shape[-1] // 2
    return np.concatenate([w[..., half:], w[..., :half]], axis=-1)


def rope_tables():
    inv = (1.0 / np.float32(10000.0) ** (np.arange(0, P, 2, dtype=np.float32) / np.float32(P))).astype(np.float32)
    freqs = np.arange(SEQ, dtype=np.float32)[:, None] * inv[None, :]
    emb = np.concatenate([freqs, freqs], axis=-1).T
    sign = np.where(np.arange(P) < P // 2, np.float32(-1), np.float32(1))[:, None]
    return np.ascontiguousarray(np.cos(emb)), np.ascontiguousarray(np.sin(emb) * sign)


def pack_attention1(w):
    comp = np.concatenate([w["wq"], w["wkv"]], axis=1)
    from_x = [comp, w["wqr"], swap_halves(w["wqr"]), w["wkr"], swap_halves(w["wkr"])]
    none = np.zeros_like
    parts = [rows_to_blocks(m).reshape(P, -1) for m in from_x]
    parts += [np.concatenate([w["wqc"], none(w["wqc"])]), np.concatenate([none(w["wkc"]), w["wkc"]]),
              np.concatenate([none(w["wv"]), w["wv"]]), rows_to_blocks(w["wo"]).reshape(P, -1)]
    flat = np.concatenate(parts, axis=1)
    flat = np.concatenate([flat, np.zeros((P, 4096 - flat.shape[1]), np.float32)], axis=1)
    bv = w["bv"].reshape(KD, P)
    bias = np.stack([np.concatenate([w["bq"], w["bkv"]]), w["bqr"], swap_halves(w["bqr"]), w["bkr"], swap_halves(w["bkr"]),
                     w["bqc"], w["bkc"], bv[0], bv[1]], axis=1)
    cos, sin = rope_tables()
    odd = (np.arange(P) // DK1) % 2
    return dict(wa1=np.ascontiguousarray(flat.reshape(P, 4, 1024).transpose(1, 0, 2)), bias1=np.ascontiguousarray(bias),
                bo=w["bo"].reshape(1, D), cos=cos, sin=sin,
                head_mask=np.stack([1 - odd, odd], axis=1).astype(np.float32))


def build(nc, dram, out):
    with ExitStack() as ctx:
        core = Core(nc, ctx, dram)

        def attention_weights(sub, name):
            return ([core.sb(sub, f"{name}_in{i}", [P, PIECE]) for i in range(2)],
                    [core.sb(sub, f"{name}_{part}", [P, 4 * PIECE], F32R) for part in ("hi", "lo")])

        with ExitStack() as sub:
            w_in, w_qk = attention_weights(sub, "w_qk")
            patch_phase(core, w_in, w_qk)
            attention0_phase(core, w_in, w_qk)
        with ExitStack() as sub:
            w_in, w = attention_weights(sub, "w_attention1")
            experts_phase(core, 0, E0, 8, 2, next_w=(w_in, w))
            attention1_phase(core, w)
        experts_phase(core, 1, E1, 16, 4, out=out)


def kernel(**inputs):
    from concourse import bacc
    from concourse.bass_utils import run_bass_kernel_spmd

    a = {k: np.asarray(v) for k, v in inputs.items()}
    arrays = {}
    x = a["x"].reshape(IMAGES, 3, 8, 16, 8, 16).transpose(1, 3, 5, 0, 2, 4).reshape(KP, P, TILES, TILE)
    arrays["x"] = x.transpose(2, 1, 0, 3)
    arrays["W1"], arrays["W2"] = rows_to_blocks(a["L0_tok_W1"]), rows_to_blocks(a["L0_tok_W2"])
    arrays["b1"], arrays["b2"] = a["L0_tok_b1"].reshape(KD, P).T, a["L0_tok_b2"]
    arrays["wa0"] = pack_attention0(*(a[f"L0_attn_W{n}"] for n in "qkvo"))
    arrays.update(pack_attention1({n: a[f"L1_attn_{n}"] for n in (
        "wq", "wqc", "wqr", "wkv", "wkr", "wkc", "wv", "wo", "bq", "bqc", "bqr", "bkv", "bkr", "bkc", "bv", "bo")}))
    arrays["bo"] = a["L1_attn_bo"]

    def pack_experts(gate, up, down):
        wide = [w.reshape(-1, KD, P, INNER).transpose(0, 2, 1, 3).reshape(-1, P, KD * INNER) for w in (gate, up)]
        return np.concatenate(wide + [down], axis=2)

    arrays["we0"] = pack_experts(*(np.concatenate([a[f"L0_ffn_r_{n}"], a[f"L0_ffn_sh_{n}"][None]]) for n in ("gate", "up", "down")))
    arrays["we1"] = pack_experts(*(a[f"L1_ffn_w_{n}"].transpose(0, 2, 1) for n in ("gate", "up", "down")))
    pad = lambda m: np.concatenate([m, np.zeros(m.shape[:-1] + (1,), m.dtype)], axis=-1)
    arrays["wr0"] = rows_to_blocks(pad(a["L0_ffn_w_r"]))
    arrays["rb0"] = np.stack([pad(a["L0_ffn_b_r"]), pad(a["L0_ffn_routing_bias"])])
    arrays["wr1"] = rows_to_blocks(a["L1_ffn_router_weight"].T)
    arrays["rb1"] = np.stack([np.zeros(E1, np.float32), a["L1_ffn_router_bias"]])
    arrays["ident"] = np.eye(P, dtype=np.float32)
    at = np.arange(SEQ)
    arrays["mask"] = np.tile(np.where(at[None, :] > at[:, None], np.float32(NEG), np.float32(0)), (2, 1))

    nc = bacc.Bacc("TRN2", target_bir_lowering=False, num_devices=1)
    arrays = {f"in_{k}": np.ascontiguousarray(v, dtype=np.float32) for k, v in arrays.items()}
    dram = {k[3:]: nc.dram_tensor(k, v.shape, F32, kind="ExternalInput").ap() for k, v in arrays.items()}
    out = nc.dram_tensor("out_h", (TOKENS, D), F32, kind="ExternalOutput").ap()
    build(nc, dram, out.rearrange("(b p) n -> p b n", p=P))
    r = run_bass_kernel_spmd(nc, [arrays], core_ids=[0])
    return r.results[0]["out_h"].reshape(IMAGES, SEQ, D)
```
